# Optimizing a Trainium2 kernel written in Bass

```python
import numpy as np
import jax
import jax.numpy as jnp

def _softmax(x, axis=-1):
    return jax.nn.softmax(x, axis=axis)

def _gelu(x):
    return jax.nn.gelu(x, approximate=True)

def _silu(x):
    return jax.nn.silu(x)

def _sigmoid(x):
    return jax.nn.sigmoid(x)

def _layernorm(x, axis=-1, eps=1e-05):
    m = jnp.mean(x, axis=axis, keepdims=True)
    v = jnp.var(x, axis=axis, keepdims=True)
    return (x - m) / jnp.sqrt(v + eps)

def _scatter_add(tgt, idx, src, axis=0):
    return tgt.at[idx].add(src)

def _segment_sum(src, seg, n):
    return jax.ops.segment_sum(src, seg, n)
kernel_name = 'mk_gnn_preln_d2_gnn_r16_56b960'

def setup_inputs(seed: int=0):
    np.random.seed(seed)
    _w = jnp.asarray

    def _rec_inputs():
        import jax
        import jax.numpy as jnp
        _gk = jax.random.key(seed)
        x = -0.0003713 + 1 * jax.random.normal(jax.random.fold_in(_gk, 1), (6250, 256), jnp.float32)
        src = jax.random.randint(jax.random.fold_in(_gk, 2), (100000,), 0, 6250, jnp.int32)
        dst = jnp.minimum((6250 * jax.random.uniform(jax.random.fold_in(_gk, 3), (100000,)) ** 2.0).astype(jnp.int32), 99999)
        _o = jnp.argsort(dst, stable=True)
        src = src[_o]
        dst = dst[_o]
        edge_weight1 = jax.random.uniform(jax.random.fold_in(_gk, 13), (100000, 1), jnp.float32, 0.0, 1)
        node_vec1 = jax.random.uniform(jax.random.fold_in(_gk, 14), (6250, 1), jnp.float32, 0.0, 1)
        return (x, src, dst, edge_weight1, node_vec1)
    x, src, dst, edge_weight1, node_vec1 = _rec_inputs()

    def _L0_gnn_setup():
        import jax, jax.numpy as jnp
        import numpy as np
        N_NODES = 3125
        N_EDGES = 50000
        DIM = 256
        HEADS = 8
        DIM_OUT = 32
        key = jax.random.key(seed)
        ks = jax.random.split(key, 9)
        s = 1.0 / np.sqrt(DIM)
        inner = HEADS * DIM_OUT
        return {'x': jax.random.normal(ks[0], (N_NODES, DIM), dtype=jnp.float32), 'Wq': jax.random.uniform(ks[1], (DIM, inner), jnp.float32, -s, s), 'bq': jax.random.uniform(ks[2], (inner,), jnp.float32, -s, s), 'Wk': jax.random.uniform(ks[3], (DIM, inner), jnp.float32, -s, s), 'bk': jax.random.uniform(ks[4], (inner,), jnp.float32, -s, s), 'Wv': jax.random.uniform(ks[5], (DIM, inner), jnp.float32, -s, s), 'bv': jax.random.uniform(ks[6], (inner,), jnp.float32, -s, s), 'src': jax.random.randint(ks[7], (N_EDGES,), 0, N_NODES), 'dst': jax.random.randint(ks[8], (N_EDGES,), 0, N_NODES)}
    _L0_gnn_all = _L0_gnn_setup()
    _L0_gnn_in = {k: v for k, v in _L0_gnn_all.items() if k in ('Wq', 'bq', 'Wk', 'bk', 'Wv', 'bv')}
    del _L0_gnn_all

    def _L1_gnn_setup():
        import jax, jax.numpy as jnp
        import numpy as np
        C = 1.0
        K = 1.0 / C
        SQRTK = K ** 0.5
        EPS = 1e-07
        MIN_NORM = 1e-15
        MAX_NORM = 1000000.0
        NORM_FACTOR = 100.0

        def mink_dot(x, y):
            return -x[..., 0:1] * y[..., 0:1] + jnp.sum(x[..., 1:] * y[..., 1:], axis=-1, keepdims=True)

        def mink_norm(u):
            return jnp.sqrt(jnp.clip(mink_dot(u, u), EPS, None))

        def arcosh(t):
            return jnp.arccosh(jnp.clip(t, 1.0 + EPS, None))

        def proj(x):
            y = x[..., 1:]
            x0 = jnp.sqrt(K + jnp.sum(y * y, axis=-1, keepdims=True))
            return jnp.concatenate([x0, y], axis=-1)

        def proj_tan(u, x):
            ux = jnp.sum(x[..., 1:] * u[..., 1:], axis=-1, keepdims=True)
            u0 = ux / jnp.clip(x[..., 0:1], EPS, None)
            return jnp.concatenate([u0, u[..., 1:]], axis=-1)

        def expmap(u, x):
            normu = jnp.clip(mink_norm(u), None, MAX_NORM)
            theta = jnp.clip(normu / SQRTK, MIN_NORM, None)
            return proj(jnp.cosh(theta) * x + jnp.sinh(theta) * u / theta)

        def sqdist(x, y):
            theta = jnp.clip(-mink_dot(x, y) / K, 1.0 + EPS, None)
            return jnp.clip(K * arcosh(theta) ** 2, None, 50.0)

        def logmap(x, y):
            xy = jnp.clip(mink_dot(x, y) + K, None, -EPS) - K
            u = y + xy * x * C
            normu = jnp.clip(mink_norm(u), MIN_NORM, None)
            dist = jnp.sqrt(sqdist(x, y))
            return proj_tan(dist * u / normu, x)

        def logmap0(x):
            y = x[..., 1:]
            y_norm = jnp.clip(jnp.linalg.norm(y, axis=-1, keepdims=True), MIN_NORM, None)
            theta = jnp.clip(x[..., 0:1] / SQRTK, 1.0 + EPS, None)
            res = SQRTK * arcosh(theta) * y / y_norm
            return jnp.concatenate([jnp.zeros_like(x[..., 0:1]), res], axis=-1)

        def expmap0(u):
            y = u[..., 1:]
            y_norm = jnp.clip(jnp.linalg.norm(y, axis=-1, keepdims=True), MIN_NORM, None)
            theta = y_norm / SQRTK
            return proj(jnp.concatenate([SQRTK * jnp.cosh(theta), SQRTK * jnp.sinh(theta) * y / y_norm], axis=-1))
        N, E, D, EDGE_DIM = (625, 20000, 256, 1)
        key = jax.random.key(seed)
        ks = jax.random.split(key, 12)
        u = jnp.concatenate([jnp.zeros((N, 1), jnp.float32), 0.1 * jax.random.normal(ks[0], (N, D - 1), jnp.float32)], axis=-1)
        x = expmap0(u)
        distances = jax.random.uniform(ks[1], (E, EDGE_DIM), jnp.float32)
        edges = jax.random.randint(ks[2], (2, E), 0, N)
        node_mask = jnp.ones((N, 1), jnp.float32)
        edge_mask = jnp.ones((E, 1), jnp.float32)
        s = 0.02
        return {'x': x, 'distances': distances, 'edges': edges, 'node_mask': node_mask, 'edge_mask': edge_mask, 'att_w1': s * jax.random.normal(ks[3], (2 * D + EDGE_DIM, D), jnp.float32), 'att_b1': jnp.zeros((D,), jnp.float32), 'att_w2': s * jax.random.normal(ks[4], (D, 1), jnp.float32), 'att_b2': jnp.zeros((1,), jnp.float32), 'mlp_w1': s * jax.random.normal(ks[5], (D, D), jnp.float32), 'mlp_b1': jnp.zeros((D,), jnp.float32), 'mlp_w2': s * jax.random.normal(ks[6], (D, D), jnp.float32), 'mlp_b2': jnp.zeros((D,), jnp.float32)}
    _L1_gnn_all = _L1_gnn_setup()
    _L1_gnn_in = {k: v for k, v in _L1_gnn_all.items() if k in ('att_w1', 'att_b1', 'att_w2', 'att_b2', 'mlp_w1', 'mlp_b1', 'mlp_w2', 'mlp_b2')}
    del _L1_gnn_all
    return {'x': x, 'src': src, 'dst': dst, 'edge_weight1': edge_weight1, 'node_vec1': node_vec1, 'L0_gnn_Wq': _L0_gnn_in['Wq'], 'L0_gnn_bq': _L0_gnn_in['bq'], 'L0_gnn_Wk': _L0_gnn_in['Wk'], 'L0_gnn_bk': _L0_gnn_in['bk'], 'L0_gnn_Wv': _L0_gnn_in['Wv'], 'L0_gnn_bv': _L0_gnn_in['bv'], 'L1_gnn_att_w1': _L1_gnn_in['att_w1'], 'L1_gnn_att_b1': _L1_gnn_in['att_b1'], 'L1_gnn_att_w2': _L1_gnn_in['att_w2'], 'L1_gnn_att_b2': _L1_gnn_in['att_b2'], 'L1_gnn_mlp_w1': _L1_gnn_in['mlp_w1'], 'L1_gnn_mlp_b1': _L1_gnn_in['mlp_b1'], 'L1_gnn_mlp_w2': _L1_gnn_in['mlp_w2'], 'L1_gnn_mlp_b2': _L1_gnn_in['mlp_b2']}

def reference(x, src, dst, edge_weight1, node_vec1, L0_gnn_Wq, L0_gnn_bq, L0_gnn_Wk, L0_gnn_bk, L0_gnn_Wv, L0_gnn_bv, L1_gnn_att_w1, L1_gnn_att_b1, L1_gnn_att_w2, L1_gnn_att_b2, L1_gnn_mlp_w1, L1_gnn_mlp_b1, L1_gnn_mlp_w2, L1_gnn_mlp_b2):
    import jax
    import jax.numpy as jnp

    def _L0_gnn_ref(x, Wq, bq, Wk, bk, Wv, bv, src, dst):
        import jax, jax.numpy as jnp
        import numpy as np
        N_NODES = 3125
        N_EDGES = 50000
        DIM = 256
        HEADS = 8
        DIM_OUT = 32
        n = x.shape[0]
        q = (x @ Wq + bq).reshape(n, HEADS, DIM_OUT)
        k = (x @ Wk + bk).reshape(n, HEADS, DIM_OUT)
        v = (x @ Wv + bv).reshape(n, HEADS, DIM_OUT)
        scores = jnp.einsum('ehd,ehd->eh', q[src], k[dst]) / jnp.sqrt(jnp.asarray(DIM_OUT, dtype=x.dtype))
        m = jax.ops.segment_max(scores, dst, num_segments=n)
        m = jnp.where(jnp.isfinite(m), m, 0.0)
        e = jnp.exp(scores - m[dst])
        z = jax.ops.segment_sum(e, dst, num_segments=n)
        p = e / jnp.maximum(z[dst], 1e-16)
        out = jax.ops.segment_sum(v[src] * p[:, :, None], dst, num_segments=n)
        return out.reshape(n, HEADS * DIM_OUT)

    def _L1_gnn_ref(x, distances, edges, node_mask, edge_mask, att_w1, att_b1, att_w2, att_b2, mlp_w1, mlp_b1, mlp_w2, mlp_b2):
        import jax, jax.numpy as jnp
        import numpy as np
        C = 1.0
        K = 1.0 / C
        SQRTK = K ** 0.5
        EPS = 1e-07
        MIN_NORM = 1e-15
        MAX_NORM = 1000000.0
        NORM_FACTOR = 100.0

        def mink_dot(x, y):
            return -x[..., 0:1] * y[..., 0:1] + jnp.sum(x[..., 1:] * y[..., 1:], axis=-1, keepdims=True)

        def mink_norm(u):
            return jnp.sqrt(jnp.clip(mink_dot(u, u), EPS, None))

        def arcosh(t):
            return jnp.arccosh(jnp.clip(t, 1.0 + EPS, None))

        def proj(x):
            y = x[..., 1:]
            x0 = jnp.sqrt(K + jnp.sum(y * y, axis=-1, keepdims=True))
            return jnp.concatenate([x0, y], axis=-1)

        def proj_tan(u, x):
            ux = jnp.sum(x[..., 1:] * u[..., 1:], axis=-1, keepdims=True)
            u0 = ux / jnp.clip(x[..., 0:1], EPS, None)
            return jnp.concatenate([u0, u[..., 1:]], axis=-1)

        def expmap(u, x):
            normu = jnp.clip(mink_norm(u), None, MAX_NORM)
            theta = jnp.clip(normu / SQRTK, MIN_NORM, None)
            return proj(jnp.cosh(theta) * x + jnp.sinh(theta) * u / theta)

        def sqdist(x, y):
            theta = jnp.clip(-mink_dot(x, y) / K, 1.0 + EPS, None)
            return jnp.clip(K * arcosh(theta) ** 2, None, 50.0)

        def logmap(x, y):
            xy = jnp.clip(mink_dot(x, y) + K, None, -EPS) - K
            u = y + xy * x * C
            normu = jnp.clip(mink_norm(u), MIN_NORM, None)
            dist = jnp.sqrt(sqdist(x, y))
            return proj_tan(dist * u / normu, x)

        def logmap0(x):
            y = x[..., 1:]
            y_norm = jnp.clip(jnp.linalg.norm(y, axis=-1, keepdims=True), MIN_NORM, None)
            theta = jnp.clip(x[..., 0:1] / SQRTK, 1.0 + EPS, None)
            res = SQRTK * arcosh(theta) * y / y_norm
            return jnp.concatenate([jnp.zeros_like(x[..., 0:1]), res], axis=-1)

        def expmap0(u):
            y = u[..., 1:]
            y_norm = jnp.clip(jnp.linalg.norm(y, axis=-1, keepdims=True), MIN_NORM, None)
            theta = y_norm / SQRTK
            return proj(jnp.concatenate([SQRTK * jnp.cosh(theta), SQRTK * jnp.sinh(theta) * y / y_norm], axis=-1))
        row, col = (edges[0], edges[1])
        N = x.shape[0]
        x_tangent = logmap0(x)
        x_local_tangent = logmap(x[row], x[col])
        x_local_self_tangent = logmap(x, x)
        cat = jnp.concatenate([x_tangent[row], x_tangent[col], distances], axis=-1)
        h = jax.nn.silu(cat @ att_w1 + att_b1)
        att = jax.nn.sigmoid(h @ att_w2 + att_b2) * edge_mask
        agg = jax.ops.segment_sum(x_local_tangent * att, row, num_segments=N) / NORM_FACTOR
        mlp_out = jax.nn.silu(agg @ mlp_w1 + mlp_b1) @ mlp_w2 + mlp_b2
        out = x_local_self_tangent + mlp_out
        support_t = proj_tan(out, x)
        return expmap(support_t, x)
    edge_index = jnp.stack([src, dst])
    h = jnp.maximum(_layernorm(x, axis=-1), 0.0)
    x = x + _L0_gnn_ref(h, L0_gnn_Wq, L0_gnn_bq, L0_gnn_Wk, L0_gnn_bk, L0_gnn_Wv, L0_gnn_bv, src, dst)
    h = jnp.maximum(_layernorm(x, axis=-1), 0.0)
    x = x + _L1_gnn_ref(h, edge_weight1, edge_index, node_vec1, edge_weight1, L1_gnn_att_w1, L1_gnn_att_b1, L1_gnn_att_w2, L1_gnn_att_b2, L1_gnn_mlp_w1, L1_gnn_mlp_b1, L1_gnn_mlp_w2, L1_gnn_mlp_b2)
    return x

_drawn_inputs = setup_inputs


def setup_inputs(seed=0):
    import zlib

    import numpy as np

    out = dict(_drawn_inputs(seed))
    spreads = {'L1_gnn_att_b1': (0.0, 0.8), 'L1_gnn_mlp_b1': (0.0, 0.1), 'L1_gnn_mlp_b2': (0.0, 0.1)}
    factors = {'L0_gnn_bq': 8.0, 'L1_gnn_att_w1': 8.0, 'L1_gnn_att_w2': 8.0}
    for name, (base, spread) in spreads.items():
        noise = np.random.default_rng([zlib.crc32(name.encode()), seed]).standard_normal(out[name].shape)
        drawn = base * np.exp(spread * noise) if base else spread * noise
        out[name] = jnp.asarray(drawn.astype(out[name].dtype))
    for name, factor in factors.items():
        out[name] = (out[name] * factor).astype(out[name].dtype)
    return out
```

```python
import math
from contextlib import ExitStack

import concourse.bass as bass
from concourse import mybir

F32 = mybir.dt.float32
BF16 = mybir.dt.bfloat16
I32 = mybir.dt.int32
ALU = mybir.AluOpType
ACT = mybir.ActivationFunctionType
AX = mybir.AxisListType

P = 128
NODES, DIM, HEADS = 6250, 256, 8
DH = DIM // HEADS
EDGES = 100000
NB = -(-NODES // P)
NP_ = NB * P
ET = -(-EDGES // P)
ET = -(-ET // 8) * 8
PAD_NODE = NP_ - 1
CHUNKS = P // HEADS
STEPS = -(-(ET + NB - 1) // 16) * 16
SCOL = -(-STEPS // P)
SP_ = SCOL * P
CSTEPS = STEPS // CHUNKS
CLEN = CSTEPS * P
AW = DIM + HEADS
BIG = 1e30
EPS = 1e-7
FAR = 50.0
SCORE = 1.0 / math.sqrt(DH)
G = 8


class Links:

    def __init__(self, eng, sem, base=0):
        self.eng, self.sem, self.base, self.n = eng, sem, base, 0

    def mark(self, ins):
        ins.then_inc(self.sem, 1)
        self.n += 1

    def wait(self, back=0):
        self.eng.wait_ge(self.sem, self.base + (self.n - back))


class Mem:
    pass


class Stage(ExitStack):

    def __init__(self, nc, tag):
        super().__init__()
        self.nc, self.tag, self.sems = nc, tag, []

    def sem(self, name):
        handle = self.enter_context(self.nc.semaphore(f"{self.tag}_{name}"))
        self.sems.append(handle)
        return handle

    def gather_sem(self, m, name):
        return m.ctx.enter_context(self.nc.semaphore(f"{self.tag}_{name}"))

    def close_stage(self):
        with self.nc.Block() as block:
            @block.gpsimd
            def _(pool):
                for handle in self.sems:
                    pool.sem_clear(handle)

    def __exit__(self, *error):
        if error[0] is None:
            self.close_stage()
        return super().__exit__(*error)


def bcast(ap, n):
    return ap.unsqueeze(2).to_broadcast([ap.shape[0], ap.shape[1], n])


def consts(nc, m):
    with Stage(nc, "consts") as ctx:
        sem = ctx.sem
        pool_done, load_done = sem("const_pool"), sem("const_load")
        with nc.Block() as block:

            @block.gpsimd
            def _(pool):
                ln = Links(pool, pool_done)
                ln.mark(nc.gpsimd.iota(m.ramp[:, :], pattern=[[1, P]], base=0, channel_multiplier=0,
                                       allow_small_or_imprecise_dtypes=True))
                ln.mark(nc.gpsimd.iota(m.lane[:, :], pattern=[[0, 1]], base=0, channel_multiplier=1,
                                       allow_small_or_imprecise_dtypes=True))
                ln.mark(nc.gpsimd.iota(m.step_no[:, :], pattern=[[P, SCOL]], base=0, channel_multiplier=1,
                                       allow_small_or_imprecise_dtypes=True))
                ln.mark(nc.gpsimd.memset(m.ones[:, :], 1.0))
                ln.mark(nc.gpsimd.memset(m.zeros[:, :], 0.0))
                ln.mark(nc.gpsimd.memset(m.ident[:, :], 0.0))
                ln.mark(nc.gpsimd.memset(m.half[:, :], 0.5))
                ln.mark(nc.gpsimd.memset(m.mhalf[:, :], -0.5))
                ln.mark(nc.gpsimd.memset(m.mone[:, :], -1.0))
                ln.mark(nc.gpsimd.memset(m.neg_ln2[:, :], -math.log(2.0)))
                ln.wait()
                ln.mark(nc.gpsimd.tensor_copy(m.ramp16[:, :], m.ramp[:, :]))
                ln.mark(nc.gpsimd.affine_select(out=m.ident[:, :], in_=m.ident[:, :], compare_op=ALU.not_equal, fill=1.0,
                                                base=0, pattern=[[-1, P]], channel_multiplier=1))
                ln.mark(nc.gpsimd.affine_select(out=m.before_row[:, :], in_=m.ones[:, :], compare_op=ALU.is_gt, fill=0.0,
                                                base=0, pattern=[[-1, P]], channel_multiplier=1))
                ln.mark(nc.gpsimd.affine_select(out=m.before_col[:, :], in_=m.ones[:, :], compare_op=ALU.is_gt, fill=0.0,
                                                base=0, pattern=[[1, P]], channel_multiplier=-1))
                ln.wait()



def sort_edges(nc, m, tag, key_in, other_in, rec, d_lk, d_cols, d_off, d_skey):
    with Stage(nc, tag) as ctx:
        sb = lambda n, s, d: ctx.enter_context(nc.sbuf_tensor(f"{tag}_{n}", s, d))
        pb = lambda n, s: ctx.enter_context(nc.psum_tensor(f"{tag}_{n}", s, F32))
        sem = ctx.sem
        RT = -(-ET // P)
        FULL = ET // P
        row_i = sb("row_i", [P, 2, RT, P], I32)
        hi_i = sb("hi_i", [P, 2, RT, P], I32)
        rows = sb("rows", [P, 5, RT, P], F32)
        cols = sb("cols", [P, 5, RT * P], F32)
        recs = sb("recs", [P, RT * P, 4], I32)
        hot_lo = sb("hot_lo", [P, 2, G, P], BF16)
        hot_hi = sb("hot_hi", [P, 2, G, NB], BF16)
        lo_bc = sb("lo_bc", [P, 2, G * P], F32)
        key_bc = sb("key_bc", [P, 2, G * P], F32)
        hot_loT = sb("hot_loT", [P, 2, G, P], F32)
        total = sb("total", [P, NB], F32)
        shifted = sb("shifted", [P, NB], F32)
        base = sb("base", [P, 2, G + 1, NB], F32)
        bounds = sb("bounds", [P, NB + 1], F32)
        picked = sb("picked", [P, 2, G, NB], F32)
        rank = sb("rank", [P, 2, G], F32)
        taken = sem("taken")
        credit = sb("credit", [1, 2, 4], I32)
        dup = sb("dup", [P, 2, G], F32)
        eq = sb("eq", [P, 2, P], F32)
        rank_i = sb("rank_i", [P, 2, G], I32)
        rec_st = sb("rec_st", [P, 2, G, 4], I32)
        bk = sb("bk", [P, 12, NB + 1], F32)
        bk_i = sb("bk_i", [P, 2, NB + 1], I32)
        stp = sb("stp", [P, 6, SCOL], F32)
        tile_i = sb("tile_i", [P, SCOL], I32)
        offT = sb("offT", [SCOL, 2, P], I32)
        got = sb("got", [P, 2, P, 4], I32)
        scol = sb("scol", [P, SP_, 3], I32)
        srow = sb("srow", [P, 2, 4, P], F32)
        ps_t = pb("ps_t", [P, 2, 512])
        ps_hist = pb("ps_hist", [P, 512])
        ps_up = pb("ps_up", [P, 2, 512])
        ps_look = pb("ps_look", [P, 2, 512])
        NGRP = ET // G

        loaded, split, turned, evac, stored, zeroed = (sem(n) for n in ("loaded", "split", "turned", "evac", "stored", "zeroed"))
        dl = sem("dve1")
        with nc.Block() as block:
            @block.sync
            def _(sp):
                sp.wait_ge(zeroed, 3)
                for n, src in enumerate((key_in, other_in)):
                    sp.dma_start(row_i[:, n, 0:FULL, :], src[0:FULL * P, :].rearrange("(j t) e -> t j e", t=P)).then_inc(loaded, 16)
                    sp.dma_start(row_i[0:ET - FULL * P, n, FULL, :], src[FULL * P:ET, :]).then_inc(loaded, 16)
                sp.dma_start(rows[:, 4, 0:FULL, :], m.in_w[0:FULL * P, :].rearrange("(j t) e -> t j e", t=P)).then_inc(loaded, 16)
                sp.dma_start(rows[0:ET - FULL * P, 4, FULL, :], m.in_w[FULL * P:ET, :]).then_inc(loaded, 16)
                sp.wait_ge(split, 1)
                for n, dst in ((0, m.d_key), (3, m.d_lo)):
                    sp.dma_start(dst[0:FULL * P, :].rearrange("(j t) e -> t j e", t=P), rows[:, n, 0:FULL, :]).then_inc(stored, 16)
                    sp.dma_start(dst[FULL * P:ET, :], rows[0:ET - FULL * P, n, FULL, :]).then_inc(stored, 16)
                sp.wait_ge(stored, 64)

            @block.vector
            def _(dve):
                ln = Links(dve, dl)
                nc.vector.memset(row_i[:, 0, FULL, :], 0).then_inc(zeroed, 1)
                nc.vector.memset(row_i[:, 1, FULL, :], 0).then_inc(zeroed, 1)
                nc.vector.memset(rows[:, 4, FULL, :], 0.0).then_inc(zeroed, 1)
                dve.wait_ge(loaded, 96)
                ln.mark(nc.vector.tensor_single_scalar(hi_i[:, 0], row_i[:, 0], 7, ALU.arith_shift_right))
                ln.mark(nc.vector.tensor_single_scalar(hi_i[:, 1], row_i[:, 0], P - 1, ALU.bitwise_and))
                ln.wait()
                nc.vector.tensor_copy(rows[:, 0:2], row_i[:, :])
                nc.vector.tensor_copy(rows[:, 2:4], hi_i[:, :]).then_inc(split, 1)
                for g in range(RT * 5 // 5):
                    for n in range(5):
                        u = g * 5 + n
                        dve.wait_ge(turned, u + 1)
                        nc.vector.tensor_copy(cols[:, n, g * P:(g + 1) * P], ps_t[:, u % 2, 0:P]).then_inc(evac, 1)
                dve.wait_ge(evac, RT * 5)
                nc.vector.tensor_copy(recs[:, :, 0], cols[:, 0, :])
                nc.vector.tensor_copy(recs[:, :, 1], cols[:, 1, :])
                nc.vector.tensor_copy(recs[:, :, 2].bitcast(F32), cols[:, 4, :])
                nc.vector.memset(recs[:, :, 3], 0)

            @block.tensor
            def _(pe):
                pe.wait_ge(split, 1)
                for g in range(RT):
                    for n in range(5):
                        u = g * 5 + n
                        if u >= 2:
                            pe.wait_ge(evac, u - 1)
                        nc.tensor.transpose(ps_t[:, u % 2, 0:P], rows[:, n, g, :], m.ident[:, :]).then_inc(turned, 1)

        hots, counted = sem("hots"), sem("counted")
        with nc.Block() as block:
            @block.vector
            def _(dve):
                with dve.Fori(0, NGRP // 2) as i:
                    for h in range(2):
                        dve.wait_ge(counted, i * 2 + h + 1)
                        at = bass.ds((i * 2 + h) * G, G)
                        nc.vector.tensor_tensor(hot_hi[:, h], m.ramp16[:, 0:NB].unsqueeze(1).to_broadcast([P, G, NB]),
                                                bcast(cols[:, 2, at], NB), ALU.is_equal)
                        nc.vector.tensor_tensor(hot_lo[:, h], m.ramp16[:, :].unsqueeze(1).to_broadcast([P, G, P]),
                                                bcast(cols[:, 3, at], P), ALU.is_equal).then_inc(hots, 1)

            @block.tensor
            def _(pe):
                nc.tensor.matmul(ps_hist[:, 0:NB], m.zeros[:, :], m.ident[:, 0:NB], start=True, stop=False).then_inc(counted, 2)
                with pe.Fori(0, NGRP // 2) as i:
                    for h in range(2):
                        pe.wait_ge(hots, i * 2 + h + 1)
                        for k in range(G):
                            last = nc.tensor.matmul(ps_hist[:, 0:NB], hot_lo[:, h, k], hot_hi[:, h, k], start=False, stop=False)
                        last.then_inc(counted, 1)
                nc.tensor.matmul(ps_hist[:, 0:NB], m.zeros[:, :], m.ident[:, 0:NB], start=False, stop=True)

        ready, summed = sem("ready"), sem("summed")
        dl2 = sem("dve2")
        with nc.Block() as block:
            @block.vector
            def _(dve):
                ln = Links(dve, dl2)
                V = nc.vector

                def op(ins):
                    ln.mark(ins)
                    ln.wait()

                op(V.tensor_copy(total[:, :], ps_hist[:, 0:NB]))
                op(V.memset(shifted[:, 0:1], 0.0))
                op(V.tensor_tensor_scan(shifted[:, 1:NB], m.ones[:, 0:NB - 1], total[:, 0:NB - 1], 0.0, ALU.mult, ALU.add))
                dve.sem_inc(ready, 1)
                dve.wait_ge(summed, 1)
                op(V.tensor_copy(base[:, 0, 0, :], ps_look[:, 0, 0:NB]))
                op(V.tensor_copy(bounds[:, 0:NB], ps_look[:, 1, 0:NB]))
                op(V.memset(bounds[:, NB:NB + 1], float(ET * P)))
                first, last, some, n, start, g, dg, lastk = (bk[:, j, :] for j in range(8))
                op(V.tensor_copy(bk_i[:, 0, :], bounds[:, :]))
                op(V.tensor_single_scalar(bk_i[:, 1, :], bk_i[:, 0, :], 7, ALU.arith_shift_right))
                op(V.tensor_copy(first, bk_i[:, 1, :]))
                op(V.tensor_scalar(lastk, bounds[:, :], -1.0, None, ALU.add))
                op(V.tensor_copy(bk_i[:, 0, :], lastk))
                op(V.tensor_single_scalar(bk_i[:, 1, :], bk_i[:, 0, :], 7, ALU.arith_shift_right))
                op(V.tensor_copy(last, bk_i[:, 1, :]))
                op(V.memset(n, 0.0))
                op(V.tensor_tensor(some[:, 0:NB], bounds[:, 1:NB + 1], bounds[:, 0:NB], ALU.is_gt))
                op(V.tensor_tensor(n[:, 0:NB], last[:, 1:NB + 1], first[:, 0:NB], ALU.subtract))
                op(V.scalar_tensor_tensor(n[:, 0:NB], n[:, 0:NB], 1.0, some[:, 0:NB], ALU.add, ALU.mult))
                op(V.memset(start, 0.0))
                op(V.tensor_tensor_scan(start[:, 1:NB + 1], m.ones[:, 0:NB], n[:, 0:NB], 0.0, ALU.mult, ALU.add))
                op(V.tensor_tensor(g, first, start, ALU.subtract))
                op(V.tensor_copy(dg, g))
                op(V.tensor_tensor(dg[:, 1:NB], g[:, 1:NB], g[:, 0:NB - 1], ALU.subtract))
                for j in range(SCOL):
                    s = m.step_no[:, j:j + 1]
                    op(V.tensor_scalar(bk[:, 8, 0:NB], start[:, 1:NB + 1], s, 0.0, ALU.is_le, ALU.add, accum_out=stp[:, 0, j:j + 1]))
                    op(V.scalar_tensor_tensor(bk[:, 9, 0:NB], start[:, 0:NB], s, dg[:, 0:NB], ALU.is_le, ALU.mult,
                                              accum_out=stp[:, 1, j:j + 1]))
                op(V.tensor_tensor(stp[:, 1, :], stp[:, 1, :], m.step_no[:, :], ALU.add))
                op(V.tensor_scalar(stp[:, 1, :], stp[:, 1, :], float(ET - 1), 0.0, ALU.min, ALU.max))
                op(V.tensor_copy(tile_i[:, :], stp[:, 1, :]))
                op(V.tensor_scalar(stp[:, 2, :], stp[:, 0, :], float(P), None, ALU.mult))
                op(V.tensor_scalar(stp[:, 3, :], stp[:, 0, :], float(NB - 1), float(DIM), ALU.min, ALU.mult))
                op(V.tensor_scalar(stp[:, 4, :], stp[:, 0, :], float(NB - 1), float(AW), ALU.min, ALU.mult))
                dve.sem_inc(ready, 1)
                dve.wait_ge(summed, 2)
                op(V.tensor_copy(offT[:, 0, :], ps_t[0:SCOL, 0, 0:P]))
                op(V.tensor_copy(offT[:, 1, :], ps_t[0:SCOL, 1, 0:P]))
                dve.sem_inc(ready, 1)

            @block.tensor
            def _(pe):
                pe.wait_ge(ready, 1)
                nc.tensor.matmul(ps_look[:, 0, 0:NB], m.ones[:, :], shifted[:, :], start=True, stop=False)
                nc.tensor.matmul(ps_look[:, 0, 0:NB], m.before_col[:, :], total[:, :], start=False, stop=True)
                nc.tensor.matmul(ps_look[:, 1, 0:NB], m.ones[:, :], shifted[:, :], start=True, stop=True).then_inc(summed, 1)
                pe.wait_ge(ready, 2)
                nc.tensor.transpose(ps_t[0:SCOL, 0, 0:P], stp[:, 3, :], m.ident[:, :])
                nc.tensor.transpose(ps_t[0:SCOL, 1, 0:P], stp[:, 4, :], m.ident[:, :]).then_inc(summed, 1)

            @block.sync
            def _(sp):
                sp.wait_ge(ready, 3)
                sp.dma_start(d_off.rearrange("n (j s) -> j n s", s=P), offT[:, :, :]).then_inc(stored, 16)
                sp.wait_ge(stored, 80)

        bc_in = [sem("bc_in0"), sem("bc_in1")]
        hots2, upd, tabs, looked, placed, bc_used = (sem(n) for n in ("hots2", "upd", "tabs", "looked", "placed", "bc_used"))
        dl3 = sem("dve3")
        scat = [ctx.gather_sem(m, f"scat{h}") for h in range(2)]
        with nc.Block() as block:
            @block.sync
            def _(sp):
                sp.sem_inc(bc_used, 2)
                with sp.Fori(0, NGRP // 2) as i:
                    for h in range(2):
                        g = i * 2 + h
                        sp.wait_ge(bc_used, g + 1)
                        sp.dma_start(key_bc[:, h, :], m.d_key_flat[:, bass.ds(g * (G * P), G * P)].to_broadcast([P, G * P])).then_inc(bc_in[h], 16)
                        sp.dma_start(lo_bc[:, h, :], m.d_lo_flat[:, bass.ds(g * (G * P), G * P)].to_broadcast([P, G * P])).then_inc(bc_in[h], 16)

            @block.vector
            def _(dve):
                V = nc.vector
                per = 2 * (G + 6)
                with dve.Fori(0, NGRP // 2) as i:
                    ln = Links(dve, dl3, i * per)
                    for h in range(2):
                        g = i * 2 + h
                        at = bass.ds(g * G, G)
                        dve.wait_ge(bc_in[h], (i + 1) * 32)
                        V.tensor_tensor(hot_hi[:, h], m.ramp16[:, 0:NB].unsqueeze(1).to_broadcast([P, G, NB]),
                                        bcast(cols[:, 2, at], NB), ALU.is_equal)
                        V.tensor_tensor(hot_lo[:, h], m.ramp16[:, :].unsqueeze(1).to_broadcast([P, G, P]),
                                        bcast(cols[:, 3, at], P), ALU.is_equal).then_inc(hots2, 1)
                        V.tensor_scalar(hot_loT[:, h], lo_bc[:, h, :].rearrange("p (k e) -> p k e", k=G), m.lane[:, 0:1], None, ALU.is_equal)
                        for k in range(G):
                            if k >= 2:
                                ln.wait(1)
                            ln.mark(V.scalar_tensor_tensor(eq[:, k % 2, :], key_bc[:, h, k * P:(k + 1) * P],
                                                           cols[:, 0, bass.ds(g * G + k, 1)], m.before_row[:, :],
                                                           ALU.is_equal, ALU.mult, accum_out=dup[:, h, k:k + 1]))
                        ln.wait()
                        dve.sem_inc(bc_used, 1)
                        dve.wait_ge(upd, g + 1)
                        ln.mark(V.tensor_tensor(base[:, h, 1:G + 1, :], ps_up[:, h, 0:G * NB].rearrange("p (k b) -> p k b", k=G),
                                                base[:, h, 0:1, :].to_broadcast([P, G, NB]), ALU.add))
                        ln.wait()
                        dve.sem_inc(tabs, 1)
                        ln.mark(V.tensor_copy(base[:, 1 - h, 0, :], base[:, h, G, :]))
                        dve.wait_ge(looked, g + 1)
                        ln.mark(V.tensor_tensor(picked[:, h], ps_look[:, h, 0:G * NB].rearrange("p (k b) -> p k b", k=G), hot_hi[:, h], ALU.mult))
                        ln.wait()
                        ln.mark(V.tensor_reduce(rank[:, h], picked[:, h], axis=AX.X, op=ALU.add))
                        ln.wait()
                        dve.wait_ge(scat[h], 16 + i * (16 * G))
                        ln.mark(V.tensor_tensor(rank_i[:, h], rank[:, h], dup[:, h], ALU.add))
                        ln.mark(V.tensor_copy(rec_st[:, h], recs[:, at, :]))
                        ln.wait()
                        dve.sem_inc(placed, 1)
                    assert ln.n == per

            @block.tensor
            def _(pe):
                with pe.Fori(0, NGRP // 2) as i:
                    for h in range(2):
                        g = i * 2 + h
                        pe.wait_ge(hots2, g + 1)
                        for k in range(G):
                            for j in range(k + 1):
                                last = nc.tensor.matmul(ps_up[:, h, k * NB:(k + 1) * NB], hot_lo[:, h, j], hot_hi[:, h, j],
                                                        start=(j == 0), stop=(j == k))
                        last.then_inc(upd, 1)
                        pe.wait_ge(tabs, g + 1)
                        for k in range(G):
                            last = nc.tensor.matmul(ps_look[:, h, k * NB:(k + 1) * NB], hot_loT[:, h, k], base[:, h, k, :],
                                                    start=True, stop=True)
                        last.then_inc(looked, 1)

            @block.gpsimd
            def _(pool):
                for h in range(2):
                    pool.dma_start(credit[:, h, :], d_off[0:1, 0:4]).then_inc(scat[h], 16)
                with pool.Fori(0, NGRP // 2) as i:
                    for h in range(2):
                        g = i * 2 + h
                        pool.wait_ge(placed, g + 1)
                        pool.sem_inc(taken, 1)
                        for k in range(G):
                            pool.indirect_dma_start(out=rec[:, :], out_offset=bass.IndirectOffsetOnAxis(ap=rank_i[:, h, k:k + 1], axis=0),
                                                    in_=rec_st[:, h, k, :], in_offset=None).then_inc(scat[h], 16)
                for h in range(2):
                    pool.wait_ge(scat[h], 16 + (NGRP // 2) * (16 * G))

        fetched, spread, tt, te = ([ctx.gather_sem(m, f"fetched{h}") for h in range(2)], sem("spread"), sem("tt"), sem("te"))
        st2 = [sem("kept0"), sem("kept1")]
        dl4 = sem("dve4")
        with nc.Block() as block:
            rec_tiles = rec.rearrange("(t e) w -> t (e w)", e=P)

            @block.gpsimd
            def _(pool):
                for j in range(SCOL):
                    if j >= 2:
                        pool.wait_ge(spread, j - 1)
                    pool.indirect_dma_start(out=got[:, j % 2].rearrange("p e w -> p (e w)"), out_offset=None, in_=rec_tiles,
                                            in_offset=bass.IndirectOffsetOnAxis(ap=tile_i[:, j:j + 1], axis=0)).then_inc(fetched[j % 2], 16)

            @block.vector
            def _(dve):
                V = nc.vector
                ln = Links(dve, dl4)
                for j in range(SCOL):
                    r = srow[:, j % 2]
                    dve.wait_ge(fetched[j % 2], (j // 2 + 1) * 16)
                    if j >= 2:
                        dve.wait_ge(st2[j % 2], (j // 2) * 32)
                        dve.wait_ge(te, (j - 1) * 3)
                    ln.mark(V.tensor_copy(r[:, 0, :], got[:, j % 2, :, 0]))
                    ln.mark(V.tensor_copy(r[:, 2, :], got[:, j % 2, :, 1]))
                    ln.mark(V.tensor_copy(r[:, 3, :], got[:, j % 2, :, 2].bitcast(F32)))
                    ln.wait()
                    ln.mark(V.tensor_scalar(r[:, 1, :], r[:, 0, :], stp[:, 2, j:j + 1], None, ALU.subtract))
                    ln.wait()
                    dve.sem_inc(spread, 1)
                    for n, dst in enumerate((scol[:, :, 1].bitcast(F32), scol[:, :, 0], scol[:, :, 2].bitcast(F32))):
                        u = j * 3 + n
                        dve.wait_ge(tt, u + 1)
                        V.tensor_copy(dst[:, j * P:(j + 1) * P], ps_t[:, u % 2, 0:P]).then_inc(te, 1)

            @block.tensor
            def _(pe):
                for j in range(SCOL):
                    pe.wait_ge(spread, j + 1)
                    for n in range(3):
                        u = j * 3 + n
                        if u >= 2:
                            pe.wait_ge(te, u - 1)
                        nc.tensor.transpose(ps_t[:, u % 2, 0:P], srow[:, j % 2, 1 + n, :], m.ident[:, :]).then_inc(tt, 1)

            @block.sync
            def _(sp):
                for j in range(SCOL):
                    sp.wait_ge(spread, j + 1)
                    sp.dma_start(d_skey[0:1, 1 + j * P * P:1 + (j + 1) * P * P].rearrange("o (s e) -> (o s) e", e=P), srow[:, j % 2, 0, :]).then_inc(st2[j % 2], 16)
                    sp.dma_start(d_lk[j * P:(j + 1) * P, :], srow[:, j % 2, 1, :]).then_inc(st2[j % 2], 16)
                sp.wait_ge(te, 3 * SCOL)
                sp.dma_start(d_cols, scol[:, :, :]).then_inc(stored, 16)
                sp.wait_ge(stored, 96)
                for h in range(2):
                    sp.wait_ge(st2[h], 32 * ((SCOL + 1 - h) // 2))


RB = 7
ROUNDS = NB // RB
assert ROUNDS * RB == NB


def arcosh(nc, ops, ask_sqrt, ask_ln, t, w):
    z, a, r, ln1, q, q2, s = w[1:8]
    ops.ts(a, t, 1.0, None, ALU.subtract)
    ops.ts(r, t, 1.0, None, ALU.add)
    ops.tt(r, r, a, ALU.mult)
    ask_sqrt(r, r)
    ops.tt(z, a, r, ALU.add)
    ask_ln(ln1, z)
    ops.ts(q, z, 2.0, None, ALU.add)
    ops.recip(q, q)
    ops.tt(q, q, z, ALU.mult)
    ops.tt(q2, q, q, ALU.mult)
    ops.ts(s, q2, 2.0 / 7, 2.0 / 5, ALU.mult, ALU.add)
    ops.tt(s, s, q2, ALU.mult)
    ops.ts(s, s, 2.0 / 3, None, ALU.add)
    ops.tt(s, s, q2, ALU.mult)
    ops.ts(s, s, 2.0, None, ALU.add)
    ops.tt(s, s, q, ALU.mult)
    ops.tt(s, s, ln1, ALU.subtract)
    ops.ts(a, z, 0.25, None, ALU.is_lt)
    ops.tt(s, s, a, ALU.mult)
    ops.tt(w[0], s, ln1, ALU.add)


class Small:

    def __init__(self, eng, ns, ln, mhalf=None):
        self.eng, self.ns, self.ln, self.mhalf = eng, ns, ln, mhalf

    def do(self, ins):
        self.ln.mark(ins)
        self.ln.wait()

    def ts(self, out, a, s1, s2, op0, op1=None):
        if op1 is None:
            self.do(self.ns.tensor_scalar(out, a, s1, None, op0))
        else:
            self.do(self.ns.tensor_scalar(out, a, s1, s2, op0, op1))

    def tt(self, out, a, b, op):
        self.do(self.ns.tensor_tensor(out, a, b, op))

    def recip(self, out, a):
        self.do(self.ns.reciprocal(out, a))


def node_stage(nc, m, tag, kind):
    with Stage(nc, tag) as ctx:
        sb = lambda n, s, d=F32: ctx.enter_context(nc.sbuf_tensor(f"{tag}_{n}", s, d))
        pb = lambda n, s: ctx.enter_context(nc.psum_tensor(f"{tag}_{n}", s, F32))
        sem = ctx.sem
        NW = 3 if kind == "qkv" else 2
        wts = sb("wts", [P, NW, 2, DIM])
        bias = sb("bias", [P, NW, DIM])
        xt = sb("xt", [P, RB, DIM])
        xc = sb("xc", [P, RB, DIM])
        tmp = sb("tmp", [P, RB, DIM])
        hT = sb("hT", [P, RB, 2, P])
        st = sb("st", [P, 24, RB])
        rowst = sb("rowst", [P, RB, 512 if kind != "out" else DIM])
        pt = pb("pt", [P, 2, 512])
        pj = pb("pj", [P, 4, 512])
        w_in, x_in, x_used, dv, ask, answer, turned, evac, hready, hT_ready, proj, proj_used, rows_ready, rows_out = (
            sem(n) for n in ("w_in", "x_in", "x_used", "dve", "ask", "answer", "turned", "evac", "hready", "hT_ready",
                             "proj", "proj_used", "rows_ready", "rows_out"))
        s_x = (m.d_x1 if kind == "out" else m.in_x).rearrange("(b p) d -> p b d", p=P)
        if kind == "qkv":
            mats, vecs = (m.in_wq, m.in_wv, m.in_wk), (m.in_bq, m.in_bv, m.in_bk)
        elif kind == "mid":
            mats, vecs = (m.in_aw1[0:DIM, :], m.in_aw1[DIM:2 * DIM, :]), (m.in_ab1, None)
        else:
            mats, vecs = (m.in_mw1, m.in_mw2), (m.in_mb1, m.in_mb2)
        passes = 2 if kind == "out" else 1

        PER_DVE = {"qkv": 10, "mid": 47, "out": 80}[kind]
        ASKS = {"qkv": 1, "mid": 4, "out": 7}[kind]
        

        with nc.Block() as block:
            @block.sync
            def _(sp):
                n_w = 0
                for n in range(NW):
                    sp.dma_start(wts[:, n], mats[n].rearrange("(c p) n -> p c n", p=P)).then_inc(w_in, 16)
                    n_w += 1
                    if vecs[n] is not None:
                        sp.dma_start(bias[:, n, :], vecs[n].unsqueeze(0).to_broadcast([P, DIM])).then_inc(w_in, 16)
                        n_w += 1
                sp.wait_ge(w_in, 16 * n_w)
                with sp.Fori(0, ROUNDS) as i:
                    sp.wait_ge(x_used, i + 1)
                    sp.dma_start(xt[:, :, :], s_x[:, bass.ds(i * RB, RB), :]).then_inc(x_in, 16)
                    sp.wait_ge(rows_ready, i + 1)
                    at = bass.ds(i * RB, RB)
                    if kind == "qkv":
                        sp.dma_start(m.d_q.rearrange("(b p) d -> p b d", p=P)[:, at, :], rowst[:, :, 0:DIM]).then_inc(rows_out, 16)
                        sp.dma_start(m.d_v.rearrange("(b p) d -> p b d", p=P)[:, at, :], rowst[:, :, DIM:2 * DIM]).then_inc(rows_out, 16)
                    elif kind == "mid":
                        sp.dma_start(m.d_xr.rearrange("(b p) d -> p b d", p=P)[:, at, :], rowst[:, :, :]).then_inc(rows_out, 16)
                        sp.dma_start(m.d_x1.rearrange("(b p) d -> p b d", p=P)[:, at, :], xt[:, :, :]).then_inc(rows_out, 16)
                    else:
                        sp.dma_start(m.d_out.rearrange("(b p) d -> p b d", p=P)[:, at, :], rowst[:, :, :]).then_inc(rows_out, 16)
                        sp.dma_start(m.d_sink[0:1, :], rowst[0:1, 0, 0:16]).then_inc(rows_out, 16)
                sp.wait_ge(rows_out, 32 + 32 * ROUNDS)

            @block.vector
            def _(dve):
                V = nc.vector
                dve.sem_inc(x_used, 1)
                dve.wait_ge(w_in, 16 * (2 * NW - (1 if kind == "mid" else 0)))
                with dve.Fori(0, ROUNDS) as i:
                    ln = Links(dve, dv, i * PER_DVE)
                    sm = Small(dve, V, ln)
                    S_ = lambda j: st[:, j, :]
                    asked = [0]
                    nb = lambda ap: bcast(ap, DIM)
                    nb1 = lambda ap: bcast(ap, DIM - 1)

                    def ask_act():
                        dve.sem_inc(ask, 1)
                        asked[0] += 1
                        dve.wait_ge(answer, i * ASKS + asked[0])

                    tp = [0]

                    def turn_and_project(biases, outs):
                        dve.sem_inc(hready, 1)
                        for g in range(RB):
                            dve.wait_ge(turned, i * (RB * passes) + tp[0] * RB + g + 1)
                            ins = V.tensor_copy(hT[:, g].rearrange("p c n -> p (c n)"), pt[:, g % 2, 0:2 * P])
                            ins.then_inc(evac, 1)
                        for b in range(RB):
                            dve.wait_ge(proj, i * (RB * passes) + tp[0] * RB + b + 1)
                            for n, (bi, o) in enumerate(zip(biases, outs)):
                                bank = pj[:, (b % 2) * 2 + n // 2, (n % 2) * DIM:(n % 2 + 1) * DIM]
                                if bi is None:
                                    last = V.tensor_copy(o(b), bank)
                                else:
                                    last = V.tensor_tensor(o(b), bank, bias[:, bi, :], ALU.add)
                            last.then_inc(proj_used, 1)
                        tp[0] += 1

                    dve.wait_ge(x_in, (i + 1) * 16)
                    if kind == "mid":
                        acc = m.acc_l0[:, bass.ds(i * (RB * AW), RB * AW)].rearrange("p (b a) -> p b a", a=AW)
                        z, zr = tmp[:, :, 0:HEADS], tmp[:, :, HEADS:2 * HEADS]
                        sm.ts(z, acc[:, :, DIM:AW], 1e-16, None, ALU.max)
                        sm.recip(zr, z)
                        for b in range(RB):
                            ab = m.acc_l0[:, bass.ds(i * (RB * AW) + b * AW, DIM)].rearrange("p (h d) -> p h d", h=HEADS)
                            ln.mark(V.tensor_tensor(xc[:, b, :].rearrange("p (h d) -> p h d", h=HEADS), ab, bcast(zr[:, b, :], DH), ALU.mult))
                        ln.wait()
                        sm.tt(xt[:, :, :], xt[:, :, :], xc[:, :, :], ALU.add)
                    if kind in ("qkv", "mid"):
                        ln.mark(V.tensor_reduce(S_(0), xt[:, :, :], axis=AX.X, op=ALU.add)); ln.wait()
                        sm.ts(S_(1), S_(0), 1.0 / DIM, None, ALU.mult)
                        sm.tt(xc[:, :, :], xt[:, :, :], nb(S_(1)), ALU.subtract)
                        if kind == "qkv":
                            dve.sem_inc(x_used, 1)
                        sm.tt(tmp[:, :, :], xc[:, :, :], xc[:, :, :], ALU.mult)
                        ln.mark(V.tensor_reduce(S_(2), tmp[:, :, :], axis=AX.X, op=ALU.add)); ln.wait()
                        sm.ts(S_(3), S_(2), 1.0 / DIM, 1e-5, ALU.mult, ALU.add)
                        ask_act()
                        sm.recip(S_(5), S_(4))
                        sm.tt(xc[:, :, :], xc[:, :, :], nb(S_(5)), ALU.mult)
                        if kind == "qkv":
                            sm.ts(xc[:, :, :], xc[:, :, :], 0.0, None, ALU.max)
                            turn = [(0, lambda b: rowst[:, b, 0:DIM]), (1, lambda b: rowst[:, b, DIM:2 * DIM]),
                                    (2, lambda b: m.tab_a[:, bass.ds(i * (RB * DIM) + b * DIM, DIM)])]
                            dve.wait_ge(rows_out, i * 32 + 32)
                            turn_and_project([t[0] for t in turn], [t[1] for t in turn])
                            ln.mark(V.memset(S_(23), 0.0)); ln.wait()
                            dve.sem_inc(rows_ready, 1)
                    if kind == "mid":
                        dve.wait_ge(rows_out, i * 32 + 32)
                        sm.ts(rowst[:, :, 0:DIM], xc[:, :, :], 0.0, None, ALU.max)
                        h = rowst[:, :, 0:DIM]
                        ln.mark(V.tensor_copy(m.tab_a[:, bass.ds(i * (RB * DIM), RB * DIM)].rearrange("p (b d) -> p b d", d=DIM), h))
                        sm.tt(tmp[:, :, 1:DIM], h[:, :, 1:DIM], h[:, :, 1:DIM], ALU.mult)
                        ln.mark(V.tensor_reduce(S_(6), tmp[:, :, 1:DIM], axis=AX.X, op=ALU.add)); ln.wait()
                        sm.ts(S_(7), h[:, :, 0], 1.0 + EPS, None, ALU.max)
                        arcosh(nc, sm, lambda o, a: ask_act(), lambda o, a: ask_act(), S_(7), [S_(j) for j in range(8, 16)])
                        ask_act()
                        sm.ts(S_(17), S_(16), 1e-15, None, ALU.max)
                        sm.recip(S_(18), S_(17))
                        sm.tt(S_(19), S_(18), S_(8), ALU.mult)
                        sm.tt(xc[:, :, :], h, nb(S_(19)), ALU.mult)
                        ln.mark(V.memset(xc[:, :, 0], 0.0)); ln.wait()
                        turn_and_project([0, None], [lambda b: m.tab_c[:, bass.ds(i * (RB * DIM) + b * DIM, DIM)],
                                                     lambda b: rowst[:, b, DIM:2 * DIM]])
                        ln.mark(V.memset(S_(23), 0.0)); ln.wait()
                        dve.sem_inc(rows_ready, 1)
                        dve.wait_ge(rows_out, (i + 1) * 32 + 32)
                        dve.sem_inc(x_used, 1)
                    if kind == "out":
                        h = m.tab_a[:, bass.ds(i * (RB * DIM), RB * DIM)].rearrange("p (b d) -> p b d", d=DIM)
                        ac = m.acc_l1[:, bass.ds(i * (RB * DIM), RB * DIM)].rearrange("p (b d) -> p b d", d=DIM)
                        hv, h0 = h[:, :, 1:DIM], h[:, :, 0]
                        t1 = tmp[:, :, 1:DIM]
                        s0, inv0, hh = S_(0), S_(1), S_(2)
                        sm.ts(s0, h0, EPS, None, ALU.max)
                        sm.recip(inv0, s0)
                        sm.ts(xc[:, :, :], ac, 0.01, None, ALU.mult)
                        sm.tt(t1, hv, xc[:, :, 1:DIM], ALU.mult)
                        ln.mark(V.tensor_reduce(S_(3), t1, axis=AX.X, op=ALU.add)); ln.wait()
                        sm.tt(xc[:, :, 0], S_(3), inv0, ALU.mult)
                        dve.wait_ge(rows_out, i * 32 + 32)
                        turn_and_project([0], [lambda b: rowst[:, b, :]])
                        ln.mark(V.memset(S_(23), 0.0)); ln.wait()
                        ask_act()
                        turn_and_project([1], [lambda b: rowst[:, b, :]])
                        sm.tt(t1, hv, hv, ALU.mult)
                        ln.mark(V.tensor_reduce(hh, t1, axis=AX.X, op=ALU.add)); ln.wait()
                        sm.tt(S_(4), h0, h0, ALU.mult)
                        sm.tt(hh, hh, S_(4), ALU.subtract)
                        sm.ts(S_(5), hh, 1.0, -EPS, ALU.add, ALU.min)
                        sm.ts(S_(5), S_(5), 1.0, None, ALU.subtract)
                        sm.tt(xc[:, :, :], h, nb(S_(5)), ALU.mult)
                        sm.tt(xc[:, :, :], xc[:, :, :], h, ALU.add)
                        sm.tt(t1, xc[:, :, 1:DIM], xc[:, :, 1:DIM], ALU.mult)
                        ln.mark(V.tensor_reduce(S_(3), t1, axis=AX.X, op=ALU.add)); ln.wait()
                        sm.tt(S_(4), xc[:, :, 0], xc[:, :, 0], ALU.mult)
                        sm.tt(S_(6), S_(3), S_(4), ALU.subtract)
                        sm.ts(S_(6), S_(6), EPS, None, ALU.max)
                        sm.ts(S_(7), hh, -1.0, 1.0 + EPS, ALU.mult, ALU.max)
                        arcosh(nc, sm, lambda o, a: ask_act(), lambda o, a: ask_act(), S_(7), [S_(j) for j in range(8, 16)])
                        sm.ts(S_(8), S_(8), math.sqrt(FAR), None, ALU.min)
                        ask_act()
                        sm.ts(S_(16), S_(16), 1e-15, None, ALU.max)
                        sm.recip(S_(16), S_(16))
                        sm.tt(S_(16), S_(16), S_(8), ALU.mult)
                        sm.tt(xc[:, :, :], xc[:, :, :], nb(S_(16)), ALU.mult)
                        sm.tt(xc[:, :, :], xc[:, :, :], rowst[:, :, :], ALU.add)
                        sm.tt(t1, hv, xc[:, :, 1:DIM], ALU.mult)
                        ln.mark(V.tensor_reduce(S_(3), t1, axis=AX.X, op=ALU.add)); ln.wait()
                        sm.tt(S_(3), S_(3), inv0, ALU.mult)
                        sm.tt(S_(3), S_(3), S_(3), ALU.mult)
                        sm.tt(t1, xc[:, :, 1:DIM], xc[:, :, 1:DIM], ALU.mult)
                        ln.mark(V.tensor_reduce(S_(4), t1, axis=AX.X, op=ALU.add)); ln.wait()
                        sm.tt(S_(6), S_(4), S_(3), ALU.subtract)
                        sm.ts(S_(6), S_(6), EPS, None, ALU.max)
                        ask_act()
                        th, ep, en, po, small, t2 = S_(17), S_(18), S_(19), S_(20), S_(21), S_(22)
                        sm.ts(th, S_(16), 1e6, 1e-15, ALU.min, ALU.max)
                        ask_act()
                        sm.ts(t2, th, 1.0, None, ALU.min)
                        sm.tt(t2, t2, t2, ALU.mult)
                        sm.ts(po, t2, 1.0 / 362880, 1.0 / 5040, ALU.mult, ALU.add)
                        sm.tt(po, po, t2, ALU.mult)
                        sm.ts(po, po, 1.0 / 120, None, ALU.add)
                        sm.tt(po, po, t2, ALU.mult)
                        sm.ts(po, po, 1.0 / 6, None, ALU.add)
                        sm.tt(po, po, t2, ALU.mult)
                        sm.ts(po, po, 1.0, None, ALU.add)
                        sm.recip(t2, th)
                        sm.tt(small, ep, en, ALU.subtract)
                        sm.tt(t2, t2, small, ALU.mult)
                        sm.ts(small, th, 1.0, None, ALU.is_lt)
                        sm.tt(po, po, small, ALU.mult)
                        sm.ts(small, th, 1.0, None, ALU.is_ge)
                        sm.tt(t2, t2, small, ALU.mult)
                        sm.tt(t2, t2, po, ALU.add)
                        sm.tt(ep, ep, en, ALU.add)
                        sm.tt(xc[:, :, :], xc[:, :, :], nb(t2), ALU.mult)
                        sm.tt(tmp[:, :, :], h, nb(ep), ALU.mult)
                        sm.tt(rowst[:, :, :], xc[:, :, :], tmp[:, :, :], ALU.add)
                        sm.tt(t1, rowst[:, :, 1:DIM], rowst[:, :, 1:DIM], ALU.mult)
                        ln.mark(V.tensor_reduce(S_(6), t1, axis=AX.X, op=ALU.add)); ln.wait()
                        sm.ts(S_(6), S_(6), 1.0, None, ALU.add)
                        ask_act()
                        sm.ts(rowst[:, :, 0], S_(16), 1.0, None, ALU.mult)
                        sm.tt(rowst[:, :, :], rowst[:, :, :], xt[:, :, :], ALU.add)
                        dve.sem_inc(x_used, 1)
                        dve.sem_inc(rows_ready, 1)
                    assert ln.n == PER_DVE, ln.n
                    assert asked[0] == ASKS, asked[0]

            @block.scalar
            def _(act):
                A = nc.scalar
                act.dma_start(m.d_sink[1:2, :], m.ones[0:1, 0:16]).then_inc(rows_out, 16)
                act.dma_start(m.d_sink[2:3, :], m.ones[0:1, 0:16]).then_inc(rows_out, 16)
                S_ = lambda j: st[:, j, :]
                one = m.ones[:, 0:1]
                jobs = {
                    "qkv": [lambda: A.activation(S_(4), S_(3), ACT.Sqrt)],
                    "mid": [lambda: A.activation(S_(4), S_(3), ACT.Sqrt),
                            lambda: A.activation(S_(11), S_(11), ACT.Sqrt),
                            lambda: A.activation(S_(12), S_(9), ACT.Ln, bias=one),
                            lambda: A.activation(S_(16), S_(6), ACT.Sqrt)],
                    "out": [lambda: A.activation(xc[:, :, :], rowst[:, :, :], ACT.Silu),
                            lambda: A.activation(S_(11), S_(11), ACT.Sqrt),
                            lambda: A.activation(S_(12), S_(9), ACT.Ln, bias=one),
                            lambda: A.activation(S_(16), S_(6), ACT.Sqrt),
                            lambda: A.activation(S_(16), S_(6), ACT.Sqrt),
                            lambda: (A.activation(S_(18), S_(17), ACT.Exp, bias=m.neg_ln2[:, 0:1]),
                                     A.activation(S_(19), S_(17), ACT.Exp, bias=m.neg_ln2[:, 0:1], scale=-1.0))[1],
                            lambda: A.activation(S_(16), S_(6), ACT.Sqrt)],
                }[kind]
                ASK = len(jobs)
                assert ASK == ASKS, ASK
                with act.Fori(0, ROUNDS) as i:
                    for j, job in enumerate(jobs):
                        act.wait_ge(ask, i * ASK + j + 1)
                        job().then_inc(answer, 1)

            @block.tensor
            def _(pe):
                T = nc.tensor
                pe.wait_ge(w_in, 16 * (2 * NW - (1 if kind == "mid" else 0)))
                T.transpose(pt[:, 0, 0:P], m.ident[:, :], m.ident[:, :])
                pe.sem_inc(evac, 2)
                pe.sem_inc(proj_used, 2)
                with pe.Fori(0, ROUNDS) as i:
                    for tp in range(passes):
                        base = i * (RB * passes) + tp * RB
                        pe.wait_ge(hready, i * passes + tp + 1)
                        for g in range(RB):
                            pe.wait_ge(evac, base + g + 1)
                            for c in range(2):
                                last = T.transpose(pt[:, g % 2, c * P:(c + 1) * P], xc[:, g, c * P:(c + 1) * P], m.ident[:, :])
                            last.then_inc(turned, 1)
                        for b in range(RB):
                            pe.wait_ge(evac, base + b + 3)
                            pe.wait_ge(proj_used, base + b + 1)
                            for n in ((0, 1, 2) if kind == "qkv" else (0, 1) if kind == "mid" else (tp,)):
                                slot = n if kind != "out" else 0
                                bank = pj[:, (b % 2) * 2 + slot // 2, (slot % 2) * DIM:(slot % 2 + 1) * DIM]
                                for c in range(2):
                                    last = T.matmul(bank, hT[:, b, c, :], wts[:, n, c, :], start=(c == 0), stop=(c == 1))
                            last.then_inc(proj, 1)


GROUPS = STEPS // G


def fetch_steps(sp, edges, used, bc_in, bc, col_in, col):
    with sp.Fori(0, GROUPS // 2) as i:
        for h in range(2):
            g = i * 2 + h
            sp.wait_ge(used, g + 1)
            sp.dma_start(col[:, h], edges.cols[:, bass.ds(g * G, G), :]).then_inc(col_in[h], 16)
            if bc is not None:
                sp.dma_start(bc[:, h, :], edges.lk[:, bass.ds(g * (G * P), G * P)].to_broadcast([P, G * P])).then_inc(bc_in[h], 16)


def gather(nc, m, pool, i, h, col_in, col, ring, got, table):
    pool.wait_ge(col_in[h], (i + 1) * 16)
    pool.sem_inc(m.nothing, 1)
    for k in range(G):
        pool.indirect_dma_start(out=ring[:, h, k, :], out_offset=None, in_=table,
                                in_offset=bass.IndirectOffsetOnAxis(ap=col[:, h, k, 0:1], axis=0)).then_inc(got[h], 16)


def scores(nc, m, edges):
    with Stage(nc, "sc") as ctx:
        sb = lambda n, s, d=F32: ctx.enter_context(nc.sbuf_tensor(f"sc_{n}", s, d))
        pb = lambda n, s: ctx.enter_context(nc.psum_tensor(f"sc_{n}", s, F32))
        sem = ctx.sem
        ring = sb("ring", [P, 2, G, DIM])
        col = sb("col", [P, 2, G, 3], I32)
        hotT = sb("hotT", [P, 2, G * P])
        prod = sb("prod", [P, 2, G, DIM])
        kx = pb("kx", [P, 4, 512])
        bc_in, col_in = ([sem(f"{n}{h}") for h in range(2)] for n in ("bc_in", "col_in"))
        got = [ctx.gather_sem(m, f"got{h}") for h in range(2)]
        used, hot, kx_in, kx_used, dv = (sem(n) for n in ("used", "hot", "kx_in", "kx_used", "dve"))
        off = sb("off", [1, STEPS], I32)
        off_in = sem("off_in")
        with nc.Block() as block:
            @block.sync
            def _(sp):
                sp.dma_start(off[:, :], edges.off[0:1, 0:STEPS]).then_inc(off_in, 16)
                sp.sem_inc(used, 2)
                fetch_steps(sp, edges, used, bc_in, hotT, col_in, col)

            @block.gpsimd
            def _(pool):
                with pool.Fori(0, GROUPS // 2) as i:
                    for h in range(2):
                        gather(nc, m, pool, i, h, col_in, col, ring, got, m.d_q)

            @block.tensor
            def _(pe):
                pe.wait_ge(off_in, 16)
                pe.sem_inc(kx_used, 4)
                with pe.Fori(0, GROUPS // 2) as i:
                    for h in range(2):
                        g = i * 2 + h
                        pe.wait_ge(hot, g + 1)
                        for k in range(G):
                            if k % 2 == 0:
                                pe.wait_ge(kx_used, g * 4 + k // 2 + 1)
                            start = pe.value_load(off[0:1, bass.ds(g * G + k, 1)], min_val=0, max_val=(NB - 1) * DIM)
                            last = nc.tensor.matmul(kx[:, k // 2, (k % 2) * DIM:(k % 2 + 1) * DIM], hotT[:, h, k * P:(k + 1) * P],
                                                    m.tab_a[:, bass.ds(start, DIM)], start=True, stop=True)
                            if k % 2 == 1:
                                last.then_inc(kx_in, 1)

            @block.vector
            def _(dve):
                V = nc.vector
                per = 2 * 5
                with dve.Fori(0, GROUPS // 2) as i:
                    ln = Links(dve, dv, i * per)
                    for h in range(2):
                        g = i * 2 + h
                        dve.wait_ge(bc_in[h], (i + 1) * 16)
                        V.tensor_scalar(hotT[:, h, :], hotT[:, h, :], m.lane[:, 0:1], None, ALU.is_equal).then_inc(hot, 1)
                        dve.wait_ge(got[h], (i + 1) * (16 * G))
                        for k2 in range(G // 2):
                            dve.wait_ge(kx_in, g * 4 + k2 + 1)
                            ln.mark(V.tensor_tensor(prod[:, h, 2 * k2:2 * k2 + 2, :], ring[:, h, 2 * k2:2 * k2 + 2, :],
                                                    kx[:, k2, :].rearrange("p (a d) -> p a d", a=2), ALU.mult))
                            ln.wait()
                            dve.sem_inc(kx_used, 1)
                        dve.sem_inc(used, 1)
                        ln.mark(V.tensor_reduce(m.sc[:, bass.ds(g * (G * HEADS), G * HEADS)],
                                                prod[:, h].rearrange("p k (h d) -> p (k h) d", d=DH), axis=AX.X, op=ALU.add))
                    assert ln.n == per


def softmax_weights(nc, m):
    with Stage(nc, "sm") as ctx:
        sb = lambda n, s, d=F32: ctx.enter_context(nc.sbuf_tensor(f"sm_{n}", s, d))
        pb = lambda n, s: ctx.enter_context(nc.psum_tensor(f"sm_{n}", s, F32))
        sem = ctx.sem
        sT = m.big[:, 0:CLEN]
        pen = m.big[:, CLEN:2 * CLEN + 1]
        fwd = m.big[:, 2 * CLEN + 1:3 * CLEN + 1]
        keys = m.big[:, 3 * CLEN + 1:4 * CLEN + 3]
        carry = sb("carry", [P, 8])
        crow = sb("crow", [1, 4, P])
        pt = pb("pt", [P, 2, 4, P])
        pr = pb("pr", [P, 2, P])
        key_in, dv, ask, answer, turned, evac, stored = (sem(n) for n in ("key_in", "dve", "ask", "answer", "turned", "evac", "stored"))
        NT = CSTEPS // 4
        with nc.Block() as block:
            @block.sync
            def _(sp):
                sp.wait_ge(dv, 1)
                sp.dma_start(m.d_skey[0:1, 0:1], carry[0:1, 0:1]).then_inc(stored, 16)
                sp.dma_start(m.d_skey[0:1, 1 + STEPS * P:2 + STEPS * P], carry[0:1, 0:1]).then_inc(stored, 16)
                sp.wait_ge(stored, 32)
                for c in range(CHUNKS):
                    sp.dma_start(keys[c * HEADS:(c + 1) * HEADS, :],
                                 m.d_skey[0:1, c * CLEN:(c + 1) * CLEN + 2].to_broadcast([HEADS, CLEN + 2])).then_inc(key_in, 16)
                sp.wait_ge(key_in, 16 * CHUNKS)

            @block.tensor
            def _(pe):
                T = nc.tensor
                pe.wait_ge(evac, 2)
                for n in range(NT):
                    if n >= 2:
                        pe.wait_ge(evac, n + 1)
                    for k in range(4):
                        last = T.transpose(pt[:, n % 2, k, :], pen[:, (4 * n + k) * P:(4 * n + k + 1) * P], m.ident[:, :])
                    last.then_inc(turned, 1)
                for r in range(2):
                    pe.wait_ge(ask, 2 * r + 1)
                    T.transpose(pr[0:1, 0, :], carry[:, 1:2], m.ident[:, :])
                    T.transpose(pr[0:1, 1, :], carry[:, 2:3], m.ident[:, :]).then_inc(answer, 1)
                    pe.wait_ge(ask, 2 * r + 2)
                    T.matmul(pr[:, 0, 0:1], crow[0:1, 3, :], m.ones[0:1, 0:1], start=True, stop=True).then_inc(answer, 1)
                pe.wait_ge(ask, 5)
                for n in range(NT):
                    pe.wait_ge(evac, NT + n + 1)
                    for k in range(4):
                        last = T.transpose(pt[:, n % 2, k, :], sT[:, (4 * n + k) * P:(4 * n + k + 1) * P], m.ident[:, :])
                    last.then_inc(turned, 1)

            @block.vector
            def _(dve):
                V = nc.vector
                ln = Links(dve, dv)
                sm = Small(dve, V, ln)
                sm.do(V.memset(carry[:, 0:1], -1.0))
                sm.do(V.tensor_copy(pen[:, 0:CLEN].rearrange("p (j c h) -> p c j h", c=CHUNKS, h=HEADS),
                                    m.sc[:, :].rearrange("p (c j h) -> p c j h", c=CHUNKS, h=HEADS)))
                dve.sem_inc(evac, 2)
                for n in range(NT):
                    dve.wait_ge(turned, n + 1)
                    V.tensor_copy(sT[:, 4 * n * P:4 * (n + 1) * P], pt[:, n % 2].rearrange("p k e -> p (k e)")).then_inc(evac, 1)
                dve.wait_ge(key_in, 16 * CHUNKS)
                sm.tt(pen, keys[:, 1:CLEN + 2], keys[:, 0:CLEN + 1], ALU.not_equal)
                sm.ts(pen, pen, -BIG, None, ALU.mult)

                def scan(out, pn, data, back, first):
                    f = (lambda ap: ap[:, ::-1]) if back else (lambda ap: ap)
                    sm.do(V.tensor_tensor_scan(f(out), f(pn), f(data), first, ALU.add, ALU.max))

                def both(out, pn, data, back, r):
                    scan(out, pn, data, back, -BIG)
                    end = 0 if back else CLEN - 1
                    sm.ts(carry[:, 1:2], out[:, end:end + 1], 1.0, None, ALU.mult)
                    sm.do(V.tensor_reduce(carry[:, 2:3], pn, axis=AX.X, op=ALU.add))
                    dve.sem_inc(ask, 1)
                    dve.wait_ge(answer, 2 * r + 1)
                    sm.do(V.tensor_copy(crow[0:1, 0:2, :], pr[0:1, :, :]))
                    sm.do(V.memset(crow[0:1, 2:4, :], -BIG))
                    for h in range(HEADS):
                        pick = lambda n: crow[0:1, n, :].rearrange("o (c h) -> o c h", h=HEADS)[:, :, h]
                        f = (lambda ap: ap[:, ::-1]) if back else (lambda ap: ap)
                        sm.do(V.tensor_tensor_scan(f(pick(2)), f(pick(1)), f(pick(0)), -BIG, ALU.add, ALU.max))
                    if back:
                        sm.do(V.tensor_copy(crow[0:1, 3, 0:P - HEADS], crow[0:1, 2, HEADS:P]))
                    else:
                        sm.do(V.tensor_copy(crow[0:1, 3, HEADS:P], crow[0:1, 2, 0:P - HEADS]))
                    dve.sem_inc(ask, 1)
                    dve.wait_ge(answer, 2 * r + 2)
                    sm.do(V.tensor_copy(carry[:, 3:4], pr[:, 0, 0:1]))
                    scan(out, pn, data, back, carry[:, 3:4])

                both(fwd, pen[:, 0:CLEN], sT, False, 0)
                both(keys[:, 0:CLEN], pen[:, 1:CLEN + 1], fwd, True, 1)
                sm.tt(sT, sT, keys[:, 0:CLEN], ALU.subtract)
                dve.sem_inc(ask, 1)
                scv = m.sc[:, :].rearrange("p (c j h) -> p c j h", c=CHUNKS, h=HEADS)
                for n in range(NT):
                    dve.wait_ge(turned, NT + n + 1)
                    if n == 0:
                        pass
                    V.tensor_copy(scv[:, :, 4 * n:4 * n + 4, :].rearrange("p c j h -> p j c h"),
                                  pt[:, n % 2].rearrange("p k (c h) -> p k c h", h=HEADS)).then_inc(evac, 1)
                dve.wait_ge(evac, 2 + 2 * NT)
                dve.sem_inc(ask, 1)

            @block.scalar
            def _(act):
                act.wait_ge(ask, 6)
                nc.scalar.activation(m.sc[:, :], m.sc[:, :], ACT.Exp, scale=SCORE).then_inc(answer, 1)


def attend(nc, m, edges):
    with Stage(nc, "at") as ctx:
        sb = lambda n, s, d=F32: ctx.enter_context(nc.sbuf_tensor(f"at_{n}", s, d))
        pb = lambda n, s: ctx.enter_context(nc.psum_tensor(f"at_{n}", s, F32))
        sem = ctx.sem
        ring = sb("ring", [P, 2, G, DIM])
        col = sb("col", [P, 2, G, 3], I32)
        pv = sb("pv", [P, 2, G, AW])
        hot = sb("hot", [P, 2, G, P])
        out = pb("out", [P, 8, 512])
        col_in = [sem(f"col_in{h}") for h in range(2)]
        got = [ctx.gather_sem(m, f"got{h}") for h in range(2)]
        used, ready, out_in, out_used, dv, zero = (sem(n) for n in ("used", "ready", "out_in", "out_used", "dve", "zero"))
        off = sb("off", [1, STEPS], I32)
        off_in = sem("off_in")
        with nc.Block() as block:
            @block.sync
            def _(sp):
                sp.dma_start(off[:, :], edges.off[1:2, 0:STEPS]).then_inc(off_in, 16)
                sp.sem_inc(used, 2)
                fetch_steps(sp, edges, used, None, None, col_in, col)

            @block.gpsimd
            def _(pool):
                with pool.Fori(0, GROUPS // 2) as i:
                    for h in range(2):
                        gather(nc, m, pool, i, h, col_in, col, ring, got, m.d_v)

            @block.tensor
            def _(pe):
                pe.sem_inc(out_used, 8)
                with pe.Fori(0, GROUPS // 2) as i:
                    for h in range(2):
                        g = i * 2 + h
                        pe.wait_ge(ready, g + 1)
                        for k in range(G):
                            pe.wait_ge(out_used, g * G + k + 1)
                            nc.tensor.matmul(out[:, k, 0:AW], hot[:, h, k, :], pv[:, h, k, :], start=True, stop=True).then_inc(out_in, 1)

            @block.vector
            def _(dve):
                dve.wait_ge(off_in, 16)
                V = nc.vector
                V.memset(m.acc_l0, 0.0).then_inc(zero, 1)
                dve.wait_ge(zero, 1)
                per = 2 * 3

                def weigh(i, h, g, ln):
                    dve.wait_ge(col_in[h], (i + 1) * 16)
                    dve.wait_ge(got[h], (i + 1) * (16 * G))
                    ex = m.sc[:, bass.ds(g * (G * HEADS), G * HEADS)].rearrange("p (k h) -> p k h", h=HEADS)
                    ln.mark(V.tensor_tensor(hot[:, h], m.ramp[:, :].unsqueeze(1).to_broadcast([P, G, P]),
                                            bcast(col[:, h, :, 1].bitcast(F32), P), ALU.is_equal))
                    ln.mark(V.tensor_copy(pv[:, h, :, DIM:AW], ex))
                    for k in range(G):
                        w = V.tensor_tensor(pv[:, h, k, 0:DIM].rearrange("p (h d) -> p h d", d=DH),
                                            ring[:, h, k, :].rearrange("p (h d) -> p h d", d=DH),
                                            bcast(m.sc[:, bass.ds(g * (G * HEADS) + k * HEADS, HEADS)], DH), ALU.mult)
                    ln.mark(w)
                    ln.wait()
                    dve.sem_inc(used, 1)
                    dve.sem_inc(ready, 1)

                with dve.Fori(0, GROUPS // 2) as i:
                    ln = Links(dve, dv, i * per)
                    for h in range(2):
                        g = i * 2 + h
                        weigh(i, h, g, ln)
                        for k in range(G):
                            start = dve.value_load(off[0:1, bass.ds(g * G + k, 1)], min_val=0, max_val=(NB - 1) * AW)
                            dve.wait_ge(out_in, g * G + k + 1)
                            row = m.acc_l0[:, bass.ds(start, AW)]
                            dve.wait_ge(zero, g * G + k + 1)
                            V.tensor_tensor(row, row, out[:, k, 0:AW], ALU.add).then_inc(zero, 1)
                            dve.wait_ge(zero, g * G + k + 2)
                            dve.sem_inc(out_used, 1)
                    assert ln.n == per


class PoolSmall(Small):

    def __init__(self, m, eng, ns, ln):
        super().__init__(eng, ns, ln)
        self.m = m

    def do(self, ins):
        self.ln.mark(ins)
        self.ln.wait()
        self.eng.sem_inc(self.m.nothing, 1)

    def recip(self, out, a):
        self.tt(out, a, self.m.mone[:, :], ALU.pow)


def messages(nc, m, edges):
    with Stage(nc, "ms") as ctx:
        sb = lambda n, s, d=F32: ctx.enter_context(nc.sbuf_tensor(f"ms_{n}", s, d))
        pb = lambda n, s: ctx.enter_context(nc.psum_tensor(f"ms_{n}", s, F32))
        sem = ctx.sem
        ring = sb("ring", [P, 2, G, 2 * DIM])
        col = sb("col", [P, 2, G, 3], I32)
        hotT = sb("hotT", [P, 2, G * P])
        hot = sb("hot", [P, 4, P])
        r_wd, r_aw2, nb2 = sb("r_wd", [P, DIM]), sb("r_aw2", [P, DIM]), sb("nb2", [P, 1])
        junk, junk2 = sb("junk", [P, 2, DIM], BF16), sb("junk2", [P, 2, DIM], BF16)
        w = sb("w", [P, 24, G])
        px = pb("px", [P, 4, 512])
        out = pb("out", [P, 4, 512])
        bc_in, col_in = ([sem(f"{n}{h}") for h in range(2)] for n in ("bc_in", "col_in"))
        got = [ctx.gather_sem(m, f"got{h}") for h in range(2)]
        (c_in, used, hotT_in, px_in, px_used, dv, pl, acc_s, u_in, v_in, uu_in, silu_in, al_in, mink_in, z_in, ln_in, ex_in,
         c_ready, hot_in, out_in, out_used, hot_s, al_s) = (sem(n) for n in (
             "c_in", "used", "hotT_in", "px_in", "px_used", "dve", "pool", "acc", "u_in", "v_in", "uu_in", "silu_in", "al_in",
             "mink_in", "z_in", "ln_in", "ex_in", "c_ready", "hot_in", "out_in", "out_used", "hot_s", "al_s"))
        W = lambda j: w[:, j, :]
        MINK, XY, UU, AL, EX, C, X0Y0, DOT = range(8)
        off = sb("off", [1, STEPS], I32)
        off_in = sem("off_in")
        with nc.Block() as block:
            @block.sync
            def _(sp):
                sp.dma_start(off[:, :], edges.off[0:1, 0:STEPS]).then_inc(off_in, 16)
                sp.dma_start(r_wd[:, :], m.in_aw1[2 * DIM:2 * DIM + 1, :].to_broadcast([P, DIM])).then_inc(c_in, 16)
                sp.dma_start(r_aw2[:, :], m.in_aw2.rearrange("n o -> o n").to_broadcast([P, DIM])).then_inc(c_in, 16)
                sp.dma_start(nb2[:, :], m.in_ab2.unsqueeze(0).to_broadcast([P, 1])).then_inc(c_in, 16)
                sp.sem_inc(used, 2)
                fetch_steps(sp, edges, used, bc_in, hotT, col_in, col)

            @block.gpsimd
            def _(pool):
                Q = nc.gpsimd
                per = 30

                def chain(h, g):
                    ln = Links(pool, pl, g * per)
                    sm = PoolSmall(m, pool, Q, ln)
                    t, A, nn, sg = W(10), [W(j) for j in range(11, 19)], W(19), W(20)

                    def after(sem, v):
                        pool.wait_ge(sem, v)
                        pool.sem_inc(m.nothing, 1)

                    after(mink_in, g + 1)
                    sm.ts(t, W(MINK), -1.0, 1.0 + EPS, ALU.mult, ALU.max)

                    def ask_ln(o, a):
                        pool.sem_inc(z_in, 1)
                        after(ln_in, g + 1)

                    arcosh(nc, sm, lambda o, a: sm.tt(o, a, m.half[:, :], ALU.pow), ask_ln, t, A)
                    sm.ts(A[0], A[0], math.sqrt(FAR), None, ALU.min)
                    sm.tt(A[0], A[0], col[:, h, :, 2].bitcast(F32), ALU.mult)
                    after(uu_in, g * G + G)
                    sm.tt(nn, ring[:, h, :, 0], ring[:, h, :, 0], ALU.mult)
                    sm.tt(nn, W(UU), nn, ALU.subtract)
                    sm.ts(nn, nn, EPS, None, ALU.max)
                    sm.tt(nn, nn, m.mhalf[:, :], ALU.pow)
                    sm.tt(A[0], A[0], nn, ALU.mult)
                    after(ex_in, g + 1)
                    sm.ts(sg, W(EX), 1.0, None, ALU.add)
                    sm.recip(sg, sg)
                    sm.tt(W(C), A[0], sg, ALU.mult)
                    pool.sem_inc(c_ready, 1)
                    assert ln.n == per, ln.n

                gather(nc, m, pool, 0, 0, col_in, col, ring, got, m.d_xr)
                with pool.Fori(0, GROUPS // 2 - 1) as i:
                    gather(nc, m, pool, i, 1, col_in, col, ring, got, m.d_xr)
                    chain(0, i * 2)
                    gather(nc, m, pool, i + 1, 0, col_in, col, ring, got, m.d_xr)
                    chain(1, i * 2 + 1)
                gather(nc, m, pool, GROUPS // 2 - 1, 1, col_in, col, ring, got, m.d_xr)
                chain(0, GROUPS - 2)
                chain(1, GROUPS - 1)

            @block.tensor
            def _(pe):
                pe.wait_ge(off_in, 16)
                T = nc.tensor
                pe.sem_inc(px_used, 2)
                pe.sem_inc(out_used, 4)
                with pe.Fori(0, GROUPS // 2) as i:
                    for h in range(2):
                        g = i * 2 + h
                        pe.wait_ge(hotT_in, g + 1)
                        pe.wait_ge(got[h], (i + 1) * (16 * G))
                        for k in range(G):
                            b = k % 4
                            if k % 2 == 0:
                                pe.wait_ge(px_used, g * 4 + k // 2 + 1)
                            start = pe.value_load(off[0:1, bass.ds(g * G + k, 1)], min_val=0, max_val=(NB - 1) * DIM)
                            hk = hotT[:, h, k * P:(k + 1) * P]
                            T.matmul(px[:, b, 0:DIM], hk, m.tab_a[:, bass.ds(start, DIM)], start=True, stop=True)
                            T.matmul(px[:, b, DIM:2 * DIM], hk, m.tab_c[:, bass.ds(start, DIM)], start=True, stop=False)
                            last = T.matmul(px[:, b, DIM:2 * DIM], m.ident[:, :], ring[:, h, k, DIM:2 * DIM], start=False, stop=True)
                            if k % 2 == 1:
                                last.then_inc(px_in, 1)
                        for k in range(G):
                            pe.wait_ge(hot_in, g * G + k + 1)
                            pe.wait_ge(out_used, g * G + k + 1)
                            T.matmul(out[:, k % 4, 0:DIM], hot[:, k % 4, :], ring[:, h, k, 0:DIM], start=True, stop=True).then_inc(out_in, 1)

            @block.scalar
            def _(act):
                A = nc.scalar
                one = m.ones[:, 0:1]
                act.wait_ge(hot_s, 1)
                with act.Fori(0, GROUPS // 2) as i:
                    for h in range(2):
                        g = i * 2 + h
                        for k in range(G):
                            act.wait_ge(u_in, g * G + k + 1)
                            if k >= 2:
                                act.wait_ge(uu_in, g * G + k - 1)
                            A.activation(junk2[:, k % 2, 1:DIM], ring[:, h, k, 1:DIM], ACT.Square, accum_out=w[:, UU, k:k + 1]).then_inc(uu_in, 1)
                            act.wait_ge(v_in, g * G + k + 1)
                            A.activation(ring[:, h, k, DIM:2 * DIM], ring[:, h, k, DIM:2 * DIM], ACT.Silu).then_inc(silu_in, 1)
                        act.wait_ge(z_in, g + 1)
                        A.activation(W(15), W(12), ACT.Ln, bias=one).then_inc(ln_in, 1)
                        act.wait_ge(al_in, g + 1)
                        A.activation(W(EX), W(AL), ACT.Exp, scale=-1.0, bias=nb2[:, 0:1]).then_inc(ex_in, 1)

            @block.vector
            def _(dve):
                dve.wait_ge(off_in, 16)
                V = nc.vector
                V.memset(m.acc_l1, 0.0).then_inc(acc_s, 1)
                dve.wait_ge(c_in, 48)
                V.tensor_scalar(nb2[:, :], nb2[:, :], -1.0, None, ALU.mult).then_inc(hot_s, 1)
                per = 2 * (4 * 7 + G)
                with dve.Fori(0, GROUPS // 2) as i:
                    ln = Links(dve, dv, i * per)
                    for h in range(2):
                        g = i * 2 + h
                        dve.wait_ge(bc_in[h], (i + 1) * 16)
                        V.tensor_scalar(hotT[:, h, :], hotT[:, h, :], m.lane[:, 0:1], None, ALU.is_equal).then_inc(hotT_in, 1)
                        dve.wait_ge(col_in[h], (i + 1) * 16)
                        dve.wait_ge(got[h], (i + 1) * (16 * G))
                        for p in range(G // 2):
                            b0, k0 = (p % 2) * 2, 2 * p
                            two = lambda j: w[:, j, k0:k0 + 2]
                            dve.wait_ge(px_in, g * 4 + p + 1)
                            for k in range(2):
                                ln.mark(V.tensor_tensor_reduce(out=junk[:, k, 1:DIM], in0=px[:, b0 + k, 1:DIM], in1=ring[:, h, k0 + k, 1:DIM],
                                                               scale=1.0, scalar=0.0, op0=ALU.mult, op1=ALU.add,
                                                               accum_out=w[:, DOT, k0 + k:k0 + k + 1]))
                            ln.mark(V.tensor_tensor(two(X0Y0), px[:, b0:b0 + 2, 0], ring[:, h, k0:k0 + 2, 0], ALU.mult))
                            ln.wait()
                            ln.mark(V.tensor_tensor(two(MINK), two(DOT), two(X0Y0), ALU.subtract)); ln.wait()
                            ln.mark(V.tensor_scalar(two(XY), two(MINK), 1.0, -EPS, ALU.add, ALU.min)); ln.wait()
                            ln.mark(V.tensor_scalar(two(XY), two(XY), 1.0, None, ALU.subtract)); ln.wait()
                            for k in range(2):
                                V.scalar_tensor_tensor(ring[:, h, k0 + k, 0:DIM], px[:, b0 + k, 0:DIM], w[:, XY, k0 + k:k0 + k + 1],
                                                       ring[:, h, k0 + k, 0:DIM], ALU.mult, ALU.add).then_inc(u_in, 1)
                            for k in range(2):
                                V.scalar_tensor_tensor(ring[:, h, k0 + k, DIM:2 * DIM], r_wd[:, :], col[:, h, k0 + k, 2:3].bitcast(F32),
                                                       px[:, b0 + k, DIM:2 * DIM], ALU.mult, ALU.add).then_inc(v_in, 1)
                            dve.wait_ge(v_in, g * G + k0 + 2)
                            dve.sem_inc(px_used, 1)
                            ln.n += 1
                            dve.sem_inc(dv, 1)
                        dve.sem_inc(mink_in, 1)
                        for k in range(G):
                            dve.wait_ge(silu_in, g * G + k + 1)
                            if k >= 2:
                                ln.wait(1)
                            ln.mark(V.tensor_tensor_reduce(out=junk[:, k % 2, :], in0=ring[:, h, k, DIM:2 * DIM], in1=r_aw2[:, :],
                                                           scale=1.0, scalar=0.0, op0=ALU.mult, op1=ALU.add,
                                                           accum_out=w[:, AL, k:k + 1]))
                        ln.wait()
                        dve.sem_inc(al_in, 1)
                        dve.wait_ge(c_ready, g + 1)

                        def scaled_hot(k):
                            V.tensor_scalar(hot[:, k % 4, :], m.ramp[:, :], col[:, h, k, 1:2].bitcast(F32), w[:, C, k:k + 1],
                                            ALU.is_equal, ALU.mult).then_inc(hot_in, 1)

                        for k in range(4):
                            scaled_hot(k)
                        for k in range(G):
                            start = dve.value_load(off[0:1, bass.ds(g * G + k, 1)], min_val=0, max_val=(NB - 1) * DIM)
                            dve.wait_ge(out_in, g * G + k + 1)
                            if k + 4 < G:
                                scaled_hot(k + 4)
                            row = m.acc_l1[:, bass.ds(start, DIM)]
                            dve.wait_ge(acc_s, g * G + k + 1)
                            V.tensor_tensor(row, row, out[:, k % 4, 0:DIM], ALU.add).then_inc(acc_s, 1)
                            dve.wait_ge(acc_s, g * G + k + 2)
                            dve.sem_inc(out_used, 1)
                        dve.sem_inc(used, 1)
                    assert ln.n == per, ln.n


_INS = ["x", "src", "dst", "edge_weight1", "L0_gnn_Wq", "L0_gnn_bq", "L0_gnn_Wk", "L0_gnn_bk", "L0_gnn_Wv", "L0_gnn_bv",
        "L1_gnn_att_w1", "L1_gnn_att_b1", "L1_gnn_att_w2", "L1_gnn_att_b2", "L1_gnn_mlp_w1", "L1_gnn_mlp_b1",
        "L1_gnn_mlp_w2", "L1_gnn_mlp_b2"]
_OUTS = [((NODES, DIM), "float32")]
_DEBUG = []


def program(nc, ins, out, dbg):
    m = Mem()
    (m.in_x, m.in_src, m.in_dst, m.in_w, m.in_wq, m.in_bq, m.in_wk, m.in_bk, m.in_wv, m.in_bv, m.in_aw1, m.in_ab1,
     m.in_aw2, m.in_ab2, m.in_mw1, m.in_mb1, m.in_mw2, m.in_mb2) = ins
    m.out = out
    with ExitStack() as ctx:
        sb = lambda n, s, d=F32: ctx.enter_context(nc.sbuf_tensor(n, s, d))
        m.ctx = ctx
        dr = lambda n, s, d=F32: nc.dram_tensor(n, s, d).ap()
        m.ramp, m.ramp16, m.lane = sb("ramp", [P, P]), sb("ramp16", [P, P], BF16), sb("lane", [P, 1])
        m.step_no = sb("step_no", [P, SCOL])
        m.ones, m.ident, m.zeros = sb("ones", [P, P]), sb("ident", [P, P]), sb("zeros", [P, P])
        m.before_row, m.before_col = sb("before_row", [P, P]), sb("before_col", [P, P])
        m.half, m.mhalf = sb("half", [P, G]), sb("mhalf", [P, G])
        m.mone, m.neg_ln2 = sb("mone", [P, G]), sb("neg_ln2", [P, 1])
        m.sink = sb("sink", [1, 2, 4])

        m.nothing = ctx.enter_context(nc.semaphore("nothing"))
        m.d_key, m.d_lo = dr("d_key", (ET, P)), dr("d_lo", (ET, P))
        m.d_key_flat, m.d_lo_flat = (d.rearrange("(o t) e -> o (t e)", o=1) for d in (m.d_key, m.d_lo))
        m.d_skey, m.d_skey2 = dr("d_skey", (1, SP_ * P + P)), dr("d_skey2", (1, SP_ * P + P))
        m.d_q, m.d_v, m.d_x1, m.d_xr = dr("d_q", (NP_, DIM)), dr("d_v", (NP_, DIM)), dr("d_x1", (NP_, DIM)), dr("d_xr", (NP_, 2 * DIM))
        m.d_sink = dr("d_sink", (4, 16))
        m.d_out = dr("d_out", (NP_, DIM))
        rec = dr("rec", (ET * P, 4), I32)
        consts(nc, m)
        by_dst, by_src = Mem(), Mem()
        for tag, e, key, other in (("by_dst", by_dst, m.in_dst, m.in_src), ("by_src", by_src, m.in_src, m.in_dst)):
            lk = dr(f"{tag}_lk", (SP_, P))
            e.lk, e.cols, e.off = lk.rearrange("(o s) e -> o (s e)", o=1), dr(f"{tag}_edge_cols", (P, SP_, 3), I32), dr(f"{tag}_block_at", (2, SP_), I32)
            sort_edges(nc, m, tag, key, other, rec, lk, e.cols, e.off, m.d_skey if e is by_dst else m.d_skey2)
        TAB, SUMS = NB * DIM, NB * AW
        m.big = sb("big", [P, 2 * TAB + SUMS])
        m.tab_a = m.big[:, 0:TAB]
        m.acc_l0 = m.big[:, TAB:TAB + SUMS]
        m.acc_l1 = m.big[:, TAB:2 * TAB]
        m.tab_c = m.big[:, TAB + SUMS:2 * TAB + SUMS]
        m.sc = m.big[:, 2 * TAB + SUMS - STEPS * HEADS:2 * TAB + SUMS]
        node_stage(nc, m, "qkv", "qkv")
        scores(nc, m, by_dst)
        softmax_weights(nc, m)
        attend(nc, m, by_dst)
        node_stage(nc, m, "mid", "mid")
        messages(nc, m, by_src)
        node_stage(nc, m, "fin", "out")
        store(nc, m)


def store(nc, m):
    with nc.semaphore("out_done") as done, nc.Block() as block:
        @block.sync
        def _(sp):
            sp.dma_start(m.out, m.d_out[0:NODES, :]).then_inc(done, 16)
            sp.wait_ge(done, 16)


def kernel(**inputs):
    import numpy as _np
    import concourse.bacc as _bacc
    from concourse import mybir as _mybir
    from concourse.bass_utils import run_bass_kernel_spmd as _run

    nc = _bacc.Bacc("TRN2", target_bir_lowering=False, num_devices=1)
    arrays, args = {}, []
    for name in _INS:
        a = _np.ascontiguousarray(inputs[name])
        if name == "x":
            a = _np.concatenate([a, _np.zeros((NP_ - NODES, DIM), a.dtype)])
        elif name in ("src", "dst"):
            a = _np.concatenate([a, _np.full(ET * P - EDGES, PAD_NODE, a.dtype)]).reshape(ET, P)
        elif name == "edge_weight1":
            a = _np.concatenate([a.reshape(-1), _np.zeros(ET * P - EDGES, a.dtype)]).reshape(ET, P)
        arrays[f"in_{name}_dram"] = a
        args.append(nc.dram_tensor(f"in_{name}_dram", a.shape, _mybir.dt.from_np(a.dtype), kind="ExternalInput").ap())
    outs = []
    for i, (shape, dtype) in enumerate(_OUTS + _DEBUG):
        dt = _mybir.dt.from_np(_np.dtype(dtype))
        outs.append(nc.dram_tensor(f"out_{i}_dram", shape, dt, kind="ExternalOutput").ap())
    program(nc, args, outs[0], outs[1:])
    r = _run(nc, [arrays], core_ids=[0])
    return r.results[0]["out_0_dram"]
```

```python
import math
from contextlib import ExitStack

import concourse.bass as bass
from concourse import mybir

F32 = mybir.dt.float32
BF16 = mybir.dt.bfloat16
I32 = mybir.dt.int32
ALU = mybir.AluOpType
ACT = mybir.ActivationFunctionType
AX = mybir.AxisListType

P = 128
NODES, DIM, HEADS = 6250, 256, 8
DH = DIM // HEADS
EDGES = 100000
NB = -(-NODES // P)
NP_ = NB * P
ET = -(-EDGES // P)
ET = -(-ET // 8) * 8
PAD_NODE = NP_ - 1
CHUNKS = P // HEADS
STEPS = -(-(ET + NB - 1) // 16) * 16
SCOL = -(-STEPS // P)
SP_ = SCOL * P
CSTEPS = STEPS // CHUNKS
CLEN = CSTEPS * P
AW = DIM + HEADS
BIG = 1e30
EPS = 1e-7
FAR = 50.0
SCORE = 1.0 / math.sqrt(DH)
G = 8


class Links:

    def __init__(self, eng, sem, base=0):
        self.eng, self.sem, self.base, self.n = eng, sem, base, 0

    def mark(self, ins):
        ins.then_inc(self.sem, 1)
        self.n += 1

    def wait(self, back=0):
        self.eng.wait_ge(self.sem, self.base + (self.n - back))


class Mem:
    pass


class Stage(ExitStack):

    def __init__(self, nc, tag):
        super().__init__()
        self.nc, self.tag, self.sems = nc, tag, []

    def sem(self, name):
        handle = self.enter_context(self.nc.semaphore(f"{self.tag}_{name}"))
        self.sems.append(handle)
        return handle

    def gather_sem(self, m, name):
        return m.ctx.enter_context(self.nc.semaphore(f"{self.tag}_{name}"))

    def close_stage(self):
        with self.nc.Block() as block:
            @block.gpsimd
            def _(pool):
                for handle in self.sems:
                    pool.sem_clear(handle)

    def __exit__(self, *error):
        if error[0] is None:
            self.close_stage()
        return super().__exit__(*error)


def bcast(ap, n):
    return ap.unsqueeze(2).to_broadcast([ap.shape[0], ap.shape[1], n])


def consts(nc, m):
    with Stage(nc, "consts") as ctx:
        sem = ctx.sem
        pool_done, load_done = sem("const_pool"), sem("const_load")
        with nc.Block() as block:

            @block.gpsimd
            def _(pool):
                ln = Links(pool, pool_done)
                ln.mark(nc.gpsimd.iota(m.ramp[:, :], pattern=[[1, P]], base=0, channel_multiplier=0,
                                       allow_small_or_imprecise_dtypes=True))
                ln.mark(nc.gpsimd.iota(m.lane[:, :], pattern=[[0, 1]], base=0, channel_multiplier=1,
                                       allow_small_or_imprecise_dtypes=True))
                ln.mark(nc.gpsimd.iota(m.step_no[:, :], pattern=[[P, SCOL]], base=0, channel_multiplier=1,
                                       allow_small_or_imprecise_dtypes=True))
                ln.mark(nc.gpsimd.memset(m.ones[:, :], 1.0))
                ln.mark(nc.gpsimd.memset(m.zeros[:, :], 0.0))
                ln.mark(nc.gpsimd.memset(m.ident[:, :], 0.0))
                ln.mark(nc.gpsimd.memset(m.half[:, :], 0.5))
                ln.mark(nc.gpsimd.memset(m.mhalf[:, :], -0.5))
                ln.mark(nc.gpsimd.memset(m.mone[:, :], -1.0))
                ln.mark(nc.gpsimd.memset(m.neg_ln2[:, :], -math.log(2.0)))
                ln.wait()
                ln.mark(nc.gpsimd.tensor_copy(m.ramp16[:, :], m.ramp[:, :]))
                ln.mark(nc.gpsimd.affine_select(out=m.ident[:, :], in_=m.ident[:, :], compare_op=ALU.not_equal, fill=1.0,
                                                base=0, pattern=[[-1, P]], channel_multiplier=1))
                ln.mark(nc.gpsimd.affine_select(out=m.before_row[:, :], in_=m.ones[:, :], compare_op=ALU.is_gt, fill=0.0,
                                                base=0, pattern=[[-1, P]], channel_multiplier=1))
                ln.mark(nc.gpsimd.affine_select(out=m.before_col[:, :], in_=m.ones[:, :], compare_op=ALU.is_gt, fill=0.0,
                                                base=0, pattern=[[1, P]], channel_multiplier=-1))
                ln.wait()



def sort_edges(nc, m, tag, key_in, other_in, rec, d_lk, d_cols, d_off, d_skey):
    with Stage(nc, tag) as ctx:
        sb = lambda n, s, d: ctx.enter_context(nc.sbuf_tensor(f"{tag}_{n}", s, d))
        pb = lambda n, s: ctx.enter_context(nc.psum_tensor(f"{tag}_{n}", s, F32))
        sem = ctx.sem
        RT = -(-ET // P)
        FULL = ET // P
        row_i = sb("row_i", [P, 2, RT, P], I32)
        hi_i = sb("hi_i", [P, 2, RT, P], I32)
        rows = sb("rows", [P, 5, RT, P], F32)
        cols = sb("cols", [P, 5, RT * P], F32)
        recs = sb("recs", [P, RT * P, 4], I32)
        hot_lo = sb("hot_lo", [P, 2, G, P], BF16)
        hot_hi = sb("hot_hi", [P, 2, G, NB], BF16)
        lo_bc = sb("lo_bc", [P, 2, G * P], F32)
        key_bc = sb("key_bc", [P, 2, G * P], F32)
        hot_loT = sb("hot_loT", [P, 2, G, P], F32)
        total = sb("total", [P, NB], F32)
        shifted = sb("shifted", [P, NB], F32)
        base = sb("base", [P, 2, G + 1, NB], F32)
        bounds = sb("bounds", [P, NB + 1], F32)
        picked = sb("picked", [P, 2, G, NB], F32)
        rank = sb("rank", [P, 2, G], F32)
        taken = sem("taken")
        credit = sb("credit", [1, 2, 4], I32)
        dup = sb("dup", [P, 2, G], F32)
        eq = sb("eq", [P, 2, P], F32)
        rank_i = sb("rank_i", [P, 2, G], I32)
        rec_st = sb("rec_st", [P, 2, G, 4], I32)
        bk = sb("bk", [P, 12, NB + 1], F32)
        bk_i = sb("bk_i", [P, 2, NB + 1], I32)
        stp = sb("stp", [P, 6, SCOL], F32)
        tile_i = sb("tile_i", [P, SCOL], I32)
        offT = sb("offT", [SCOL, 2, P], I32)
        got = sb("got", [P, 2, P, 4], I32)
        scol = sb("scol", [P, SP_, 3], I32)
        srow = sb("srow", [P, 2, 4, P], F32)
        ps_t = pb("ps_t", [P, 2, 512])
        ps_hist = pb("ps_hist", [P, 512])
        ps_up = pb("ps_up", [P, 2, 512])
        ps_look = pb("ps_look", [P, 2, 512])
        NGRP = ET // G

        loaded, split, turned, evac, stored, zeroed = (sem(n) for n in ("loaded", "split", "turned", "evac", "stored", "zeroed"))
        dl = sem("dve1")
        with nc.Block() as block:
            @block.sync
            def _(sp):
                sp.wait_ge(zeroed, 3)
                for n, src in enumerate((key_in, other_in)):
                    sp.dma_start(row_i[:, n, 0:FULL, :], src[0:FULL * P, :].rearrange("(j t) e -> t j e", t=P)).then_inc(loaded, 16)
                    sp.dma_start(row_i[0:ET - FULL * P, n, FULL, :], src[FULL * P:ET, :]).then_inc(loaded, 16)
                sp.dma_start(rows[:, 4, 0:FULL, :], m.in_w[0:FULL * P, :].rearrange("(j t) e -> t j e", t=P)).then_inc(loaded, 16)
                sp.dma_start(rows[0:ET - FULL * P, 4, FULL, :], m.in_w[FULL * P:ET, :]).then_inc(loaded, 16)
                sp.wait_ge(split, 1)
                for n, dst in ((0, m.d_key), (3, m.d_lo)):
                    sp.dma_start(dst[0:FULL * P, :].rearrange("(j t) e -> t j e", t=P), rows[:, n, 0:FULL, :]).then_inc(stored, 16)
                    sp.dma_start(dst[FULL * P:ET, :], rows[0:ET - FULL * P, n, FULL, :]).then_inc(stored, 16)
                sp.wait_ge(stored, 64)

            @block.vector
            def _(dve):
                ln = Links(dve, dl)
                nc.vector.memset(row_i[:, 0, FULL, :], 0).then_inc(zeroed, 1)
                nc.vector.memset(row_i[:, 1, FULL, :], 0).then_inc(zeroed, 1)
                nc.vector.memset(rows[:, 4, FULL, :], 0.0).then_inc(zeroed, 1)
                dve.wait_ge(loaded, 96)
                ln.mark(nc.vector.tensor_single_scalar(hi_i[:, 0], row_i[:, 0], 7, ALU.arith_shift_right))
                ln.mark(nc.vector.tensor_single_scalar(hi_i[:, 1], row_i[:, 0], P - 1, ALU.bitwise_and))
                ln.wait()
                nc.vector.tensor_copy(rows[:, 0:2], row_i[:, :])
                nc.vector.tensor_copy(rows[:, 2:4], hi_i[:, :]).then_inc(split, 1)
                for g in range(RT * 5 // 5):
                    for n in range(5):
                        u = g * 5 + n
                        dve.wait_ge(turned, u + 1)
                        nc.vector.tensor_copy(cols[:, n, g * P:(g + 1) * P], ps_t[:, u % 2, 0:P]).then_inc(evac, 1)
                dve.wait_ge(evac, RT * 5)
                nc.vector.tensor_copy(recs[:, :, 0], cols[:, 0, :])
                nc.vector.tensor_copy(recs[:, :, 1], cols[:, 1, :])
                nc.vector.tensor_copy(recs[:, :, 2].bitcast(F32), cols[:, 4, :])
                nc.vector.memset(recs[:, :, 3], 0)

            @block.tensor
            def _(pe):
                pe.wait_ge(split, 1)
                for g in range(RT):
                    for n in range(5):
                        u = g * 5 + n
                        if u >= 2:
                            pe.wait_ge(evac, u - 1)
                        nc.tensor.transpose(ps_t[:, u % 2, 0:P], rows[:, n, g, :], m.ident[:, :]).then_inc(turned, 1)

        hots, counted = sem("hots"), sem("counted")
        with nc.Block() as block:
            @block.vector
            def _(dve):
                with dve.Fori(0, NGRP // 2) as i:
                    for h in range(2):
                        dve.wait_ge(counted, i * 2 + h + 1)
                        at = bass.ds((i * 2 + h) * G, G)
                        nc.vector.tensor_tensor(hot_hi[:, h], m.ramp16[:, 0:NB].unsqueeze(1).to_broadcast([P, G, NB]),
                                                bcast(cols[:, 2, at], NB), ALU.is_equal)
                        nc.vector.tensor_tensor(hot_lo[:, h], m.ramp16[:, :].unsqueeze(1).to_broadcast([P, G, P]),
                                                bcast(cols[:, 3, at], P), ALU.is_equal).then_inc(hots, 1)

            @block.tensor
            def _(pe):
                nc.tensor.matmul(ps_hist[:, 0:NB], m.zeros[:, :], m.ident[:, 0:NB], start=True, stop=False).then_inc(counted, 2)
                with pe.Fori(0, NGRP // 2) as i:
                    for h in range(2):
                        pe.wait_ge(hots, i * 2 + h + 1)
                        for k in range(G):
                            last = nc.tensor.matmul(ps_hist[:, 0:NB], hot_lo[:, h, k], hot_hi[:, h, k], start=False, stop=False)
                        last.then_inc(counted, 1)
                nc.tensor.matmul(ps_hist[:, 0:NB], m.zeros[:, :], m.ident[:, 0:NB], start=False, stop=True)

        ready, summed = sem("ready"), sem("summed")
        dl2 = sem("dve2")
        with nc.Block() as block:
            @block.vector
            def _(dve):
                ln = Links(dve, dl2)
                V = nc.vector

                def op(ins):
                    ln.mark(ins)
                    ln.wait()

                op(V.tensor_copy(total[:, :], ps_hist[:, 0:NB]))
                op(V.memset(shifted[:, 0:1], 0.0))
                op(V.tensor_tensor_scan(shifted[:, 1:NB], m.ones[:, 0:NB - 1], total[:, 0:NB - 1], 0.0, ALU.mult, ALU.add))
                dve.sem_inc(ready, 1)
                dve.wait_ge(summed, 1)
                op(V.tensor_copy(base[:, 0, 0, :], ps_look[:, 0, 0:NB]))
                op(V.tensor_copy(bounds[:, 0:NB], ps_look[:, 1, 0:NB]))
                op(V.memset(bounds[:, NB:NB + 1], float(ET * P)))
                first, last, some, n, start, g, dg, lastk = (bk[:, j, :] for j in range(8))
                op(V.tensor_copy(bk_i[:, 0, :], bounds[:, :]))
                op(V.tensor_single_scalar(bk_i[:, 1, :], bk_i[:, 0, :], 7, ALU.arith_shift_right))
                op(V.tensor_copy(first, bk_i[:, 1, :]))
                op(V.tensor_scalar(lastk, bounds[:, :], -1.0, None, ALU.add))
                op(V.tensor_copy(bk_i[:, 0, :], lastk))
                op(V.tensor_single_scalar(bk_i[:, 1, :], bk_i[:, 0, :], 7, ALU.arith_shift_right))
                op(V.tensor_copy(last, bk_i[:, 1, :]))
                op(V.memset(n, 0.0))
                op(V.tensor_tensor(some[:, 0:NB], bounds[:, 1:NB + 1], bounds[:, 0:NB], ALU.is_gt))
                op(V.tensor_tensor(n[:, 0:NB], last[:, 1:NB + 1], first[:, 0:NB], ALU.subtract))
                op(V.scalar_tensor_tensor(n[:, 0:NB], n[:, 0:NB], 1.0, some[:, 0:NB], ALU.add, ALU.mult))
                op(V.memset(start, 0.0))
                op(V.tensor_tensor_scan(start[:, 1:NB + 1], m.ones[:, 0:NB], n[:, 0:NB], 0.0, ALU.mult, ALU.add))
                op(V.tensor_tensor(g, first, start, ALU.subtract))
                op(V.tensor_copy(dg, g))
                op(V.tensor_tensor(dg[:, 1:NB], g[:, 1:NB], g[:, 0:NB - 1], ALU.subtract))
                for j in range(SCOL):
                    s = m.step_no[:, j:j + 1]
                    op(V.tensor_scalar(bk[:, 8, 0:NB], start[:, 1:NB + 1], s, 0.0, ALU.is_le, ALU.add, accum_out=stp[:, 0, j:j + 1]))
                    op(V.scalar_tensor_tensor(bk[:, 9, 0:NB], start[:, 0:NB], s, dg[:, 0:NB], ALU.is_le, ALU.mult,
                                              accum_out=stp[:, 1, j:j + 1]))
                op(V.tensor_tensor(stp[:, 1, :], stp[:, 1, :], m.step_no[:, :], ALU.add))
                op(V.tensor_scalar(stp[:, 1, :], stp[:, 1, :], float(ET - 1), 0.0, ALU.min, ALU.max))
                op(V.tensor_copy(tile_i[:, :], stp[:, 1, :]))
                op(V.tensor_scalar(stp[:, 2, :], stp[:, 0, :], float(P), None, ALU.mult))
                op(V.tensor_scalar(stp[:, 3, :], stp[:, 0, :], float(NB - 1), float(DIM), ALU.min, ALU.mult))
                op(V.tensor_scalar(stp[:, 4, :], stp[:, 0, :], float(NB - 1), float(AW), ALU.min, ALU.mult))
                dve.sem_inc(ready, 1)
                dve.wait_ge(summed, 2)
                op(V.tensor_copy(offT[:, 0, :], ps_t[0:SCOL, 0, 0:P]))
                op(V.tensor_copy(offT[:, 1, :], ps_t[0:SCOL, 1, 0:P]))
                dve.sem_inc(ready, 1)

            @block.tensor
            def _(pe):
                pe.wait_ge(ready, 1)
                nc.tensor.matmul(ps_look[:, 0, 0:NB], m.ones[:, :], shifted[:, :], start=True, stop=False)
                nc.tensor.matmul(ps_look[:, 0, 0:NB], m.before_col[:, :], total[:, :], start=False, stop=True)
                nc.tensor.matmul(ps_look[:, 1, 0:NB], m.ones[:, :], shifted[:, :], start=True, stop=True).then_inc(summed, 1)
                pe.wait_ge(ready, 2)
                nc.tensor.transpose(ps_t[0:SCOL, 0, 0:P], stp[:, 3, :], m.ident[:, :])
                nc.tensor.transpose(ps_t[0:SCOL, 1, 0:P], stp[:, 4, :], m.ident[:, :]).then_inc(summed, 1)

            @block.sync
            def _(sp):
                sp.wait_ge(ready, 3)
                sp.dma_start(d_off.rearrange("n (j s) -> j n s", s=P), offT[:, :, :]).then_inc(stored, 16)
                sp.wait_ge(stored, 80)

        bc_in = [sem("bc_in0"), sem("bc_in1")]
        hots2, upd, tabs, looked, placed, bc_used = (sem(n) for n in ("hots2", "upd", "tabs", "looked", "placed", "bc_used"))
        dl3 = sem("dve3")
        scat = [ctx.gather_sem(m, f"scat{h}") for h in range(2)]
        with nc.Block() as block:
            @block.sync
            def _(sp):
                sp.sem_inc(bc_used, 2)
                with sp.Fori(0, NGRP // 2) as i:
                    for h in range(2):
                        g = i * 2 + h
                        sp.wait_ge(bc_used, g + 1)
                        sp.dma_start(key_bc[:, h, :], m.d_key_flat[:, bass.ds(g * (G * P), G * P)].to_broadcast([P, G * P])).then_inc(bc_in[h], 16)
                        sp.dma_start(lo_bc[:, h, :], m.d_lo_flat[:, bass.ds(g * (G * P), G * P)].to_broadcast([P, G * P])).then_inc(bc_in[h], 16)

            @block.vector
            def _(dve):
                V = nc.vector
                per = 2 * (G + 6)
                with dve.Fori(0, NGRP // 2) as i:
                    ln = Links(dve, dl3, i * per)
                    for h in range(2):
                        g = i * 2 + h
                        at = bass.ds(g * G, G)
                        dve.wait_ge(bc_in[h], (i + 1) * 32)
                        V.tensor_tensor(hot_hi[:, h], m.ramp16[:, 0:NB].unsqueeze(1).to_broadcast([P, G, NB]),
                                        bcast(cols[:, 2, at], NB), ALU.is_equal)
                        V.tensor_tensor(hot_lo[:, h], m.ramp16[:, :].unsqueeze(1).to_broadcast([P, G, P]),
                                        bcast(cols[:, 3, at], P), ALU.is_equal).then_inc(hots2, 1)
                        V.tensor_scalar(hot_loT[:, h], lo_bc[:, h, :].rearrange("p (k e) -> p k e", k=G), m.lane[:, 0:1], None, ALU.is_equal)
                        for k in range(G):
                            if k >= 2:
                                ln.wait(1)
                            ln.mark(V.scalar_tensor_tensor(eq[:, k % 2, :], key_bc[:, h, k * P:(k + 1) * P],
                                                           cols[:, 0, bass.ds(g * G + k, 1)], m.before_row[:, :],
                                                           ALU.is_equal, ALU.mult, accum_out=dup[:, h, k:k + 1]))
                        ln.wait()
                        dve.sem_inc(bc_used, 1)
                        dve.wait_ge(upd, g + 1)
                        ln.mark(V.tensor_tensor(base[:, h, 1:G + 1, :], ps_up[:, h, 0:G * NB].rearrange("p (k b) -> p k b", k=G),
                                                base[:, h, 0:1, :].to_broadcast([P, G, NB]), ALU.add))
                        ln.wait()
                        dve.sem_inc(tabs, 1)
                        ln.mark(V.tensor_copy(base[:, 1 - h, 0, :], base[:, h, G, :]))
                        dve.wait_ge(looked, g + 1)
                        ln.mark(V.tensor_tensor(picked[:, h], ps_look[:, h, 0:G * NB].rearrange("p (k b) -> p k b", k=G), hot_hi[:, h], ALU.mult))
                        ln.wait()
                        ln.mark(V.tensor_reduce(rank[:, h], picked[:, h], axis=AX.X, op=ALU.add))
                        ln.wait()
                        dve.wait_ge(scat[h], 16 + i * (16 * G))
                        ln.mark(V.tensor_tensor(rank_i[:, h], rank[:, h], dup[:, h], ALU.add))
                        ln.mark(V.tensor_copy(rec_st[:, h], recs[:, at, :]))
                        ln.wait()
                        dve.sem_inc(placed, 1)
                    assert ln.n == per

            @block.tensor
            def _(pe):
                with pe.Fori(0, NGRP // 2) as i:
                    for h in range(2):
                        g = i * 2 + h
                        pe.wait_ge(hots2, g + 1)
                        for k in range(G):
                            for j in range(k + 1):
                                last = nc.tensor.matmul(ps_up[:, h, k * NB:(k + 1) * NB], hot_lo[:, h, j], hot_hi[:, h, j],
                                                        start=(j == 0), stop=(j == k))
                        last.then_inc(upd, 1)
                        pe.wait_ge(tabs, g + 1)
                        for k in range(G):
                            last = nc.tensor.matmul(ps_look[:, h, k * NB:(k + 1) * NB], hot_loT[:, h, k], base[:, h, k, :],
                                                    start=True, stop=True)
                        last.then_inc(looked, 1)

            @block.gpsimd
            def _(pool):
                for h in range(2):
                    pool.dma_start(credit[:, h, :], d_off[0:1, 0:4]).then_inc(scat[h], 16)
                with pool.Fori(0, NGRP // 2) as i:
                    for h in range(2):
                        g = i * 2 + h
                        pool.wait_ge(placed, g + 1)
                        pool.sem_inc(taken, 1)
                        for k in range(G):
                            pool.indirect_dma_start(out=rec[:, :], out_offset=bass.IndirectOffsetOnAxis(ap=rank_i[:, h, k:k + 1], axis=0),
                                                    in_=rec_st[:, h, k, :], in_offset=None).then_inc(scat[h], 16)
                for h in range(2):
                    pool.wait_ge(scat[h], 16 + (NGRP // 2) * (16 * G))

        fetched, spread, tt, te = ([ctx.gather_sem(m, f"fetched{h}") for h in range(2)], sem("spread"), sem("tt"), sem("te"))
        st2 = [sem("kept0"), sem("kept1")]
        dl4 = sem("dve4")
        with nc.Block() as block:
            rec_tiles = rec.rearrange("(t e) w -> t (e w)", e=P)

            @block.gpsimd
            def _(pool):
                for j in range(SCOL):
                    if j >= 2:
                        pool.wait_ge(spread, j - 1)
                    pool.indirect_dma_start(out=got[:, j % 2].rearrange("p e w -> p (e w)"), out_offset=None, in_=rec_tiles,
                                            in_offset=bass.IndirectOffsetOnAxis(ap=tile_i[:, j:j + 1], axis=0)).then_inc(fetched[j % 2], 16)

            @block.vector
            def _(dve):
                V = nc.vector
                ln = Links(dve, dl4)
                for j in range(SCOL):
                    r = srow[:, j % 2]
                    dve.wait_ge(fetched[j % 2], (j // 2 + 1) * 16)
                    if j >= 2:
                        dve.wait_ge(st2[j % 2], (j // 2) * 32)
                        dve.wait_ge(te, (j - 1) * 3)
                    ln.mark(V.tensor_copy(r[:, 0, :], got[:, j % 2, :, 0]))
                    ln.mark(V.tensor_copy(r[:, 2, :], got[:, j % 2, :, 1]))
                    ln.mark(V.tensor_copy(r[:, 3, :], got[:, j % 2, :, 2].bitcast(F32)))
                    ln.wait()
                    ln.mark(V.tensor_scalar(r[:, 1, :], r[:, 0, :], stp[:, 2, j:j + 1], None, ALU.subtract))
                    ln.wait()
                    dve.sem_inc(spread, 1)
                    for n, dst in enumerate((scol[:, :, 1].bitcast(F32), scol[:, :, 0], scol[:, :, 2].bitcast(F32))):
                        u = j * 3 + n
                        dve.wait_ge(tt, u + 1)
                        V.tensor_copy(dst[:, j * P:(j + 1) * P], ps_t[:, u % 2, 0:P]).then_inc(te, 1)

            @block.tensor
            def _(pe):
                for j in range(SCOL):
                    pe.wait_ge(spread, j + 1)
                    for n in range(3):
                        u = j * 3 + n
                        if u >= 2:
                            pe.wait_ge(te, u - 1)
                        nc.tensor.transpose(ps_t[:, u % 2, 0:P], srow[:, j % 2, 1 + n, :], m.ident[:, :]).then_inc(tt, 1)

            @block.sync
            def _(sp):
                for j in range(SCOL):
                    sp.wait_ge(spread, j + 1)
                    sp.dma_start(d_skey[0:1, 1 + j * P * P:1 + (j + 1) * P * P].rearrange("o (s e) -> (o s) e", e=P), srow[:, j % 2, 0, :]).then_inc(st2[j % 2], 16)
                    sp.dma_start(d_lk[j * P:(j + 1) * P, :], srow[:, j % 2, 1, :]).then_inc(st2[j % 2], 16)
                sp.wait_ge(te, 3 * SCOL)
                sp.dma_start(d_cols, scol[:, :, :]).then_inc(stored, 16)
                sp.wait_ge(stored, 96)
                for h in range(2):
                    sp.wait_ge(st2[h], 32 * ((SCOL + 1 - h) // 2))


RB = 7
ROUNDS = NB // RB
assert ROUNDS * RB == NB


def arcosh(nc, ops, ask_sqrt, ask_ln, t, w):
    z, a, r, ln1, q, q2, s = w[1:8]
    ops.ts(a, t, 1.0, None, ALU.subtract)
    ops.ts(r, t, 1.0, None, ALU.add)
    ops.tt(r, r, a, ALU.mult)
    ask_sqrt(r, r)
    ops.tt(z, a, r, ALU.add)
    ask_ln(ln1, z)
    ops.ts(q, z, 2.0, None, ALU.add)
    ops.recip(q, q)
    ops.tt(q, q, z, ALU.mult)
    ops.tt(q2, q, q, ALU.mult)
    ops.ts(s, q2, 2.0 / 7, 2.0 / 5, ALU.mult, ALU.add)
    ops.tt(s, s, q2, ALU.mult)
    ops.ts(s, s, 2.0 / 3, None, ALU.add)
    ops.tt(s, s, q2, ALU.mult)
    ops.ts(s, s, 2.0, None, ALU.add)
    ops.tt(s, s, q, ALU.mult)
    ops.tt(s, s, ln1, ALU.subtract)
    ops.ts(a, z, 0.25, None, ALU.is_lt)
    ops.tt(s, s, a, ALU.mult)
    ops.tt(w[0], s, ln1, ALU.add)


class Small:

    def __init__(self, eng, ns, ln, mhalf=None):
        self.eng, self.ns, self.ln, self.mhalf = eng, ns, ln, mhalf

    def do(self, ins):
        self.ln.mark(ins)
        self.ln.wait()

    def ts(self, out, a, s1, s2, op0, op1=None):
        if op1 is None:
            self.do(self.ns.tensor_scalar(out, a, s1, None, op0))
        else:
            self.do(self.ns.tensor_scalar(out, a, s1, s2, op0, op1))

    def tt(self, out, a, b, op):
        self.do(self.ns.tensor_tensor(out, a, b, op))

    def recip(self, out, a):
        self.do(self.ns.reciprocal(out, a))


def node_stage(nc, m, tag, kind):
    with Stage(nc, tag) as ctx:
        sb = lambda n, s, d=F32: ctx.enter_context(nc.sbuf_tensor(f"{tag}_{n}", s, d))
        pb = lambda n, s: ctx.enter_context(nc.psum_tensor(f"{tag}_{n}", s, F32))
        sem = ctx.sem
        NW = 3 if kind == "qkv" else 2
        wts = sb("wts", [P, NW, 2, DIM])
        bias = sb("bias", [P, NW, DIM])
        xt = sb("xt", [P, RB, DIM])
        xc = sb("xc", [P, RB, DIM])
        tmp = sb("tmp", [P, RB, DIM])
        hT = sb("hT", [P, RB, 2, P])
        st = sb("st", [P, 24, RB])
        rowst = sb("rowst", [P, RB, 512 if kind != "out" else DIM])
        pt = pb("pt", [P, 2, 512])
        pj = pb("pj", [P, 4, 512])
        w_in, x_in, x_used, dv, ask, answer, turned, evac, hready, hT_ready, proj, proj_used, rows_ready, rows_out = (
            sem(n) for n in ("w_in", "x_in", "x_used", "dve", "ask", "answer", "turned", "evac", "hready", "hT_ready",
                             "proj", "proj_used", "rows_ready", "rows_out"))
        s_x = (m.d_x1 if kind == "out" else m.in_x).rearrange("(b p) d -> p b d", p=P)
        if kind == "qkv":
            mats, vecs = (m.in_wq, m.in_wv, m.in_wk), (m.in_bq, m.in_bv, m.in_bk)
        elif kind == "mid":
            mats, vecs = (m.in_aw1[0:DIM, :], m.in_aw1[DIM:2 * DIM, :]), (m.in_ab1, None)
        else:
            mats, vecs = (m.in_mw1, m.in_mw2), (m.in_mb1, m.in_mb2)
        passes = 2 if kind == "out" else 1

        PER_DVE = {"qkv": 10, "mid": 47, "out": 80}[kind]
        ASKS = {"qkv": 1, "mid": 4, "out": 7}[kind]
        

        with nc.Block() as block:
            @block.sync
            def _(sp):
                n_w = 0
                for n in range(NW):
                    sp.dma_start(wts[:, n], mats[n].rearrange("(c p) n -> p c n", p=P)).then_inc(w_in, 16)
                    n_w += 1
                    if vecs[n] is not None:
                        sp.dma_start(bias[:, n, :], vecs[n].unsqueeze(0).to_broadcast([P, DIM])).then_inc(w_in, 16)
                        n_w += 1
                sp.wait_ge(w_in, 16 * n_w)
                with sp.Fori(0, ROUNDS) as i:
                    sp.wait_ge(x_used, i + 1)
                    sp.dma_start(xt[:, :, :], s_x[:, bass.ds(i * RB, RB), :]).then_inc(x_in, 16)
                    sp.wait_ge(rows_ready, i + 1)
                    at = bass.ds(i * RB, RB)
                    if kind == "qkv":
                        sp.dma_start(m.d_q.rearrange("(b p) d -> p b d", p=P)[:, at, :], rowst[:, :, 0:DIM]).then_inc(rows_out, 16)
                        sp.dma_start(m.d_v.rearrange("(b p) d -> p b d", p=P)[:, at, :], rowst[:, :, DIM:2 * DIM]).then_inc(rows_out, 16)
                    elif kind == "mid":
                        sp.dma_start(m.d_xr.rearrange("(b p) d -> p b d", p=P)[:, at, :], rowst[:, :, :]).then_inc(rows_out, 16)
                        sp.dma_start(m.d_x1.rearrange("(b p) d -> p b d", p=P)[:, at, :], xt[:, :, :]).then_inc(rows_out, 16)
                    else:
                        sp.dma_start(m.d_out.rearrange("(b p) d -> p b d", p=P)[:, at, :], rowst[:, :, :]).then_inc(rows_out, 16)
                        sp.dma_start(m.d_sink[0:1, :], rowst[0:1, 0, 0:16]).then_inc(rows_out, 16)
                sp.wait_ge(rows_out, 32 + 32 * ROUNDS)

            @block.vector
            def _(dve):
                V = nc.vector
                dve.sem_inc(x_used, 1)
                dve.wait_ge(w_in, 16 * (2 * NW - (1 if kind == "mid" else 0)))
                with dve.Fori(0, ROUNDS) as i:
                    ln = Links(dve, dv, i * PER_DVE)
                    sm = Small(dve, V, ln)
                    S_ = lambda j: st[:, j, :]
                    asked = [0]
                    nb = lambda ap: bcast(ap, DIM)
                    nb1 = lambda ap: bcast(ap, DIM - 1)

                    def ask_act():
                        dve.sem_inc(ask, 1)
                        asked[0] += 1
                        dve.wait_ge(answer, i * ASKS + asked[0])

                    tp = [0]

                    def turn_and_project(biases, outs):
                        dve.sem_inc(hready, 1)
                        for g in range(RB):
                            dve.wait_ge(turned, i * (RB * passes) + tp[0] * RB + g + 1)
                            ins = V.tensor_copy(hT[:, g].rearrange("p c n -> p (c n)"), pt[:, g % 2, 0:2 * P])
                            ins.then_inc(evac, 1)
                        for b in range(RB):
                            dve.wait_ge(proj, i * (RB * passes) + tp[0] * RB + b + 1)
                            for n, (bi, o) in enumerate(zip(biases, outs)):
                                bank = pj[:, (b % 2) * 2 + n // 2, (n % 2) * DIM:(n % 2 + 1) * DIM]
                                if bi is None:
                                    last = V.tensor_copy(o(b), bank)
                                else:
                                    last = V.tensor_tensor(o(b), bank, bias[:, bi, :], ALU.add)
                            last.then_inc(proj_used, 1)
                        tp[0] += 1

                    dve.wait_ge(x_in, (i + 1) * 16)
                    if kind == "mid":
                        acc = m.acc_l0[:, bass.ds(i * (RB * AW), RB * AW)].rearrange("p (b a) -> p b a", a=AW)
                        z, zr = tmp[:, :, 0:HEADS], tmp[:, :, HEADS:2 * HEADS]
                        sm.ts(z, acc[:, :, DIM:AW], 1e-16, None, ALU.max)
                        sm.recip(zr, z)
                        for b in range(RB):
                            ab = m.acc_l0[:, bass.ds(i * (RB * AW) + b * AW, DIM)].rearrange("p (h d) -> p h d", h=HEADS)
                            ln.mark(V.tensor_tensor(xc[:, b, :].rearrange("p (h d) -> p h d", h=HEADS), ab, bcast(zr[:, b, :], DH), ALU.mult))
                        ln.wait()
                        sm.tt(xt[:, :, :], xt[:, :, :], xc[:, :, :], ALU.add)
                    if kind in ("qkv", "mid"):
                        ln.mark(V.tensor_reduce(S_(0), xt[:, :, :], axis=AX.X, op=ALU.add)); ln.wait()
                        sm.ts(S_(1), S_(0), 1.0 / DIM, None, ALU.mult)
                        sm.tt(xc[:, :, :], xt[:, :, :], nb(S_(1)), ALU.subtract)
                        if kind == "qkv":
                            dve.sem_inc(x_used, 1)
                        sm.tt(tmp[:, :, :], xc[:, :, :], xc[:, :, :], ALU.mult)
                        ln.mark(V.tensor_reduce(S_(2), tmp[:, :, :], axis=AX.X, op=ALU.add)); ln.wait()
                        sm.ts(S_(3), S_(2), 1.0 / DIM, 1e-5, ALU.mult, ALU.add)
                        ask_act()
                        sm.recip(S_(5), S_(4))
                        sm.tt(xc[:, :, :], xc[:, :, :], nb(S_(5)), ALU.mult)
                        if kind == "qkv":
                            sm.ts(xc[:, :, :], xc[:, :, :], 0.0, None, ALU.max)
                            turn = [(0, lambda b: rowst[:, b, 0:DIM]), (1, lambda b: rowst[:, b, DIM:2 * DIM]),
                                    (2, lambda b: m.tab_a[:, bass.ds(i * (RB * DIM) + b * DIM, DIM)])]
                            dve.wait_ge(rows_out, i * 32 + 32)
                            turn_and_project([t[0] for t in turn], [t[1] for t in turn])
                            ln.mark(V.memset(S_(23), 0.0)); ln.wait()
                            dve.sem_inc(rows_ready, 1)
                    if kind == "mid":
                        dve.wait_ge(rows_out, i * 32 + 32)
                        sm.ts(rowst[:, :, 0:DIM], xc[:, :, :], 0.0, None, ALU.max)
                        h = rowst[:, :, 0:DIM]
                        ln.mark(V.tensor_copy(m.tab_a[:, bass.ds(i * (RB * DIM), RB * DIM)].rearrange("p (b d) -> p b d", d=DIM), h))
                        sm.tt(tmp[:, :, 1:DIM], h[:, :, 1:DIM], h[:, :, 1:DIM], ALU.mult)
                        ln.mark(V.tensor_reduce(S_(6), tmp[:, :, 1:DIM], axis=AX.X, op=ALU.add)); ln.wait()
                        sm.ts(S_(7), h[:, :, 0], 1.0 + EPS, None, ALU.max)
                        arcosh(nc, sm, lambda o, a: ask_act(), lambda o, a: ask_act(), S_(7), [S_(j) for j in range(8, 16)])
                        ask_act()
                        sm.ts(S_(17), S_(16), 1e-15, None, ALU.max)
                        sm.recip(S_(18), S_(17))
                        sm.tt(S_(19), S_(18), S_(8), ALU.mult)
                        sm.tt(xc[:, :, :], h, nb(S_(19)), ALU.mult)
                        ln.mark(V.memset(xc[:, :, 0], 0.0)); ln.wait()
                        turn_and_project([0, None], [lambda b: m.tab_c[:, bass.ds(i * (RB * DIM) + b * DIM, DIM)],
                                                     lambda b: rowst[:, b, DIM:2 * DIM]])
                        ln.mark(V.memset(S_(23), 0.0)); ln.wait()
                        dve.sem_inc(rows_ready, 1)
                        dve.wait_ge(rows_out, (i + 1) * 32 + 32)
                        dve.sem_inc(x_used, 1)
                    if kind == "out":
                        h = m.tab_a[:, bass.ds(i * (RB * DIM), RB * DIM)].rearrange("p (b d) -> p b d", d=DIM)
                        ac = m.acc_l1[:, bass.ds(i * (RB * DIM), RB * DIM)].rearrange("p (b d) -> p b d", d=DIM)
                        hv, h0 = h[:, :, 1:DIM], h[:, :, 0]
                        t1 = tmp[:, :, 1:DIM]
                        s0, inv0, hh = S_(0), S_(1), S_(2)
                        sm.ts(s0, h0, EPS, None, ALU.max)
                        sm.recip(inv0, s0)
                        sm.ts(xc[:, :, :], ac, 0.01, None, ALU.mult)
                        sm.tt(t1, hv, xc[:, :, 1:DIM], ALU.mult)
                        ln.mark(V.tensor_reduce(S_(3), t1, axis=AX.X, op=ALU.add)); ln.wait()
                        sm.tt(xc[:, :, 0], S_(3), inv0, ALU.mult)
                        dve.wait_ge(rows_out, i * 32 + 32)
                        turn_and_project([0], [lambda b: rowst[:, b, :]])
                        ln.mark(V.memset(S_(23), 0.0)); ln.wait()
                        ask_act()
                        turn_and_project([1], [lambda b: rowst[:, b, :]])
                        sm.tt(t1, hv, hv, ALU.mult)
                        ln.mark(V.tensor_reduce(hh, t1, axis=AX.X, op=ALU.add)); ln.wait()
                        sm.tt(S_(4), h0, h0, ALU.mult)
                        sm.tt(hh, hh, S_(4), ALU.subtract)
                        sm.ts(S_(5), hh, 1.0, -EPS, ALU.add, ALU.min)
                        sm.ts(S_(5), S_(5), 1.0, None, ALU.subtract)
                        sm.tt(xc[:, :, :], h, nb(S_(5)), ALU.mult)
                        sm.tt(xc[:, :, :], xc[:, :, :], h, ALU.add)
                        sm.tt(t1, xc[:, :, 1:DIM], xc[:, :, 1:DIM], ALU.mult)
                        ln.mark(V.tensor_reduce(S_(3), t1, axis=AX.X, op=ALU.add)); ln.wait()
                        sm.tt(S_(4), xc[:, :, 0], xc[:, :, 0], ALU.mult)
                        sm.tt(S_(6), S_(3), S_(4), ALU.subtract)
                        sm.ts(S_(6), S_(6), EPS, None, ALU.max)
                        sm.ts(S_(7), hh, -1.0, 1.0 + EPS, ALU.mult, ALU.max)
                        arcosh(nc, sm, lambda o, a: ask_act(), lambda o, a: ask_act(), S_(7), [S_(j) for j in range(8, 16)])
                        sm.ts(S_(8), S_(8), math.sqrt(FAR), None, ALU.min)
                        ask_act()
                        sm.ts(S_(16), S_(16), 1e-15, None, ALU.max)
                        sm.recip(S_(16), S_(16))
                        sm.tt(S_(16), S_(16), S_(8), ALU.mult)
                        sm.tt(xc[:, :, :], xc[:, :, :], nb(S_(16)), ALU.mult)
                        sm.tt(xc[:, :, :], xc[:, :, :], rowst[:, :, :], ALU.add)
                        sm.tt(t1, hv, xc[:, :, 1:DIM], ALU.mult)
                        ln.mark(V.tensor_reduce(S_(3), t1, axis=AX.X, op=ALU.add)); ln.wait()
                        sm.tt(S_(3), S_(3), inv0, ALU.mult)
                        sm.tt(S_(3), S_(3), S_(3), ALU.mult)
                        sm.tt(t1, xc[:, :, 1:DIM], xc[:, :, 1:DIM], ALU.mult)
                        ln.mark(V.tensor_reduce(S_(4), t1, axis=AX.X, op=ALU.add)); ln.wait()
                        sm.tt(S_(6), S_(4), S_(3), ALU.subtract)
                        sm.ts(S_(6), S_(6), EPS, None, ALU.max)
                        ask_act()
                        th, ep, en, po, small, t2 = S_(17), S_(18), S_(19), S_(20), S_(21), S_(22)
                        sm.ts(th, S_(16), 1e6, 1e-15, ALU.min, ALU.max)
                        ask_act()
                        sm.ts(t2, th, 1.0, None, ALU.min)
                        sm.tt(t2, t2, t2, ALU.mult)
                        sm.ts(po, t2, 1.0 / 362880, 1.0 / 5040, ALU.mult, ALU.add)
                        sm.tt(po, po, t2, ALU.mult)
                        sm.ts(po, po, 1.0 / 120, None, ALU.add)
                        sm.tt(po, po, t2, ALU.mult)
                        sm.ts(po, po, 1.0 / 6, None, ALU.add)
                        sm.tt(po, po, t2, ALU.mult)
                        sm.ts(po, po, 1.0, None, ALU.add)
                        sm.recip(t2, th)
                        sm.tt(small, ep, en, ALU.subtract)
                        sm.tt(t2, t2, small, ALU.mult)
                        sm.ts(small, th, 1.0, None, ALU.is_lt)
                        sm.tt(po, po, small, ALU.mult)
                        sm.ts(small, th, 1.0, None, ALU.is_ge)
                        sm.tt(t2, t2, small, ALU.mult)
                        sm.tt(t2, t2, po, ALU.add)
                        sm.tt(ep, ep, en, ALU.add)
                        sm.tt(xc[:, :, :], xc[:, :, :], nb(t2), ALU.mult)
                        sm.tt(tmp[:, :, :], h, nb(ep), ALU.mult)
                        sm.tt(rowst[:, :, :], xc[:, :, :], tmp[:, :, :], ALU.add)
                        sm.tt(t1, rowst[:, :, 1:DIM], rowst[:, :, 1:DIM], ALU.mult)
                        ln.mark(V.tensor_reduce(S_(6), t1, axis=AX.X, op=ALU.add)); ln.wait()
                        sm.ts(S_(6), S_(6), 1.0, None, ALU.add)
                        ask_act()
                        sm.ts(rowst[:, :, 0], S_(16), 1.0, None, ALU.mult)
                        sm.tt(rowst[:, :, :], rowst[:, :, :], xt[:, :, :], ALU.add)
                        dve.sem_inc(x_used, 1)
                        dve.sem_inc(rows_ready, 1)
                    assert ln.n == PER_DVE, ln.n
                    assert asked[0] == ASKS, asked[0]

            @block.scalar
            def _(act):
                A = nc.scalar
                act.dma_start(m.d_sink[1:2, :], m.ones[0:1, 0:16]).then_inc(rows_out, 16)
                act.dma_start(m.d_sink[2:3, :], m.ones[0:1, 0:16]).then_inc(rows_out, 16)
                S_ = lambda j: st[:, j, :]
                one = m.ones[:, 0:1]
                jobs = {
                    "qkv": [lambda: A.activation(S_(4), S_(3), ACT.Sqrt)],
                    "mid": [lambda: A.activation(S_(4), S_(3), ACT.Sqrt),
                            lambda: A.activation(S_(11), S_(11), ACT.Sqrt),
                            lambda: A.activation(S_(12), S_(9), ACT.Ln, bias=one),
                            lambda: A.activation(S_(16), S_(6), ACT.Sqrt)],
                    "out": [lambda: A.activation(xc[:, :, :], rowst[:, :, :], ACT.Silu),
                            lambda: A.activation(S_(11), S_(11), ACT.Sqrt),
                            lambda: A.activation(S_(12), S_(9), ACT.Ln, bias=one),
                            lambda: A.activation(S_(16), S_(6), ACT.Sqrt),
                            lambda: A.activation(S_(16), S_(6), ACT.Sqrt),
                            lambda: (A.activation(S_(18), S_(17), ACT.Exp, bias=m.neg_ln2[:, 0:1]),
                                     A.activation(S_(19), S_(17), ACT.Exp, bias=m.neg_ln2[:, 0:1], scale=-1.0))[1],
                            lambda: A.activation(S_(16), S_(6), ACT.Sqrt)],
                }[kind]
                ASK = len(jobs)
                assert ASK == ASKS, ASK
                with act.Fori(0, ROUNDS) as i:
                    for j, job in enumerate(jobs):
                        act.wait_ge(ask, i * ASK + j + 1)
                        job().then_inc(answer, 1)

            @block.tensor
            def _(pe):
                T = nc.tensor
                pe.wait_ge(w_in, 16 * (2 * NW - (1 if kind == "mid" else 0)))
                T.transpose(pt[:, 0, 0:P], m.ident[:, :], m.ident[:, :])
                pe.sem_inc(evac, 2)
                pe.sem_inc(proj_used, 2)
                with pe.Fori(0, ROUNDS) as i:
                    for tp in range(passes):
                        base = i * (RB * passes) + tp * RB
                        pe.wait_ge(hready, i * passes + tp + 1)
                        for g in range(RB):
                            pe.wait_ge(evac, base + g + 1)
                            for c in range(2):
                                last = T.transpose(pt[:, g % 2, c * P:(c + 1) * P], xc[:, g, c * P:(c + 1) * P], m.ident[:, :])
                            last.then_inc(turned, 1)
                        for b in range(RB):
                            pe.wait_ge(evac, base + b + 3)
                            pe.wait_ge(proj_used, base + b + 1)
                            for n in ((0, 1, 2) if kind == "qkv" else (0, 1) if kind == "mid" else (tp,)):
                                slot = n if kind != "out" else 0
                                bank = pj[:, (b % 2) * 2 + slot // 2, (slot % 2) * DIM:(slot % 2 + 1) * DIM]
                                for c in range(2):
                                    last = T.matmul(bank, hT[:, b, c, :], wts[:, n, c, :], start=(c == 0), stop=(c == 1))
                            last.then_inc(proj, 1)


GROUPS = STEPS // G
DEPTH = 4
assert GROUPS % DEPTH == 0


def fetch_steps(sp, edges, rounds, used, bc_in, bc, col_in, col, n=G):
    depth = len(col_in)
    with sp.Fori(0, rounds) as i:
        for h in range(depth):
            g = i * depth + h
            sp.wait_ge(used, g + 1)
            sp.dma_start(col[:, h], edges.cols[:, bass.ds(g * n, n), :]).then_inc(col_in[h], 16)
            if bc is not None:
                sp.dma_start(bc[:, h, :], edges.lk[:, bass.ds(g * (n * P), n * P)].to_broadcast([P, n * P])).then_inc(bc_in[h], 16)


def gather(m, pool, i, h, col_in, col, ring, got, table, n=G):
    pool.wait_ge(col_in[h], (i + 1) * 16)
    pool.sem_inc(m.nothing, 1)
    for k in range(n):
        pool.indirect_dma_start(out=ring[:, h, k, :], out_offset=None, in_=table,
                                in_offset=bass.IndirectOffsetOnAxis(ap=col[:, h, k, 0:1], axis=0)).then_inc(got[h], 16)


class Starts:

    def __init__(self, eng, tag, off, top):
        self.eng, self.tag, self.off, self.top, self.sets = eng, tag, off, top, 0

    def load(self, step, n=4):
        self.sets += 1
        regs = [self.eng.alloc_register(name=f"{self.tag}_start{self.sets}_{j}") for j in range(n)]
        self.eng.load(regs, self.off[0:1, bass.ds(step, n)])
        return [self.eng.snap(r, min_val=0, max_val=self.top) for r in regs]


def scores(nc, m, edges):
    with Stage(nc, "sc") as ctx:
        sb = lambda n, s, d=F32: ctx.enter_context(nc.sbuf_tensor(f"sc_{n}", s, d))
        pb = lambda n, s: ctx.enter_context(nc.psum_tensor(f"sc_{n}", s, F32))
        sem = ctx.sem
        ring = sb("ring", [P, DEPTH, G, DIM])
        col = sb("col", [P, DEPTH, G, 3], I32)
        hotT = sb("hotT", [P, DEPTH, G * P])
        prod = m.acc_l0[:, 0:G * DIM].rearrange("p (g d) -> p g d", d=DIM)
        off = sb("off", [1, STEPS], I32)
        kx = pb("kx", [P, 8, 512])
        bc_in, col_in = ([sem(f"{n}{h}") for h in range(DEPTH)] for n in ("bc_in", "col_in"))
        got = [ctx.gather_sem(m, f"got{h}") for h in range(DEPTH)]
        used, hot, kx_in, kx_used, dv, off_in = (sem(n) for n in ("used", "hot", "kx_in", "kx_used", "dve", "off_in"))
        ROUND = GROUPS // DEPTH
        with nc.Block() as block:
            @block.sync
            def _(sp):
                sp.dma_start(off[:, :], edges.off[0:1, 0:STEPS]).then_inc(off_in, 16)
                sp.sem_inc(used, DEPTH)
                fetch_steps(sp, edges, ROUND, used, bc_in, hotT, col_in, col)

            @block.gpsimd
            def _(pool):
                with pool.Fori(0, ROUND) as i:
                    for h in range(DEPTH):
                        gather(m, pool, i, h, col_in, col, ring, got, m.d_q)

            @block.tensor
            def _(pe):
                pe.wait_ge(off_in, 16)
                pe.sem_inc(kx_used, 8)
                starts = Starts(pe, "sc", off, (NB - 1) * DIM)
                with pe.Fori(0, ROUND) as i:
                    for h in range(DEPTH):
                        g = i * DEPTH + h
                        at = starts.load(g * G) + starts.load(g * G + 4)
                        pe.wait_ge(hot, g + 1)
                        for k in range(G):
                            b = (h * 4 + k // 2) % 8
                            if k % 2 == 0:
                                pe.wait_ge(kx_used, g * 4 + k // 2 + 1)
                            last = nc.tensor.matmul(kx[:, b, (k % 2) * DIM:(k % 2 + 1) * DIM], hotT[:, h, k * P:(k + 1) * P],
                                                    m.tab_a[:, bass.ds(at[k], DIM)], start=True, stop=True)
                            if k % 2 == 1:
                                last.then_inc(kx_in, 1)

            @block.vector
            def _(dve):
                V = nc.vector
                with dve.Fori(0, ROUND) as i:
                    ln = Links(dve, dv, i * DEPTH)
                    for h in range(DEPTH):
                        g = i * DEPTH + h
                        dve.wait_ge(bc_in[h], (i + 1) * 16)
                        V.tensor_scalar(hotT[:, h, :], hotT[:, h, :], m.lane[:, 0:1], None, ALU.is_equal).then_inc(hot, 1)
                        dve.wait_ge(got[h], (i + 1) * (16 * G))
                        for k2 in range(G // 2):
                            dve.wait_ge(kx_in, g * 4 + k2 + 1)
                            V.tensor_tensor(prod[:, 2 * k2:2 * k2 + 2, :], ring[:, h, 2 * k2:2 * k2 + 2, :],
                                            kx[:, (h * 4 + k2) % 8, :].rearrange("p (a d) -> p a d", a=2), ALU.mult).then_inc(kx_used, 1)
                        dve.wait_ge(kx_used, g * 4 + 12)
                        dve.sem_inc(used, 1)
                        ln.mark(V.tensor_reduce(m.sc[:, bass.ds(g * (G * HEADS), G * HEADS)],
                                                prod[:, :].rearrange("p k (h d) -> p (k h) d", d=DH), axis=AX.X, op=ALU.add))
                    assert ln.n == DEPTH


def softmax_weights(nc, m):
    with Stage(nc, "sm") as ctx:
        sb = lambda n, s, d=F32: ctx.enter_context(nc.sbuf_tensor(f"sm_{n}", s, d))
        pb = lambda n, s: ctx.enter_context(nc.psum_tensor(f"sm_{n}", s, F32))
        sem = ctx.sem
        sT = m.big[:, 0:CLEN]
        pen = m.big[:, CLEN:2 * CLEN + 1]
        fwd = m.big[:, 2 * CLEN + 1:3 * CLEN + 1]
        keys = m.big[:, 3 * CLEN + 1:4 * CLEN + 3]
        carry = sb("carry", [P, 8])
        crow = sb("crow", [1, 4, P])
        pt = pb("pt", [P, 2, 4, P])
        pr = pb("pr", [P, 2, P])
        key_in, dv, ask, answer, turned, evac, stored = (sem(n) for n in ("key_in", "dve", "ask", "answer", "turned", "evac", "stored"))
        NT = CSTEPS // 4
        with nc.Block() as block:
            @block.sync
            def _(sp):
                sp.wait_ge(dv, 1)
                sp.dma_start(m.d_skey[0:1, 0:1], carry[0:1, 0:1]).then_inc(stored, 16)
                sp.dma_start(m.d_skey[0:1, 1 + STEPS * P:2 + STEPS * P], carry[0:1, 0:1]).then_inc(stored, 16)
                sp.wait_ge(stored, 32)
                for c in range(CHUNKS):
                    sp.dma_start(keys[c * HEADS:(c + 1) * HEADS, :],
                                 m.d_skey[0:1, c * CLEN:(c + 1) * CLEN + 2].to_broadcast([HEADS, CLEN + 2])).then_inc(key_in, 16)
                sp.wait_ge(key_in, 16 * CHUNKS)

            @block.tensor
            def _(pe):
                T = nc.tensor
                pe.wait_ge(evac, 2)
                for n in range(NT):
                    if n >= 2:
                        pe.wait_ge(evac, n + 1)
                    for k in range(4):
                        last = T.transpose(pt[:, n % 2, k, :], pen[:, (4 * n + k) * P:(4 * n + k + 1) * P], m.ident[:, :])
                    last.then_inc(turned, 1)
                for r in range(2):
                    pe.wait_ge(ask, 2 * r + 1)
                    T.transpose(pr[0:1, 0, :], carry[:, 1:2], m.ident[:, :])
                    T.transpose(pr[0:1, 1, :], carry[:, 2:3], m.ident[:, :]).then_inc(answer, 1)
                    pe.wait_ge(ask, 2 * r + 2)
                    T.matmul(pr[:, 0, 0:1], crow[0:1, 3, :], m.ones[0:1, 0:1], start=True, stop=True).then_inc(answer, 1)
                pe.wait_ge(ask, 5)
                for n in range(NT):
                    pe.wait_ge(evac, NT + n + 1)
                    for k in range(4):
                        last = T.transpose(pt[:, n % 2, k, :], sT[:, (4 * n + k) * P:(4 * n + k + 1) * P], m.ident[:, :])
                    last.then_inc(turned, 1)

            @block.vector
            def _(dve):
                V = nc.vector
                ln = Links(dve, dv)
                sm = Small(dve, V, ln)
                sm.do(V.memset(carry[:, 0:1], -1.0))
                sm.do(V.tensor_copy(pen[:, 0:CLEN].rearrange("p (j c h) -> p c j h", c=CHUNKS, h=HEADS),
                                    m.sc[:, :].rearrange("p (c j h) -> p c j h", c=CHUNKS, h=HEADS)))
                dve.sem_inc(evac, 2)
                for n in range(NT):
                    dve.wait_ge(turned, n + 1)
                    V.tensor_copy(sT[:, 4 * n * P:4 * (n + 1) * P], pt[:, n % 2].rearrange("p k e -> p (k e)")).then_inc(evac, 1)
                dve.wait_ge(key_in, 16 * CHUNKS)
                sm.tt(pen, keys[:, 1:CLEN + 2], keys[:, 0:CLEN + 1], ALU.not_equal)
                sm.ts(pen, pen, -BIG, None, ALU.mult)

                def scan(out, pn, data, back, first):
                    f = (lambda ap: ap[:, ::-1]) if back else (lambda ap: ap)
                    sm.do(V.tensor_tensor_scan(f(out), f(pn), f(data), first, ALU.add, ALU.max))

                def both(out, pn, data, back, r):
                    scan(out, pn, data, back, -BIG)
                    end = 0 if back else CLEN - 1
                    sm.ts(carry[:, 1:2], out[:, end:end + 1], 1.0, None, ALU.mult)
                    sm.do(V.tensor_reduce(carry[:, 2:3], pn, axis=AX.X, op=ALU.add))
                    dve.sem_inc(ask, 1)
                    dve.wait_ge(answer, 2 * r + 1)
                    sm.do(V.tensor_copy(crow[0:1, 0:2, :], pr[0:1, :, :]))
                    sm.do(V.memset(crow[0:1, 2:4, :], -BIG))
                    for h in range(HEADS):
                        pick = lambda n: crow[0:1, n, :].rearrange("o (c h) -> o c h", h=HEADS)[:, :, h]
                        f = (lambda ap: ap[:, ::-1]) if back else (lambda ap: ap)
                        sm.do(V.tensor_tensor_scan(f(pick(2)), f(pick(1)), f(pick(0)), -BIG, ALU.add, ALU.max))
                    if back:
                        sm.do(V.tensor_copy(crow[0:1, 3, 0:P - HEADS], crow[0:1, 2, HEADS:P]))
                    else:
                        sm.do(V.tensor_copy(crow[0:1, 3, HEADS:P], crow[0:1, 2, 0:P - HEADS]))
                    dve.sem_inc(ask, 1)
                    dve.wait_ge(answer, 2 * r + 2)
                    sm.do(V.tensor_copy(carry[:, 3:4], pr[:, 0, 0:1]))
                    scan(out, pn, data, back, carry[:, 3:4])

                both(fwd, pen[:, 0:CLEN], sT, False, 0)
                both(keys[:, 0:CLEN], pen[:, 1:CLEN + 1], fwd, True, 1)
                sm.tt(sT, sT, keys[:, 0:CLEN], ALU.subtract)
                dve.sem_inc(ask, 1)
                scv = m.sc[:, :].rearrange("p (c j h) -> p c j h", c=CHUNKS, h=HEADS)
                for n in range(NT):
                    dve.wait_ge(turned, NT + n + 1)
                    if n == 0:
                        pass
                    V.tensor_copy(scv[:, :, 4 * n:4 * n + 4, :].rearrange("p c j h -> p j c h"),
                                  pt[:, n % 2].rearrange("p k (c h) -> p k c h", h=HEADS)).then_inc(evac, 1)
                dve.wait_ge(evac, 2 + 2 * NT)
                dve.sem_inc(ask, 1)

            @block.scalar
            def _(act):
                act.wait_ge(ask, 6)
                nc.scalar.activation(m.sc[:, :], m.sc[:, :], ACT.Exp, scale=SCORE).then_inc(answer, 1)


def attend(nc, m, edges):
    with Stage(nc, "at") as ctx:
        sb = lambda n, s, d=F32: ctx.enter_context(nc.sbuf_tensor(f"at_{n}", s, d))
        pb = lambda n, s: ctx.enter_context(nc.psum_tensor(f"at_{n}", s, F32))
        sem = ctx.sem
        ring = m.tab_a[:, 0:DEPTH * G * DIM].rearrange("p (t g d) -> p t g d", t=DEPTH, d=DIM)
        col = sb("col", [P, DEPTH, G, 3], I32)
        pv = sb("pv", [P, 2, G, AW])
        hot = sb("hot", [P, 2, G, P])
        off = sb("off", [1, STEPS], I32)
        out = pb("out", [P, 8, 512])
        col_in = [sem(f"col_in{h}") for h in range(DEPTH)]
        got = [ctx.gather_sem(m, f"got{h}") for h in range(DEPTH)]
        used, ready, out_in, summed, dv, off_in = (sem(n) for n in ("used", "ready", "out_in", "summed", "dve", "off_in"))
        ROUND = GROUPS // DEPTH
        with nc.Block() as block:
            @block.sync
            def _(sp):
                sp.dma_start(off[:, :], edges.off[1:2, 0:STEPS]).then_inc(off_in, 16)
                sp.sem_inc(used, DEPTH)
                fetch_steps(sp, edges, ROUND, used, None, None, col_in, col)

            @block.gpsimd
            def _(pool):
                with pool.Fori(0, ROUND) as i:
                    for h in range(DEPTH):
                        gather(m, pool, i, h, col_in, col, ring, got, m.d_v)

            @block.tensor
            def _(pe):
                with pe.Fori(0, ROUND) as i:
                    for h in range(DEPTH):
                        g = i * DEPTH + h
                        pe.wait_ge(ready, g + 1)
                        for k in range(G):
                            pe.wait_ge(summed, g * G + k + 1)
                            nc.tensor.matmul(out[:, k, 0:AW], hot[:, h % 2, k, :], pv[:, h % 2, k, :], start=True, stop=True).then_inc(out_in, 1)

            @block.vector
            def _(dve):
                V = nc.vector
                dve.wait_ge(off_in, 16)
                V.memset(m.acc_l0, 0.0).then_inc(summed, 8)
                starts = Starts(dve, "at", off, (NB - 1) * AW)

                def weigh(i, h):
                    g = i * DEPTH + h
                    dve.wait_ge(col_in[h], (i + 1) * 16)
                    V.tensor_tensor(hot[:, h % 2], m.ramp[:, :].unsqueeze(1).to_broadcast([P, G, P]),
                                    bcast(col[:, h, :, 1].bitcast(F32), P), ALU.is_equal)
                    at = bass.ds(g * (G * HEADS), G * HEADS)
                    V.tensor_copy(pv[:, h % 2, :, DIM:AW], m.sc[:, at].rearrange("p (k h) -> p k h", h=HEADS))
                    dve.wait_ge(got[h], (i + 1) * (16 * G))
                    V.tensor_tensor(pv[:, h % 2, :, 0:DIM].rearrange("p k (h d) -> p k h d", d=DH),
                                    ring[:, h].rearrange("p k (h d) -> p k h d", d=DH),
                                    m.sc[:, at].rearrange("p (k h) -> p k h", h=HEADS).unsqueeze(3).to_broadcast([P, G, HEADS, DH]),
                                    ALU.mult).then_inc(ready, 1)
                    dve.wait_ge(ready, g + 1)
                    dve.sem_inc(used, 1)

                def add(i, h, at):
                    g = i * DEPTH + h
                    for k in range(G):
                        row = m.acc_l0[:, bass.ds(at[k], AW)]
                        dve.wait_ge(out_in, g * G + k + 1)
                        dve.wait_ge(summed, g * G + k + 8)
                        V.tensor_tensor(row, row, out[:, k, 0:AW], ALU.add).then_inc(summed, 1)

                def round_(i, last):
                    for h in range(DEPTH):
                        g = i * DEPTH + h
                        at = starts.load(g * G) + starts.load(g * G + 4)
                        if h + 1 < DEPTH:
                            weigh(i, h + 1)
                        elif not last:
                            weigh(i + 1, 0)
                        add(i, h, at)

                weigh(0, 0)
                with dve.Fori(0, ROUND - 1) as i:
                    round_(i, False)
                round_(ROUND - 1, True)


class PoolSmall(Small):

    def __init__(self, m, eng, ns, ln):
        super().__init__(eng, ns, ln)
        self.m = m

    def do(self, ins):
        self.ln.mark(ins)
        self.ln.wait()
        self.eng.sem_inc(self.m.nothing, 1)

    def stt(self, out, a, s1, b, op0, op1):
        self.ts(out, a, s1, None, op0)
        self.tt(out, out, b, op1)


THIRDS = 3
MG = 6
PAIRS = MG // 2
MROUNDS = -(-STEPS // (THIRDS * MG))
MSTEPS = MROUNDS * THIRDS * MG
assert MSTEPS <= SP_ and MROUNDS >= 3


def messages(nc, m, edges):
    with Stage(nc, "ms") as ctx:
        sb = lambda n, s, d=F32: ctx.enter_context(nc.sbuf_tensor(f"ms_{n}", s, d))
        pb = lambda n, s: ctx.enter_context(nc.psum_tensor(f"ms_{n}", s, F32))
        sem = ctx.sem
        ring = sb("ring", [P, THIRDS, MG, 2 * DIM])
        col = sb("col", [P, THIRDS, MG, 3], I32)
        hotT = sb("hotT", [P, THIRDS, MG * P])
        hot = sb("hot", [P, 3, P])
        r_wd, r_aw2, nb2 = sb("r_wd", [P, DIM]), sb("r_aw2", [P, DIM]), sb("nb2", [P, 1])
        junk, junk2 = sb("junk", [P, 2, DIM], BF16), sb("junk2", [P, 2, DIM], BF16)
        w = sb("w", [P, THIRDS, 20, MG])
        off = sb("off", [1, MSTEPS], I32)
        px = pb("px", [P, 6, 512])
        out = pb("out", [P, 2, 512])
        bc_in, col_in = ([sem(f"{n}{h}") for h in range(THIRDS)] for n in ("bc_in", "col_in"))
        got = [ctx.gather_sem(m, f"got{h}") for h in range(THIRDS)]
        (c_in, used, hotT_in, px_in, dv, pl, summed, u_in, v_in, uu_in, silu_in, al_in, mink_in, ab_in, root_in, z_in, ln_in,
         nn_in, norm_in, ex_in, den_in, rden_in, c_ready, hot_in, out_in, nb2_in, off_in) = (sem(n) for n in (
             "c_in", "used", "hotT_in", "px_in", "dve", "pool", "summed", "u_in", "v_in", "uu_in", "silu_in", "al_in", "mink_in",
             "ab_in", "root_in", "z_in", "ln_in", "nn_in", "norm_in", "ex_in", "den_in", "rden_in", "c_ready", "hot_in",
             "out_in", "nb2_in", "off_in"))
        MINK, XY, UU, AL, EX, C, X0Y0, DOT, T, A, R, ROOT, Z, S, LN, NN, DEN, DIST = range(18)
        U0 = 2 * PAIRS
        with nc.Block() as block:
            @block.sync
            def _(sp):
                sp.dma_start(r_wd[:, :], m.in_aw1[2 * DIM:2 * DIM + 1, :].to_broadcast([P, DIM])).then_inc(c_in, 16)
                sp.dma_start(r_aw2[:, :], m.in_aw2.rearrange("n o -> o n").to_broadcast([P, DIM])).then_inc(c_in, 16)
                sp.dma_start(nb2[:, :], m.in_ab2.unsqueeze(0).to_broadcast([P, 1])).then_inc(c_in, 16)
                sp.dma_start(off[:, :], edges.off[0:1, 0:MSTEPS]).then_inc(off_in, 16)
                sp.sem_inc(used, THIRDS)
                fetch_steps(sp, edges, MROUNDS, used, bc_in, hotT, col_in, col, MG)

            @block.gpsimd
            def _(pool):
                GP = nc.gpsimd
                PER = 21

                def chain(i, h):
                    g = i * THIRDS + h
                    ln = Links(pool, pl, g * PER)
                    sm = PoolSmall(m, pool, GP, ln)
                    W = lambda j: w[:, h, j, :]

                    def after(sem, v):
                        pool.wait_ge(sem, v)
                        pool.sem_inc(m.nothing, 1)

                    after(mink_in, g + 1)
                    sm.ts(W(T), W(MINK), -1.0, 1.0 + EPS, ALU.mult, ALU.max)
                    sm.ts(W(A), W(T), 1.0, None, ALU.subtract)
                    sm.stt(W(R), W(T), 1.0, W(A), ALU.add, ALU.mult)
                    pool.sem_inc(ab_in, 1)
                    sm.ts(W(S), W(A), 3.0 / 160, -1.0 / 12, ALU.mult, ALU.add)
                    sm.tt(W(S), W(S), W(A), ALU.mult)
                    after(uu_in, g * MG + MG)
                    sm.tt(W(NN), ring[:, h, :, 0], ring[:, h, :, 0], ALU.mult)
                    sm.tt(W(NN), W(UU), W(NN), ALU.subtract)
                    sm.ts(W(NN), W(NN), EPS, None, ALU.max)
                    pool.sem_inc(nn_in, 1)
                    after(root_in, g * 2 + 2)
                    sm.tt(W(Z), W(A), W(R), ALU.add)
                    pool.sem_inc(z_in, 1)
                    sm.stt(W(S), W(S), 1.0, W(ROOT), ALU.add, ALU.mult)
                    sm.ts(W(A), W(A), 0.01, None, ALU.is_lt)
                    after(ln_in, g + 1)
                    sm.tt(W(S), W(S), W(LN), ALU.subtract)
                    sm.tt(W(S), W(S), W(A), ALU.mult)
                    sm.tt(W(DIST), W(S), W(LN), ALU.add)
                    sm.stt(W(DIST), W(DIST), math.sqrt(FAR), col[:, h, :, 2].bitcast(F32), ALU.min, ALU.mult)
                    after(norm_in, g + 1)
                    after(ex_in, g + 1)
                    sm.stt(W(DEN), W(EX), 1.0, W(NN), ALU.add, ALU.mult)
                    pool.sem_inc(den_in, 1)
                    after(rden_in, g + 1)
                    sm.tt(W(C), W(DIST), W(DEN), ALU.mult)
                    pool.sem_inc(c_ready, 1)
                    assert ln.n == PER, ln.n

                def round_(i, last):
                    for h in range(THIRDS):
                        if h + 1 < THIRDS:
                            gather(m, pool, i, h + 1, col_in, col, ring, got, m.d_xr, MG)
                        elif not last:
                            gather(m, pool, i + 1, 0, col_in, col, ring, got, m.d_xr, MG)
                        chain(i, h)

                gather(m, pool, 0, 0, col_in, col, ring, got, m.d_xr, MG)
                with pool.Fori(0, MROUNDS - 1) as i:
                    round_(i, False)
                round_(MROUNDS - 1, True)

            @block.tensor
            def _(pe):
                TE = nc.tensor
                pe.wait_ge(off_in, 16)
                starts = Starts(pe, "ms", off, (NB - 1) * DIM)

                def near(i, h, pairs):
                    g = i * THIRDS + h
                    at = starts.load(g * MG + 2 * pairs[0], 2 * len(pairs))
                    if pairs[0] == 0:
                        pe.wait_ge(hotT_in, g + 1)
                        pe.wait_ge(got[h], (i + 1) * (16 * MG))
                    for p in pairs:
                        pe.wait_ge(u_in, (g * PAIRS + p) * 2 + 2)
                        for k in (2 * p, 2 * p + 1):
                            b = k % (2 * PAIRS)
                            hk = hotT[:, h, k * P:(k + 1) * P]
                            rows = bass.ds(at[k - 2 * pairs[0]], DIM)
                            TE.matmul(px[:, b, 0:DIM], hk, m.tab_a[:, rows], start=True, stop=True)
                            TE.matmul(px[:, b, DIM:2 * DIM], hk, m.tab_c[:, rows], start=True, stop=False)
                            last = TE.matmul(px[:, b, DIM:2 * DIM], m.ident[:, :], ring[:, h, k, DIM:2 * DIM], start=False, stop=True)
                        last.then_inc(px_in, 1)

                def sums(i, h):
                    g = i * THIRDS + h
                    for k in range(MG):
                        pe.wait_ge(hot_in, g * MG + k + 1)
                        pe.wait_ge(summed, g * MG + k + 1)
                        TE.matmul(out[:, k % 2, 0:DIM], hot[:, k % 3, :], ring[:, h, k, 0:DIM], start=True, stop=True).then_inc(out_in, 1)

                def round_(i, first, last):
                    for h in range(THIRDS):
                        near(i, h, (2,))
                        if h + 1 < THIRDS:
                            near(i, h + 1, (0, 1))
                        elif not last:
                            near(i + 1, 0, (0, 1))
                        if h > 0:
                            sums(i, h - 1)
                        elif not first:
                            sums(i - 1, THIRDS - 1)

                near(0, 0, (0, 1))
                round_(0, True, False)
                with pe.Fori(1, MROUNDS - 1) as i:
                    round_(i, False, False)
                round_(MROUNDS - 1, False, True)
                sums(MROUNDS - 1, THIRDS - 1)

            @block.scalar
            def _(act):
                AC = nc.scalar
                one = m.ones[:, 0:1]
                act.wait_ge(nb2_in, 1)
                with act.Fori(0, MROUNDS) as i:
                    for h in range(THIRDS):
                        g = i * THIRDS + h
                        W = lambda j: w[:, h, j, :]
                        for k in range(MG):
                            act.wait_ge(v_in, g * MG + k + 1)
                            AC.activation(ring[:, h, k, DIM:2 * DIM], ring[:, h, k, DIM:2 * DIM], ACT.Silu).then_inc(silu_in, 1)
                            act.wait_ge(u_in, U0 + g * MG + k + 1)
                            if k >= 2:
                                act.wait_ge(uu_in, g * MG + k - 1)
                            AC.activation(junk2[:, k % 2, 1:DIM], ring[:, h, k, 1:DIM], ACT.Square,
                                          accum_out=w[:, h, UU, k:k + 1]).then_inc(uu_in, 1)
                        act.wait_ge(ab_in, g + 1)
                        AC.activation(W(R), W(R), ACT.Sqrt).then_inc(root_in, 1)
                        AC.activation(W(ROOT), W(A), ACT.Sqrt, scale=2.0).then_inc(root_in, 1)
                        act.wait_ge(nn_in, g + 1)
                        AC.activation(W(NN), W(NN), ACT.Sqrt).then_inc(norm_in, 1)
                        act.wait_ge(z_in, g + 1)
                        AC.activation(W(LN), W(Z), ACT.Ln, bias=one).then_inc(ln_in, 1)
                        act.wait_ge(al_in, g + 1)
                        AC.activation(W(EX), W(AL), ACT.Exp, scale=-1.0, bias=nb2[:, 0:1]).then_inc(ex_in, 1)

            @block.vector
            def _(dve):
                V = nc.vector
                V.memset(m.acc_l1, 0.0).then_inc(summed, 2)
                dve.wait_ge(c_in, 48)
                V.tensor_scalar(nb2[:, :], nb2[:, :], -1.0, None, ALU.mult).then_inc(nb2_in, 1)
                dve.wait_ge(off_in, 16)
                dve.sem_inc(u_in, U0)
                starts = Starts(dve, "ms", off, (NB - 1) * DIM)
                PER = 5 * PAIRS + MG

                def compare(i, h):
                    dve.wait_ge(bc_in[h], (i + 1) * 16)
                    V.tensor_scalar(hotT[:, h, :], hotT[:, h, :], m.lane[:, 0:1], None, ALU.is_equal).then_inc(hotT_in, 1)

                def work(i, h, nxt, before_pair):
                    g = i * THIRDS + h
                    ln = Links(dve, dv, g * PER)
                    dve.wait_ge(col_in[h], (i + 1) * 16)
                    dve.wait_ge(got[h], (i + 1) * (16 * MG))
                    for p in range(PAIRS):
                        if p == PAIRS - 1 and nxt is not None:
                            compare(*nxt)
                        if p == 1 and before_pair is not None:
                            before_pair()
                        b0 = k0 = 2 * p
                        two = lambda j: w[:, h, j, k0:k0 + 2]
                        dve.wait_ge(px_in, g * PAIRS + p + 1)

                        def add_wd(k):
                            V.scalar_tensor_tensor(ring[:, h, k0 + k, DIM:2 * DIM], r_wd[:, :], col[:, h, k0 + k, 2:3].bitcast(F32),
                                                   px[:, b0 + k, DIM:2 * DIM], ALU.mult, ALU.add).then_inc(v_in, 1)

                        ln.mark(V.tensor_tensor(two(X0Y0), px[:, b0:b0 + 2, 0], ring[:, h, k0:k0 + 2, 0], ALU.mult))
                        for k in range(2):
                            ln.mark(V.tensor_tensor_reduce(out=junk[:, k, 1:DIM], in0=px[:, b0 + k, 1:DIM], in1=ring[:, h, k0 + k, 1:DIM],
                                                           scale=1.0, scalar=0.0, op0=ALU.mult, op1=ALU.add,
                                                           accum_out=w[:, h, DOT, k0 + k:k0 + k + 1]))
                        add_wd(0)
                        ln.wait()
                        ln.mark(V.tensor_tensor(two(MINK), two(DOT), two(X0Y0), ALU.subtract))
                        add_wd(1)
                        ln.wait()
                        ln.mark(V.tensor_scalar(two(XY), two(MINK), -1.0 - EPS, None, ALU.min)); ln.wait()
                        for k in range(2):
                            V.scalar_tensor_tensor(ring[:, h, k0 + k, 0:DIM], px[:, b0 + k, 0:DIM], w[:, h, XY, k0 + k:k0 + k + 1],
                                                   ring[:, h, k0 + k, 0:DIM], ALU.mult, ALU.add).then_inc(u_in, 1)
                    dve.sem_inc(mink_in, 1)
                    for k in range(MG):
                        dve.wait_ge(silu_in, g * MG + k + 1)
                        if k >= 2:
                            ln.wait(1)
                        ln.mark(V.tensor_tensor_reduce(out=junk[:, k % 2, :], in0=ring[:, h, k, DIM:2 * DIM], in1=r_aw2[:, :],
                                                       scale=1.0, scalar=0.0, op0=ALU.mult, op1=ALU.add,
                                                       accum_out=w[:, h, AL, k:k + 1]))
                    ln.wait()
                    dve.sem_inc(al_in, 1)
                    assert ln.n == PER, ln.n

                def reciprocals(i, h):
                    dve.wait_ge(den_in, i * THIRDS + h + 1)
                    V.reciprocal(w[:, h, DEN, :], w[:, h, DEN, :]).then_inc(rden_in, 1)

                def sums(i, h, at):
                    g = i * THIRDS + h
                    dve.wait_ge(c_ready, g + 1)

                    def scaled_hot(k):
                        V.tensor_scalar(hot[:, k % 3, :], m.ramp[:, :], col[:, h, k, 1:2].bitcast(F32), w[:, h, C, k:k + 1],
                                        ALU.is_equal, ALU.mult).then_inc(hot_in, 1)

                    for k in range(3):
                        scaled_hot(k)
                    for k in range(MG):
                        dve.wait_ge(out_in, g * MG + k + 1)
                        if k + 3 < MG:
                            scaled_hot(k + 3)
                        row = m.acc_l1[:, bass.ds(at[k], DIM)]
                        dve.wait_ge(summed, g * MG + k + 2)
                        V.tensor_tensor(row, row, out[:, k % 2, 0:DIM], ALU.add).then_inc(summed, 1)
                    dve.sem_inc(used, 1)

                def round_(i, first, last):
                    for h in range(THIRDS):
                        before = (i, h - 1) if h > 0 else (i - 1, THIRDS - 1)
                        after = (i, h + 1) if h + 1 < THIRDS else (i + 1, 0)
                        some = not (first and h == 0)
                        if some:
                            g = before[0] * THIRDS + before[1]
                            at = starts.load(g * MG) + starts.load(g * MG + 4, 2)
                        work(i, h, after if not (last and h + 1 == THIRDS) else None,
                             (lambda: reciprocals(*before)) if some else None)
                        if some:
                            sums(*before, at)

                compare(0, 0)
                round_(0, True, False)
                with dve.Fori(1, MROUNDS - 1) as i:
                    round_(i, False, False)
                round_(MROUNDS - 1, False, True)
                end = (MROUNDS - 1, THIRDS - 1)
                g = end[0] * THIRDS + end[1]
                at = starts.load(g * MG) + starts.load(g * MG + 4, 2)
                reciprocals(*end)
                sums(*end, at)


_INS = ["x", "src", "dst", "edge_weight1", "L0_gnn_Wq", "L0_gnn_bq", "L0_gnn_Wk", "L0_gnn_bk", "L0_gnn_Wv", "L0_gnn_bv",
        "L1_gnn_att_w1", "L1_gnn_att_b1", "L1_gnn_att_w2", "L1_gnn_att_b2", "L1_gnn_mlp_w1", "L1_gnn_mlp_b1",
        "L1_gnn_mlp_w2", "L1_gnn_mlp_b2"]
_OUTS = [((NODES, DIM), "float32")]
_DEBUG = []


def program(nc, ins, out, dbg):
    m = Mem()
    (m.in_x, m.in_src, m.in_dst, m.in_w, m.in_wq, m.in_bq, m.in_wk, m.in_bk, m.in_wv, m.in_bv, m.in_aw1, m.in_ab1,
     m.in_aw2, m.in_ab2, m.in_mw1, m.in_mb1, m.in_mw2, m.in_mb2) = ins
    m.out = out
    with ExitStack() as ctx:
        sb = lambda n, s, d=F32: ctx.enter_context(nc.sbuf_tensor(n, s, d))
        m.ctx = ctx
        dr = lambda n, s, d=F32: nc.dram_tensor(n, s, d).ap()
        m.ramp, m.ramp16, m.lane = sb("ramp", [P, P]), sb("ramp16", [P, P], BF16), sb("lane", [P, 1])
        m.step_no = sb("step_no", [P, SCOL])
        m.ones, m.ident, m.zeros = sb("ones", [P, P]), sb("ident", [P, P]), sb("zeros", [P, P])
        m.before_row, m.before_col = sb("before_row", [P, P]), sb("before_col", [P, P])
        m.half, m.mhalf = sb("half", [P, G]), sb("mhalf", [P, G])
        m.mone, m.neg_ln2 = sb("mone", [P, G]), sb("neg_ln2", [P, 1])
        m.sink = sb("sink", [1, 2, 4])

        m.nothing = ctx.enter_context(nc.semaphore("nothing"))
        m.d_key, m.d_lo = dr("d_key", (ET, P)), dr("d_lo", (ET, P))
        m.d_key_flat, m.d_lo_flat = (d.rearrange("(o t) e -> o (t e)", o=1) for d in (m.d_key, m.d_lo))
        m.d_skey, m.d_skey2 = dr("d_skey", (1, SP_ * P + P)), dr("d_skey2", (1, SP_ * P + P))
        m.d_q, m.d_v, m.d_x1, m.d_xr = dr("d_q", (NP_, DIM)), dr("d_v", (NP_, DIM)), dr("d_x1", (NP_, DIM)), dr("d_xr", (NP_, 2 * DIM))
        m.d_sink = dr("d_sink", (4, 16))
        m.d_out = dr("d_out", (NP_, DIM))
        rec = dr("rec", (ET * P, 4), I32)
        consts(nc, m)
        by_dst, by_src = Mem(), Mem()
        for tag, e, key, other in (("by_dst", by_dst, m.in_dst, m.in_src), ("by_src", by_src, m.in_src, m.in_dst)):
            lk = dr(f"{tag}_lk", (SP_, P))
            e.lk, e.cols, e.off = lk.rearrange("(o s) e -> o (s e)", o=1), dr(f"{tag}_edge_cols", (P, SP_, 3), I32), dr(f"{tag}_block_at", (2, SP_), I32)
            sort_edges(nc, m, tag, key, other, rec, lk, e.cols, e.off, m.d_skey if e is by_dst else m.d_skey2)
        TAB, SUMS = NB * DIM, NB * AW
        m.big = sb("big", [P, 2 * TAB + SUMS])
        m.tab_a = m.big[:, 0:TAB]
        m.acc_l0 = m.big[:, TAB:TAB + SUMS]
        m.acc_l1 = m.big[:, TAB:2 * TAB]
        m.tab_c = m.big[:, TAB + SUMS:2 * TAB + SUMS]
        m.sc = m.big[:, 2 * TAB + SUMS - STEPS * HEADS:2 * TAB + SUMS]
        node_stage(nc, m, "qkv", "qkv")
        scores(nc, m, by_dst)
        softmax_weights(nc, m)
        attend(nc, m, by_dst)
        node_stage(nc, m, "mid", "mid")
        messages(nc, m, by_src)
        node_stage(nc, m, "fin", "out")
        store(nc, m)


def store(nc, m):
    with nc.semaphore("out_done") as done, nc.Block() as block:
        @block.sync
        def _(sp):
            sp.dma_start(m.out, m.d_out[0:NODES, :]).then_inc(done, 16)
            sp.wait_ge(done, 16)


def kernel(**inputs):
    import numpy as _np
    import concourse.bacc as _bacc
    from concourse import mybir as _mybir
    from concourse.bass_utils import run_bass_kernel_spmd as _run

    nc = _bacc.Bacc("TRN2", target_bir_lowering=False, num_devices=1)
    arrays, args = {}, []
    for name in _INS:
        a = _np.ascontiguousarray(inputs[name])
        if name == "x":
            a = _np.concatenate([a, _np.zeros((NP_ - NODES, DIM), a.dtype)])
        elif name in ("src", "dst"):
            a = _np.concatenate([a, _np.full(ET * P - EDGES, PAD_NODE, a.dtype)]).reshape(ET, P)
        elif name == "edge_weight1":
            a = _np.concatenate([a.reshape(-1), _np.zeros(ET * P - EDGES, a.dtype)]).reshape(ET, P)
        arrays[f"in_{name}_dram"] = a
        args.append(nc.dram_tensor(f"in_{name}_dram", a.shape, _mybir.dt.from_np(a.dtype), kind="ExternalInput").ap())
    outs = []
    for i, (shape, dtype) in enumerate(_OUTS + _DEBUG):
        dt = _mybir.dt.from_np(_np.dtype(dtype))
        outs.append(nc.dram_tensor(f"out_{i}_dram", shape, dt, kind="ExternalOutput").ap())
    program(nc, args, outs[0], outs[1:])
    r = _run(nc, [arrays], core_ids=[0])
    return r.results[0]["out_0_dram"]
```

```python
import math
from contextlib import ExitStack

import concourse.bass as bass
from concourse import mybir

F32 = mybir.dt.float32
BF16 = mybir.dt.bfloat16
I32 = mybir.dt.int32
I16 = mybir.dt.int16
ALU = mybir.AluOpType
ACT = mybir.ActivationFunctionType
AX = mybir.AxisListType

P = 128
NODES, DIM, HEADS = 6250, 256, 8
DH = DIM // HEADS
EDGES = 100000
NB = -(-NODES // P)
NP_ = NB * P
ET = -(-EDGES // P)
ET = -(-ET // 8) * 8
PAD_NODE = NP_ - 1
CHUNKS = P // HEADS
STEPS = -(-(ET + NB - 1) // 16) * 16
SCOL = -(-STEPS // P)
SP_ = SCOL * P
CSTEPS = STEPS // CHUNKS
CLEN = CSTEPS * P
AW = DIM + HEADS
BIG = 1e30
EPS = 1e-7
FAR = 50.0
SCORE = 1.0 / math.sqrt(DH)
G = 8


class Links:

    def __init__(self, eng, sem, base=0):
        self.eng, self.sem, self.base, self.n = eng, sem, base, 0

    def mark(self, ins):
        ins.then_inc(self.sem, 1)
        self.n += 1

    def wait(self, back=0):
        self.eng.wait_ge(self.sem, self.base + (self.n - back))


class Mem:
    pass


class Stage(ExitStack):

    def __init__(self, nc, tag):
        super().__init__()
        self.nc, self.tag, self.sems = nc, tag, []

    def sem(self, name):
        handle = self.enter_context(self.nc.semaphore(f"{self.tag}_{name}"))
        self.sems.append(handle)
        return handle

    def gather_sem(self, m, name):
        return m.ctx.enter_context(self.nc.semaphore(f"{self.tag}_{name}"))

    def close_stage(self):
        with self.nc.Block() as block:
            @block.gpsimd
            def _(pool):
                for handle in self.sems:
                    pool.sem_clear(handle)

    def __exit__(self, *error):
        if error[0] is None:
            self.close_stage()
        return super().__exit__(*error)


def bcast(ap, n):
    return ap.unsqueeze(2).to_broadcast([ap.shape[0], ap.shape[1], n])


def consts(nc, m):
    with Stage(nc, "consts") as ctx:
        sem = ctx.sem
        pool_done, load_done = sem("const_pool"), sem("const_load")
        with nc.Block() as block:

            @block.gpsimd
            def _(pool):
                ln = Links(pool, pool_done)
                ln.mark(nc.gpsimd.iota(m.ramp[:, :], pattern=[[1, P]], base=0, channel_multiplier=0,
                                       allow_small_or_imprecise_dtypes=True))
                ln.mark(nc.gpsimd.iota(m.lane[:, :], pattern=[[0, 1]], base=0, channel_multiplier=1,
                                       allow_small_or_imprecise_dtypes=True))
                ln.mark(nc.gpsimd.iota(m.step_no[:, :], pattern=[[P, SCOL]], base=0, channel_multiplier=1,
                                       allow_small_or_imprecise_dtypes=True))
                ln.mark(nc.gpsimd.memset(m.ones[:, :], 1.0))
                ln.mark(nc.gpsimd.memset(m.zeros[:, :], 0.0))
                ln.mark(nc.gpsimd.memset(m.ident[:, :], 0.0))
                ln.mark(nc.gpsimd.memset(m.neg_ln2[:, :], -math.log(2.0)))
                ln.wait()
                ln.mark(nc.gpsimd.tensor_copy(m.ramp16[:, :], m.ramp[:, :]))
                ln.mark(nc.gpsimd.affine_select(out=m.ident[:, :], in_=m.ident[:, :], compare_op=ALU.not_equal, fill=1.0,
                                                base=0, pattern=[[-1, P]], channel_multiplier=1))
                ln.mark(nc.gpsimd.affine_select(out=m.before_row[:, :], in_=m.ones[:, :], compare_op=ALU.is_gt, fill=0.0,
                                                base=0, pattern=[[-1, P]], channel_multiplier=1))
                ln.mark(nc.gpsimd.affine_select(out=m.before_col[:, :], in_=m.ones[:, :], compare_op=ALU.is_gt, fill=0.0,
                                                base=0, pattern=[[1, P]], channel_multiplier=-1))
                ln.wait()



def sort_edges(nc, m, tag, key_in, other_in, rec, d_lk, d_cols, d_off, d_skey):
    with Stage(nc, tag) as ctx:
        sb = lambda n, s, d: ctx.enter_context(nc.sbuf_tensor(f"{tag}_{n}", s, d))
        pb = lambda n, s: ctx.enter_context(nc.psum_tensor(f"{tag}_{n}", s, F32))
        sem = ctx.sem
        RT = -(-ET // P)
        FULL = ET // P
        row_i = sb("row_i", [P, 2, RT, P], I32)
        hi_i = sb("hi_i", [P, 2, RT, P], I32)
        rows = sb("rows", [P, 5, RT, P], F32)
        cols = sb("cols", [P, 5, RT * P], F32)
        recs = sb("recs", [P, RT * P, 4], I32)
        hot_lo = sb("hot_lo", [P, 2, G, P], BF16)
        hot_hi = sb("hot_hi", [P, 2, G, NB], BF16)
        lo_bc = sb("lo_bc", [P, 2, G * P], F32)
        key_bc = sb("key_bc", [P, 2, G * P], F32)
        hot_loT = sb("hot_loT", [P, 2, G, P], F32)
        total = sb("total", [P, NB], F32)
        shifted = sb("shifted", [P, NB], F32)
        base = sb("base", [P, 2, G + 1, NB], F32)
        bounds = sb("bounds", [P, NB + 1], F32)
        picked = sb("picked", [P, 2, G, NB], F32)
        rank = sb("rank", [P, 2, G], F32)
        taken = sem("taken")
        credit = sb("credit", [1, 2, 8], I16)
        dup = sb("dup", [P, 2, G], F32)
        eq = sb("eq", [P, 2, P], F32)
        rank_i = sb("rank_i", [P, 2, G], I32)
        rec_st = sb("rec_st", [P, 2, G, 4], I32)
        bk = sb("bk", [P, 12, NB + 1], F32)
        bk_i = sb("bk_i", [P, 2, NB + 1], I32)
        stp = sb("stp", [P, 6, SCOL], F32)
        tile_i = sb("tile_i", [P, SCOL], I32)
        offT = sb("offT", [SCOL, 2, P], I16)
        got = sb("got", [P, 2, P, 4], I32)
        scol = sb("scol", [P, SP_, 3], I32)
        srow = sb("srow", [P, 2, 4, P], F32)
        ps_t = pb("ps_t", [P, 2, 512])
        ps_hist = pb("ps_hist", [P, 512])
        ps_up = pb("ps_up", [P, 2, 512])
        ps_look = pb("ps_look", [P, 2, 512])
        NGRP = ET // G

        loaded, split, turned, evac, stored, zeroed = (sem(n) for n in ("loaded", "split", "turned", "evac", "stored", "zeroed"))
        dl = sem("dve1")
        with nc.Block() as block:
            @block.sync
            def _(sp):
                sp.wait_ge(zeroed, 3)
                for n, src in enumerate((key_in, other_in)):
                    sp.dma_start(row_i[:, n, 0:FULL, :], src[0:FULL * P, :].rearrange("(j t) e -> t j e", t=P)).then_inc(loaded, 16)
                    sp.dma_start(row_i[0:ET - FULL * P, n, FULL, :], src[FULL * P:ET, :]).then_inc(loaded, 16)
                sp.dma_start(rows[:, 4, 0:FULL, :], m.in_w[0:FULL * P, :].rearrange("(j t) e -> t j e", t=P)).then_inc(loaded, 16)
                sp.dma_start(rows[0:ET - FULL * P, 4, FULL, :], m.in_w[FULL * P:ET, :]).then_inc(loaded, 16)
                sp.wait_ge(split, 1)
                for n, dst in ((0, m.d_key), (3, m.d_lo)):
                    sp.dma_start(dst[0:FULL * P, :].rearrange("(j t) e -> t j e", t=P), rows[:, n, 0:FULL, :]).then_inc(stored, 16)
                    sp.dma_start(dst[FULL * P:ET, :], rows[0:ET - FULL * P, n, FULL, :]).then_inc(stored, 16)
                sp.wait_ge(stored, 64)

            @block.vector
            def _(dve):
                ln = Links(dve, dl)
                nc.vector.memset(row_i[:, 0, FULL, :], 0).then_inc(zeroed, 1)
                nc.vector.memset(row_i[:, 1, FULL, :], 0).then_inc(zeroed, 1)
                nc.vector.memset(rows[:, 4, FULL, :], 0.0).then_inc(zeroed, 1)
                dve.wait_ge(loaded, 96)
                ln.mark(nc.vector.tensor_single_scalar(hi_i[:, 0], row_i[:, 0], 7, ALU.arith_shift_right))
                ln.mark(nc.vector.tensor_single_scalar(hi_i[:, 1], row_i[:, 0], P - 1, ALU.bitwise_and))
                ln.wait()
                nc.vector.tensor_copy(rows[:, 0:2], row_i[:, :])
                nc.vector.tensor_copy(rows[:, 2:4], hi_i[:, :]).then_inc(split, 1)
                for g in range(RT * 5 // 5):
                    for n in range(5):
                        u = g * 5 + n
                        dve.wait_ge(turned, u + 1)
                        nc.vector.tensor_copy(cols[:, n, g * P:(g + 1) * P], ps_t[:, u % 2, 0:P]).then_inc(evac, 1)
                dve.wait_ge(evac, RT * 5)
                nc.vector.tensor_copy(recs[:, :, 0], cols[:, 0, :])
                nc.vector.tensor_copy(recs[:, :, 1], cols[:, 1, :])
                nc.vector.tensor_copy(recs[:, :, 2].bitcast(F32), cols[:, 4, :])
                nc.vector.memset(recs[:, :, 3], 0)

            @block.tensor
            def _(pe):
                pe.wait_ge(split, 1)
                for g in range(RT):
                    for n in range(5):
                        u = g * 5 + n
                        if u >= 2:
                            pe.wait_ge(evac, u - 1)
                        nc.tensor.transpose(ps_t[:, u % 2, 0:P], rows[:, n, g, :], m.ident[:, :]).then_inc(turned, 1)

        hots, counted = sem("hots"), sem("counted")
        with nc.Block() as block:
            @block.vector
            def _(dve):
                with dve.Fori(0, NGRP // 2) as i:
                    for h in range(2):
                        dve.wait_ge(counted, i * 2 + h + 1)
                        at = bass.ds((i * 2 + h) * G, G)
                        nc.vector.tensor_tensor(hot_hi[:, h], m.ramp16[:, 0:NB].unsqueeze(1).to_broadcast([P, G, NB]),
                                                bcast(cols[:, 2, at], NB), ALU.is_equal)
                        nc.vector.tensor_tensor(hot_lo[:, h], m.ramp16[:, :].unsqueeze(1).to_broadcast([P, G, P]),
                                                bcast(cols[:, 3, at], P), ALU.is_equal).then_inc(hots, 1)

            @block.tensor
            def _(pe):
                nc.tensor.matmul(ps_hist[:, 0:NB], m.zeros[:, :], m.ident[:, 0:NB], start=True, stop=False).then_inc(counted, 2)
                with pe.Fori(0, NGRP // 2) as i:
                    for h in range(2):
                        pe.wait_ge(hots, i * 2 + h + 1)
                        for k in range(G):
                            last = nc.tensor.matmul(ps_hist[:, 0:NB], hot_lo[:, h, k], hot_hi[:, h, k], start=False, stop=False)
                        last.then_inc(counted, 1)
                nc.tensor.matmul(ps_hist[:, 0:NB], m.zeros[:, :], m.ident[:, 0:NB], start=False, stop=True)

        ready, summed = sem("ready"), sem("summed")
        dl2 = sem("dve2")
        with nc.Block() as block:
            @block.vector
            def _(dve):
                ln = Links(dve, dl2)
                V = nc.vector

                def op(ins):
                    ln.mark(ins)
                    ln.wait()

                op(V.tensor_copy(total[:, :], ps_hist[:, 0:NB]))
                op(V.memset(shifted[:, 0:1], 0.0))
                op(V.tensor_tensor_scan(shifted[:, 1:NB], m.ones[:, 0:NB - 1], total[:, 0:NB - 1], 0.0, ALU.mult, ALU.add))
                dve.sem_inc(ready, 1)
                dve.wait_ge(summed, 1)
                op(V.tensor_copy(base[:, 0, 0, :], ps_look[:, 0, 0:NB]))
                op(V.tensor_copy(bounds[:, 0:NB], ps_look[:, 1, 0:NB]))
                op(V.memset(bounds[:, NB:NB + 1], float(ET * P)))
                first, last, some, n, start, g, dg, lastk = (bk[:, j, :] for j in range(8))
                op(V.tensor_copy(bk_i[:, 0, :], bounds[:, :]))
                op(V.tensor_single_scalar(bk_i[:, 1, :], bk_i[:, 0, :], 7, ALU.arith_shift_right))
                op(V.tensor_copy(first, bk_i[:, 1, :]))
                op(V.tensor_scalar(lastk, bounds[:, :], -1.0, None, ALU.add))
                op(V.tensor_copy(bk_i[:, 0, :], lastk))
                op(V.tensor_single_scalar(bk_i[:, 1, :], bk_i[:, 0, :], 7, ALU.arith_shift_right))
                op(V.tensor_copy(last, bk_i[:, 1, :]))
                op(V.memset(n, 0.0))
                op(V.tensor_tensor(some[:, 0:NB], bounds[:, 1:NB + 1], bounds[:, 0:NB], ALU.is_gt))
                op(V.tensor_tensor(n[:, 0:NB], last[:, 1:NB + 1], first[:, 0:NB], ALU.subtract))
                op(V.scalar_tensor_tensor(n[:, 0:NB], n[:, 0:NB], 1.0, some[:, 0:NB], ALU.add, ALU.mult))
                op(V.memset(start, 0.0))
                op(V.tensor_tensor_scan(start[:, 1:NB + 1], m.ones[:, 0:NB], n[:, 0:NB], 0.0, ALU.mult, ALU.add))
                op(V.tensor_tensor(g, first, start, ALU.subtract))
                op(V.tensor_copy(dg, g))
                op(V.tensor_tensor(dg[:, 1:NB], g[:, 1:NB], g[:, 0:NB - 1], ALU.subtract))
                for j in range(SCOL):
                    s = m.step_no[:, j:j + 1]
                    op(V.tensor_scalar(bk[:, 8, 0:NB], start[:, 1:NB + 1], s, 0.0, ALU.is_le, ALU.add, accum_out=stp[:, 0, j:j + 1]))
                    op(V.scalar_tensor_tensor(bk[:, 9, 0:NB], start[:, 0:NB], s, dg[:, 0:NB], ALU.is_le, ALU.mult,
                                              accum_out=stp[:, 1, j:j + 1]))
                op(V.tensor_tensor(stp[:, 1, :], stp[:, 1, :], m.step_no[:, :], ALU.add))
                op(V.tensor_scalar(stp[:, 1, :], stp[:, 1, :], float(ET - 1), 0.0, ALU.min, ALU.max))
                op(V.tensor_copy(tile_i[:, :], stp[:, 1, :]))
                op(V.tensor_scalar(stp[:, 2, :], stp[:, 0, :], float(P), None, ALU.mult))
                op(V.tensor_scalar(stp[:, 3, :], stp[:, 0, :], float(NB - 1), float(DIM), ALU.min, ALU.mult))
                op(V.tensor_scalar(stp[:, 4, :], stp[:, 0, :], float(NB - 1), float(AW), ALU.min, ALU.mult))
                dve.sem_inc(ready, 1)
                dve.wait_ge(summed, 2)
                op(V.tensor_copy(offT[:, 0, :], ps_t[0:SCOL, 0, 0:P]))
                op(V.tensor_copy(offT[:, 1, :], ps_t[0:SCOL, 1, 0:P]))
                dve.sem_inc(ready, 1)

            @block.tensor
            def _(pe):
                pe.wait_ge(ready, 1)
                nc.tensor.matmul(ps_look[:, 0, 0:NB], m.ones[:, :], shifted[:, :], start=True, stop=False)
                nc.tensor.matmul(ps_look[:, 0, 0:NB], m.before_col[:, :], total[:, :], start=False, stop=True)
                nc.tensor.matmul(ps_look[:, 1, 0:NB], m.ones[:, :], shifted[:, :], start=True, stop=True).then_inc(summed, 1)
                pe.wait_ge(ready, 2)
                nc.tensor.transpose(ps_t[0:SCOL, 0, 0:P], stp[:, 3, :], m.ident[:, :])
                nc.tensor.transpose(ps_t[0:SCOL, 1, 0:P], stp[:, 4, :], m.ident[:, :]).then_inc(summed, 1)

            @block.sync
            def _(sp):
                sp.wait_ge(ready, 3)
                sp.dma_start(d_off.rearrange("n (j s) -> j n s", s=P), offT[:, :, :]).then_inc(stored, 16)
                sp.wait_ge(stored, 80)

        bc_in = [sem("bc_in0"), sem("bc_in1")]
        hots2, upd, tabs, looked, placed, bc_used = (sem(n) for n in ("hots2", "upd", "tabs", "looked", "placed", "bc_used"))
        dl3 = sem("dve3")
        scat = [ctx.gather_sem(m, f"scat{h}") for h in range(2)]
        with nc.Block() as block:
            @block.sync
            def _(sp):
                sp.sem_inc(bc_used, 2)
                with sp.Fori(0, NGRP // 2) as i:
                    for h in range(2):
                        g = i * 2 + h
                        sp.wait_ge(bc_used, g + 1)
                        sp.dma_start(key_bc[:, h, :], m.d_key_flat[:, bass.ds(g * (G * P), G * P)].to_broadcast([P, G * P])).then_inc(bc_in[h], 16)
                        sp.dma_start(lo_bc[:, h, :], m.d_lo_flat[:, bass.ds(g * (G * P), G * P)].to_broadcast([P, G * P])).then_inc(bc_in[h], 16)

            @block.vector
            def _(dve):
                V = nc.vector
                per = 2 * (G + 6)
                ROUNDS2 = NGRP // 2

                def compares(i, h, ln):
                    g = i * 2 + h
                    at = bass.ds(g * G, G)
                    dve.wait_ge(bc_in[h], (i + 1) * 32)
                    V.tensor_tensor(hot_hi[:, h], m.ramp16[:, 0:NB].unsqueeze(1).to_broadcast([P, G, NB]),
                                    bcast(cols[:, 2, at], NB), ALU.is_equal)
                    V.tensor_tensor(hot_lo[:, h], m.ramp16[:, :].unsqueeze(1).to_broadcast([P, G, P]),
                                    bcast(cols[:, 3, at], P), ALU.is_equal).then_inc(hots2, 1)
                    V.tensor_scalar(hot_loT[:, h], lo_bc[:, h, :].rearrange("p (k e) -> p k e", k=G), m.lane[:, 0:1], None, ALU.is_equal)
                    for k in range(G):
                        if k >= 2:
                            ln.wait(1)
                        ln.mark(V.scalar_tensor_tensor(eq[:, k % 2, :], key_bc[:, h, k * P:(k + 1) * P],
                                                       cols[:, 0, bass.ds(g * G + k, 1)], m.before_row[:, :],
                                                       ALU.is_equal, ALU.mult, accum_out=dup[:, h, k:k + 1]))
                    ln.wait()
                    dve.sem_inc(bc_used, 1)

                def round_(i, last):
                    ln = Links(dve, dl3, G + i * per)
                    for h in range(2):
                        g = i * 2 + h
                        at = bass.ds(g * G, G)
                        dve.wait_ge(upd, g + 1)
                        ln.mark(V.tensor_tensor(base[:, h, 1:G + 1, :], ps_up[:, h, 0:G * NB].rearrange("p (k b) -> p k b", k=G),
                                                base[:, h, 0:1, :].to_broadcast([P, G, NB]), ALU.add))
                        ln.wait()
                        dve.sem_inc(tabs, 1)
                        ln.mark(V.tensor_copy(base[:, 1 - h, 0, :], base[:, h, G, :]))
                        if h == 0:
                            compares(i, 1, ln)
                        elif not last:
                            compares(i + 1, 0, ln)
                        dve.wait_ge(looked, g + 1)
                        ln.mark(V.tensor_tensor(picked[:, h], ps_look[:, h, 0:G * NB].rearrange("p (k b) -> p k b", k=G), hot_hi[:, h], ALU.mult))
                        ln.wait()
                        ln.mark(V.tensor_reduce(rank[:, h], picked[:, h], axis=AX.X, op=ALU.add))
                        ln.wait()
                        dve.wait_ge(scat[h], 16 + i * (16 * G))
                        ln.mark(V.tensor_tensor(rank_i[:, h], rank[:, h], dup[:, h], ALU.add))
                        ln.mark(V.tensor_copy(rec_st[:, h], recs[:, at, :]))
                        ln.wait()
                        dve.sem_inc(placed, 1)
                    assert last or ln.n == per

                compares(0, 0, Links(dve, dl3))
                with dve.Fori(0, ROUNDS2 - 1) as i:
                    round_(i, False)
                round_(ROUNDS2 - 1, True)

            @block.tensor
            def _(pe):
                with pe.Fori(0, NGRP // 2) as i:
                    for h in range(2):
                        g = i * 2 + h
                        pe.wait_ge(hots2, g + 1)
                        for k in range(G):
                            for j in range(k + 1):
                                last = nc.tensor.matmul(ps_up[:, h, k * NB:(k + 1) * NB], hot_lo[:, h, j], hot_hi[:, h, j],
                                                        start=(j == 0), stop=(j == k))
                        last.then_inc(upd, 1)
                        pe.wait_ge(tabs, g + 1)
                        for k in range(G):
                            last = nc.tensor.matmul(ps_look[:, h, k * NB:(k + 1) * NB], hot_loT[:, h, k], base[:, h, k, :],
                                                    start=True, stop=True)
                        last.then_inc(looked, 1)

            @block.gpsimd
            def _(pool):
                for h in range(2):
                    pool.dma_start(credit[:, h, :], d_off[0:1, 0:8]).then_inc(scat[h], 16)
                with pool.Fori(0, NGRP // 2) as i:
                    for h in range(2):
                        g = i * 2 + h
                        pool.wait_ge(placed, g + 1)
                        pool.sem_inc(taken, 1)
                        for k in range(G):
                            pool.indirect_dma_start(out=rec[:, :], out_offset=bass.IndirectOffsetOnAxis(ap=rank_i[:, h, k:k + 1], axis=0),
                                                    in_=rec_st[:, h, k, :], in_offset=None).then_inc(scat[h], 16)
                for h in range(2):
                    pool.wait_ge(scat[h], 16 + (NGRP // 2) * (16 * G))

        fetched, spread, tt, te = ([ctx.gather_sem(m, f"fetched{h}") for h in range(2)], sem("spread"), sem("tt"), sem("te"))
        st2 = [sem("kept0"), sem("kept1")]
        dl4 = sem("dve4")
        with nc.Block() as block:
            rec_tiles = rec.rearrange("(t e) w -> t (e w)", e=P)

            @block.gpsimd
            def _(pool):
                for j in range(SCOL):
                    if j >= 2:
                        pool.wait_ge(spread, j - 1)
                    pool.indirect_dma_start(out=got[:, j % 2].rearrange("p e w -> p (e w)"), out_offset=None, in_=rec_tiles,
                                            in_offset=bass.IndirectOffsetOnAxis(ap=tile_i[:, j:j + 1], axis=0)).then_inc(fetched[j % 2], 16)

            @block.vector
            def _(dve):
                V = nc.vector
                ln = Links(dve, dl4)
                for j in range(SCOL):
                    r = srow[:, j % 2]
                    dve.wait_ge(fetched[j % 2], (j // 2 + 1) * 16)
                    if j >= 2:
                        dve.wait_ge(st2[j % 2], (j // 2) * 32)
                        dve.wait_ge(te, (j - 1) * 3)
                    ln.mark(V.tensor_copy(r[:, 0, :], got[:, j % 2, :, 0]))
                    ln.mark(V.tensor_copy(r[:, 2, :], got[:, j % 2, :, 1]))
                    ln.mark(V.tensor_copy(r[:, 3, :], got[:, j % 2, :, 2].bitcast(F32)))
                    ln.wait()
                    ln.mark(V.tensor_scalar(r[:, 1, :], r[:, 0, :], stp[:, 2, j:j + 1], None, ALU.subtract))
                    ln.wait()
                    dve.sem_inc(spread, 1)
                    for n, dst in enumerate((scol[:, :, 1].bitcast(F32), scol[:, :, 0], scol[:, :, 2].bitcast(F32))):
                        u = j * 3 + n
                        dve.wait_ge(tt, u + 1)
                        V.tensor_copy(dst[:, j * P:(j + 1) * P], ps_t[:, u % 2, 0:P]).then_inc(te, 1)

            @block.tensor
            def _(pe):
                for j in range(SCOL):
                    pe.wait_ge(spread, j + 1)
                    for n in range(3):
                        u = j * 3 + n
                        if u >= 2:
                            pe.wait_ge(te, u - 1)
                        nc.tensor.transpose(ps_t[:, u % 2, 0:P], srow[:, j % 2, 1 + n, :], m.ident[:, :]).then_inc(tt, 1)

            @block.sync
            def _(sp):
                for j in range(SCOL):
                    sp.wait_ge(spread, j + 1)
                    sp.dma_start(d_skey[0:1, 1 + j * P * P:1 + (j + 1) * P * P].rearrange("o (s e) -> (o s) e", e=P), srow[:, j % 2, 0, :]).then_inc(st2[j % 2], 16)
                    sp.dma_start(d_lk[j * P:(j + 1) * P, :], srow[:, j % 2, 1, :]).then_inc(st2[j % 2], 16)
                sp.wait_ge(te, 3 * SCOL)
                sp.dma_start(d_cols, scol[:, :, :]).then_inc(stored, 16)
                sp.wait_ge(stored, 96)
                for h in range(2):
                    sp.wait_ge(st2[h], 32 * ((SCOL + 1 - h) // 2))


RB = 7
ROUNDS = NB // RB
assert ROUNDS * RB == NB


def arcosh(nc, ops, ask_sqrt, ask_ln, t, w):
    z, a, r, ln1, q, q2, s = w[1:8]
    ops.ts(a, t, 1.0, None, ALU.subtract)
    ops.ts(r, t, 1.0, None, ALU.add)
    ops.tt(r, r, a, ALU.mult)
    ask_sqrt(r, r)
    ops.tt(z, a, r, ALU.add)
    ask_ln(ln1, z)
    ops.ts(q, z, 2.0, None, ALU.add)
    ops.recip(q, q)
    ops.tt(q, q, z, ALU.mult)
    ops.tt(q2, q, q, ALU.mult)
    ops.ts(s, q2, 2.0 / 7, 2.0 / 5, ALU.mult, ALU.add)
    ops.tt(s, s, q2, ALU.mult)
    ops.ts(s, s, 2.0 / 3, None, ALU.add)
    ops.tt(s, s, q2, ALU.mult)
    ops.ts(s, s, 2.0, None, ALU.add)
    ops.tt(s, s, q, ALU.mult)
    ops.tt(s, s, ln1, ALU.subtract)
    ops.ts(a, z, 0.25, None, ALU.is_lt)
    ops.tt(s, s, a, ALU.mult)
    ops.tt(w[0], s, ln1, ALU.add)


class Small:

    def __init__(self, eng, ns, ln, mhalf=None):
        self.eng, self.ns, self.ln, self.mhalf = eng, ns, ln, mhalf

    def do(self, ins):
        self.ln.mark(ins)
        self.ln.wait()

    def ts(self, out, a, s1, s2, op0, op1=None):
        if op1 is None:
            self.do(self.ns.tensor_scalar(out, a, s1, None, op0))
        else:
            self.do(self.ns.tensor_scalar(out, a, s1, s2, op0, op1))

    def tt(self, out, a, b, op):
        self.do(self.ns.tensor_tensor(out, a, b, op))

    def recip(self, out, a):
        self.do(self.ns.reciprocal(out, a))


def node_stage(nc, m, tag, kind):
    with Stage(nc, tag) as ctx:
        sb = lambda n, s, d=F32: ctx.enter_context(nc.sbuf_tensor(f"{tag}_{n}", s, d))
        pb = lambda n, s: ctx.enter_context(nc.psum_tensor(f"{tag}_{n}", s, F32))
        sem = ctx.sem
        NW = 3 if kind == "qkv" else 2
        wts = sb("wts", [P, NW, 2, DIM])
        bias = sb("bias", [P, NW, DIM])
        xt = sb("xt", [P, RB, DIM])
        xc = sb("xc", [P, RB, DIM])
        tmp = sb("tmp", [P, RB, DIM])
        hT = sb("hT", [P, RB, 2, P])
        st = sb("st", [P, 24, RB])
        rowst = sb("rowst", [P, RB, 512 if kind != "out" else DIM])
        pt = pb("pt", [P, 2, 512])
        pj = pb("pj", [P, 4, 512])
        w_in, x_in, x_used, dv, ask, answer, turned, evac, hready, hT_ready, proj, proj_used, rows_ready, rows_out = (
            sem(n) for n in ("w_in", "x_in", "x_used", "dve", "ask", "answer", "turned", "evac", "hready", "hT_ready",
                             "proj", "proj_used", "rows_ready", "rows_out"))
        s_x = (m.d_x1 if kind == "out" else m.in_x).rearrange("(b p) d -> p b d", p=P)
        if kind == "qkv":
            mats, vecs = (m.in_wq, m.in_wv, m.in_wk), (m.in_bq, m.in_bv, m.in_bk)
        elif kind == "mid":
            mats, vecs = (m.in_aw1[0:DIM, :], m.in_aw1[DIM:2 * DIM, :]), (m.in_ab1, None)
        else:
            mats, vecs = (m.in_mw1, m.in_mw2), (m.in_mb1, m.in_mb2)
        passes = 2 if kind == "out" else 1

        PER_DVE = {"qkv": 10, "mid": 47, "out": 80}[kind]
        ASKS = {"qkv": 1, "mid": 4, "out": 7}[kind]
        

        with nc.Block() as block:
            @block.sync
            def _(sp):
                n_w = 0
                for n in range(NW):
                    sp.dma_start(wts[:, n], mats[n].rearrange("(c p) n -> p c n", p=P)).then_inc(w_in, 16)
                    n_w += 1
                    if vecs[n] is not None:
                        sp.dma_start(bias[:, n, :], vecs[n].unsqueeze(0).to_broadcast([P, DIM])).then_inc(w_in, 16)
                        n_w += 1
                sp.wait_ge(w_in, 16 * n_w)
                with sp.Fori(0, ROUNDS) as i:
                    sp.wait_ge(x_used, i + 1)
                    sp.dma_start(xt[:, :, :], s_x[:, bass.ds(i * RB, RB), :]).then_inc(x_in, 16)
                    sp.wait_ge(rows_ready, i + 1)
                    at = bass.ds(i * RB, RB)
                    if kind == "qkv":
                        sp.dma_start(m.d_q.rearrange("(b p) d -> p b d", p=P)[:, at, :], rowst[:, :, 0:DIM]).then_inc(rows_out, 16)
                        sp.dma_start(m.d_v.rearrange("(b p) d -> p b d", p=P)[:, at, :], rowst[:, :, DIM:2 * DIM]).then_inc(rows_out, 16)
                    elif kind == "mid":
                        sp.dma_start(m.d_xr.rearrange("(b p) d -> p b d", p=P)[:, at, :], rowst[:, :, :]).then_inc(rows_out, 16)
                        sp.dma_start(m.d_x1.rearrange("(b p) d -> p b d", p=P)[:, at, :], xt[:, :, :]).then_inc(rows_out, 16)
                    else:
                        sp.dma_start(m.d_out.rearrange("(b p) d -> p b d", p=P)[:, at, :], rowst[:, :, :]).then_inc(rows_out, 16)
                        sp.dma_start(m.d_sink[0:1, :], rowst[0:1, 0, 0:16]).then_inc(rows_out, 16)
                sp.wait_ge(rows_out, 32 + 32 * ROUNDS)

            @block.vector
            def _(dve):
                V = nc.vector
                dve.sem_inc(x_used, 1)
                dve.wait_ge(w_in, 16 * (2 * NW - (1 if kind == "mid" else 0)))
                with dve.Fori(0, ROUNDS) as i:
                    ln = Links(dve, dv, i * PER_DVE)
                    sm = Small(dve, V, ln)
                    S_ = lambda j: st[:, j, :]
                    asked = [0]
                    nb = lambda ap: bcast(ap, DIM)
                    nb1 = lambda ap: bcast(ap, DIM - 1)

                    def ask_act():
                        dve.sem_inc(ask, 1)
                        asked[0] += 1
                        dve.wait_ge(answer, i * ASKS + asked[0])

                    tp = [0]

                    def turn_and_project(biases, outs):
                        dve.sem_inc(hready, 1)
                        for g in range(RB):
                            dve.wait_ge(turned, i * (RB * passes) + tp[0] * RB + g + 1)
                            ins = V.tensor_copy(hT[:, g].rearrange("p c n -> p (c n)"), pt[:, g % 2, 0:2 * P])
                            ins.then_inc(evac, 1)
                        for b in range(RB):
                            dve.wait_ge(proj, i * (RB * passes) + tp[0] * RB + b + 1)
                            for n, (bi, o) in enumerate(zip(biases, outs)):
                                bank = pj[:, (b % 2) * 2 + n // 2, (n % 2) * DIM:(n % 2 + 1) * DIM]
                                if bi is None:
                                    last = V.tensor_copy(o(b), bank)
                                else:
                                    last = V.tensor_tensor(o(b), bank, bias[:, bi, :], ALU.add)
                            last.then_inc(proj_used, 1)
                        tp[0] += 1

                    dve.wait_ge(x_in, (i + 1) * 16)
                    if kind == "mid":
                        acc = m.acc_l0[:, bass.ds(i * (RB * AW), RB * AW)].rearrange("p (b a) -> p b a", a=AW)
                        z, zr = tmp[:, :, 0:HEADS], tmp[:, :, HEADS:2 * HEADS]
                        sm.ts(z, acc[:, :, DIM:AW], 1e-16, None, ALU.max)
                        sm.recip(zr, z)
                        for b in range(RB):
                            ab = m.acc_l0[:, bass.ds(i * (RB * AW) + b * AW, DIM)].rearrange("p (h d) -> p h d", h=HEADS)
                            ln.mark(V.tensor_tensor(xc[:, b, :].rearrange("p (h d) -> p h d", h=HEADS), ab, bcast(zr[:, b, :], DH), ALU.mult))
                        ln.wait()
                        sm.tt(xt[:, :, :], xt[:, :, :], xc[:, :, :], ALU.add)
                    if kind in ("qkv", "mid"):
                        ln.mark(V.tensor_reduce(S_(0), xt[:, :, :], axis=AX.X, op=ALU.add)); ln.wait()
                        sm.ts(S_(1), S_(0), 1.0 / DIM, None, ALU.mult)
                        sm.tt(xc[:, :, :], xt[:, :, :], nb(S_(1)), ALU.subtract)
                        if kind == "qkv":
                            dve.sem_inc(x_used, 1)
                        sm.tt(tmp[:, :, :], xc[:, :, :], xc[:, :, :], ALU.mult)
                        ln.mark(V.tensor_reduce(S_(2), tmp[:, :, :], axis=AX.X, op=ALU.add)); ln.wait()
                        sm.ts(S_(3), S_(2), 1.0 / DIM, 1e-5, ALU.mult, ALU.add)
                        ask_act()
                        sm.recip(S_(5), S_(4))
                        sm.tt(xc[:, :, :], xc[:, :, :], nb(S_(5)), ALU.mult)
                        if kind == "qkv":
                            sm.ts(xc[:, :, :], xc[:, :, :], 0.0, None, ALU.max)
                            turn = [(0, lambda b: rowst[:, b, 0:DIM]), (1, lambda b: rowst[:, b, DIM:2 * DIM]),
                                    (2, lambda b: m.tab_a[:, bass.ds(i * (RB * DIM) + b * DIM, DIM)])]
                            dve.wait_ge(rows_out, i * 32 + 32)
                            turn_and_project([t[0] for t in turn], [t[1] for t in turn])
                            ln.mark(V.memset(S_(23), 0.0)); ln.wait()
                            dve.sem_inc(rows_ready, 1)
                    if kind == "mid":
                        dve.wait_ge(rows_out, i * 32 + 32)
                        sm.ts(rowst[:, :, 0:DIM], xc[:, :, :], 0.0, None, ALU.max)
                        h = rowst[:, :, 0:DIM]
                        ln.mark(V.tensor_copy(m.tab_a[:, bass.ds(i * (RB * DIM), RB * DIM)].rearrange("p (b d) -> p b d", d=DIM), h))
                        sm.tt(tmp[:, :, 1:DIM], h[:, :, 1:DIM], h[:, :, 1:DIM], ALU.mult)
                        ln.mark(V.tensor_reduce(S_(6), tmp[:, :, 1:DIM], axis=AX.X, op=ALU.add)); ln.wait()
                        sm.ts(S_(7), h[:, :, 0], 1.0 + EPS, None, ALU.max)
                        arcosh(nc, sm, lambda o, a: ask_act(), lambda o, a: ask_act(), S_(7), [S_(j) for j in range(8, 16)])
                        ask_act()
                        sm.ts(S_(17), S_(16), 1e-15, None, ALU.max)
                        sm.recip(S_(18), S_(17))
                        sm.tt(S_(19), S_(18), S_(8), ALU.mult)
                        sm.tt(xc[:, :, :], h, nb(S_(19)), ALU.mult)
                        ln.mark(V.memset(xc[:, :, 0], 0.0)); ln.wait()
                        turn_and_project([0, None], [lambda b: m.tab_c[:, bass.ds(i * (RB * DIM) + b * DIM, DIM)],
                                                     lambda b: rowst[:, b, DIM:2 * DIM]])
                        ln.mark(V.memset(S_(23), 0.0)); ln.wait()
                        dve.sem_inc(rows_ready, 1)
                        dve.wait_ge(rows_out, (i + 1) * 32 + 32)
                        dve.sem_inc(x_used, 1)
                    if kind == "out":
                        h = m.tab_a[:, bass.ds(i * (RB * DIM), RB * DIM)].rearrange("p (b d) -> p b d", d=DIM)
                        ac = m.acc_l1[:, bass.ds(i * (RB * DIM), RB * DIM)].rearrange("p (b d) -> p b d", d=DIM)
                        hv, h0 = h[:, :, 1:DIM], h[:, :, 0]
                        t1 = tmp[:, :, 1:DIM]
                        s0, inv0, hh = S_(0), S_(1), S_(2)
                        sm.ts(s0, h0, EPS, None, ALU.max)
                        sm.recip(inv0, s0)
                        sm.ts(xc[:, :, :], ac, 0.01, None, ALU.mult)
                        sm.tt(t1, hv, xc[:, :, 1:DIM], ALU.mult)
                        ln.mark(V.tensor_reduce(S_(3), t1, axis=AX.X, op=ALU.add)); ln.wait()
                        sm.tt(xc[:, :, 0], S_(3), inv0, ALU.mult)
                        dve.wait_ge(rows_out, i * 32 + 32)
                        turn_and_project([0], [lambda b: rowst[:, b, :]])
                        ln.mark(V.memset(S_(23), 0.0)); ln.wait()
                        ask_act()
                        turn_and_project([1], [lambda b: rowst[:, b, :]])
                        sm.tt(t1, hv, hv, ALU.mult)
                        ln.mark(V.tensor_reduce(hh, t1, axis=AX.X, op=ALU.add)); ln.wait()
                        sm.tt(S_(4), h0, h0, ALU.mult)
                        sm.tt(hh, hh, S_(4), ALU.subtract)
                        sm.ts(S_(5), hh, 1.0, -EPS, ALU.add, ALU.min)
                        sm.ts(S_(5), S_(5), 1.0, None, ALU.subtract)
                        sm.tt(xc[:, :, :], h, nb(S_(5)), ALU.mult)
                        sm.tt(xc[:, :, :], xc[:, :, :], h, ALU.add)
                        sm.tt(t1, xc[:, :, 1:DIM], xc[:, :, 1:DIM], ALU.mult)
                        ln.mark(V.tensor_reduce(S_(3), t1, axis=AX.X, op=ALU.add)); ln.wait()
                        sm.tt(S_(4), xc[:, :, 0], xc[:, :, 0], ALU.mult)
                        sm.tt(S_(6), S_(3), S_(4), ALU.subtract)
                        sm.ts(S_(6), S_(6), EPS, None, ALU.max)
                        sm.ts(S_(7), hh, -1.0, 1.0 + EPS, ALU.mult, ALU.max)
                        arcosh(nc, sm, lambda o, a: ask_act(), lambda o, a: ask_act(), S_(7), [S_(j) for j in range(8, 16)])
                        sm.ts(S_(8), S_(8), math.sqrt(FAR), None, ALU.min)
                        ask_act()
                        sm.ts(S_(16), S_(16), 1e-15, None, ALU.max)
                        sm.recip(S_(16), S_(16))
                        sm.tt(S_(16), S_(16), S_(8), ALU.mult)
                        sm.tt(xc[:, :, :], xc[:, :, :], nb(S_(16)), ALU.mult)
                        sm.tt(xc[:, :, :], xc[:, :, :], rowst[:, :, :], ALU.add)
                        sm.tt(t1, hv, xc[:, :, 1:DIM], ALU.mult)
                        ln.mark(V.tensor_reduce(S_(3), t1, axis=AX.X, op=ALU.add)); ln.wait()
                        sm.tt(S_(3), S_(3), inv0, ALU.mult)
                        sm.tt(S_(3), S_(3), S_(3), ALU.mult)
                        sm.tt(t1, xc[:, :, 1:DIM], xc[:, :, 1:DIM], ALU.mult)
                        ln.mark(V.tensor_reduce(S_(4), t1, axis=AX.X, op=ALU.add)); ln.wait()
                        sm.tt(S_(6), S_(4), S_(3), ALU.subtract)
                        sm.ts(S_(6), S_(6), EPS, None, ALU.max)
                        ask_act()
                        th, ep, en, po, small, t2 = S_(17), S_(18), S_(19), S_(20), S_(21), S_(22)
                        sm.ts(th, S_(16), 1e6, 1e-15, ALU.min, ALU.max)
                        ask_act()
                        sm.ts(t2, th, 1.0, None, ALU.min)
                        sm.tt(t2, t2, t2, ALU.mult)
                        sm.ts(po, t2, 1.0 / 362880, 1.0 / 5040, ALU.mult, ALU.add)
                        sm.tt(po, po, t2, ALU.mult)
                        sm.ts(po, po, 1.0 / 120, None, ALU.add)
                        sm.tt(po, po, t2, ALU.mult)
                        sm.ts(po, po, 1.0 / 6, None, ALU.add)
                        sm.tt(po, po, t2, ALU.mult)
                        sm.ts(po, po, 1.0, None, ALU.add)
                        sm.recip(t2, th)
                        sm.tt(small, ep, en, ALU.subtract)
                        sm.tt(t2, t2, small, ALU.mult)
                        sm.ts(small, th, 1.0, None, ALU.is_lt)
                        sm.tt(po, po, small, ALU.mult)
                        sm.ts(small, th, 1.0, None, ALU.is_ge)
                        sm.tt(t2, t2, small, ALU.mult)
                        sm.tt(t2, t2, po, ALU.add)
                        sm.tt(ep, ep, en, ALU.add)
                        sm.tt(xc[:, :, :], xc[:, :, :], nb(t2), ALU.mult)
                        sm.tt(tmp[:, :, :], h, nb(ep), ALU.mult)
                        sm.tt(rowst[:, :, :], xc[:, :, :], tmp[:, :, :], ALU.add)
                        sm.tt(t1, rowst[:, :, 1:DIM], rowst[:, :, 1:DIM], ALU.mult)
                        ln.mark(V.tensor_reduce(S_(6), t1, axis=AX.X, op=ALU.add)); ln.wait()
                        sm.ts(S_(6), S_(6), 1.0, None, ALU.add)
                        ask_act()
                        sm.ts(rowst[:, :, 0], S_(16), 1.0, None, ALU.mult)
                        sm.tt(rowst[:, :, :], rowst[:, :, :], xt[:, :, :], ALU.add)
                        dve.sem_inc(x_used, 1)
                        dve.sem_inc(rows_ready, 1)
                    assert ln.n == PER_DVE, ln.n
                    assert asked[0] == ASKS, asked[0]

            @block.scalar
            def _(act):
                A = nc.scalar
                act.dma_start(m.d_sink[1:2, :], m.ones[0:1, 0:16]).then_inc(rows_out, 16)
                act.dma_start(m.d_sink[2:3, :], m.ones[0:1, 0:16]).then_inc(rows_out, 16)
                S_ = lambda j: st[:, j, :]
                one = m.ones[:, 0:1]
                jobs = {
                    "qkv": [lambda: A.activation(S_(4), S_(3), ACT.Sqrt)],
                    "mid": [lambda: A.activation(S_(4), S_(3), ACT.Sqrt),
                            lambda: A.activation(S_(11), S_(11), ACT.Sqrt),
                            lambda: A.activation(S_(12), S_(9), ACT.Ln, bias=one),
                            lambda: A.activation(S_(16), S_(6), ACT.Sqrt)],
                    "out": [lambda: A.activation(xc[:, :, :], rowst[:, :, :], ACT.Silu),
                            lambda: A.activation(S_(11), S_(11), ACT.Sqrt),
                            lambda: A.activation(S_(12), S_(9), ACT.Ln, bias=one),
                            lambda: A.activation(S_(16), S_(6), ACT.Sqrt),
                            lambda: A.activation(S_(16), S_(6), ACT.Sqrt),
                            lambda: (A.activation(S_(18), S_(17), ACT.Exp, bias=m.neg_ln2[:, 0:1]),
                                     A.activation(S_(19), S_(17), ACT.Exp, bias=m.neg_ln2[:, 0:1], scale=-1.0))[1],
                            lambda: A.activation(S_(16), S_(6), ACT.Sqrt)],
                }[kind]
                ASK = len(jobs)
                assert ASK == ASKS, ASK
                with act.Fori(0, ROUNDS) as i:
                    for j, job in enumerate(jobs):
                        act.wait_ge(ask, i * ASK + j + 1)
                        job().then_inc(answer, 1)

            @block.tensor
            def _(pe):
                T = nc.tensor
                pe.wait_ge(w_in, 16 * (2 * NW - (1 if kind == "mid" else 0)))
                T.transpose(pt[:, 0, 0:P], m.ident[:, :], m.ident[:, :])
                pe.sem_inc(evac, 2)
                pe.sem_inc(proj_used, 2)
                with pe.Fori(0, ROUNDS) as i:
                    for tp in range(passes):
                        base = i * (RB * passes) + tp * RB
                        pe.wait_ge(hready, i * passes + tp + 1)
                        for g in range(RB):
                            pe.wait_ge(evac, base + g + 1)
                            for c in range(2):
                                last = T.transpose(pt[:, g % 2, c * P:(c + 1) * P], xc[:, g, c * P:(c + 1) * P], m.ident[:, :])
                            last.then_inc(turned, 1)
                        for b in range(RB):
                            pe.wait_ge(evac, base + b + 3)
                            pe.wait_ge(proj_used, base + b + 1)
                            for n in ((0, 1, 2) if kind == "qkv" else (0, 1) if kind == "mid" else (tp,)):
                                slot = n if kind != "out" else 0
                                bank = pj[:, (b % 2) * 2 + slot // 2, (slot % 2) * DIM:(slot % 2 + 1) * DIM]
                                for c in range(2):
                                    last = T.matmul(bank, hT[:, b, c, :], wts[:, n, c, :], start=(c == 0), stop=(c == 1))
                            last.then_inc(proj, 1)


GROUPS = STEPS // G
DEPTH = 4
assert GROUPS % DEPTH == 0


def fetch_steps(sp, edges, rounds, used, bc_in, bc, col_in, col, n=G):
    depth = len(col_in)
    with sp.Fori(0, rounds) as i:
        for h in range(depth):
            g = i * depth + h
            sp.wait_ge(used, g + 1)
            sp.dma_start(col[:, h], edges.cols[:, bass.ds(g * n, n), :]).then_inc(col_in[h], 16)
            if bc is not None:
                sp.dma_start(bc[:, h, :], edges.lk[:, bass.ds(g * (n * P), n * P)].to_broadcast([P, n * P])).then_inc(bc_in[h], 16)


def gather(m, pool, i, h, col_in, col, ring, got, table, n=G):
    pool.wait_ge(col_in[h], (i + 1) * 16)
    pool.sem_inc(m.nothing, 1)
    for k in range(n):
        pool.indirect_dma_start(out=ring[:, h, k, :], out_offset=None, in_=table,
                                in_offset=bass.IndirectOffsetOnAxis(ap=col[:, h, k, 0:1], axis=0)).then_inc(got[h], 16)


class Starts:

    def __init__(self, eng, tag, off, top, most=G):
        self.eng, self.off, self.top = eng, off, top
        self.regs = [eng.alloc_register(name=f"{tag}_start{j}") for j in range(most)]

    def fetch(self, at, n):
        self.eng.load(self.regs[0:n], self.off[0:1, bass.ds(at, n)])

    def values(self, first, n):
        return [self.eng.snap(r, min_val=0, max_val=self.top) for r in self.regs[first:first + n]]

    def load(self, at, n):
        self.fetch(at, n)
        return self.values(0, n)


def scores(nc, m, edges):
    with Stage(nc, "sc") as ctx:
        sb = lambda n, s, d=F32: ctx.enter_context(nc.sbuf_tensor(f"sc_{n}", s, d))
        pb = lambda n, s: ctx.enter_context(nc.psum_tensor(f"sc_{n}", s, F32))
        sem = ctx.sem
        ring = sb("ring", [P, DEPTH, G, DIM])
        col = sb("col", [P, DEPTH, G, 3], I32)
        hotT = sb("hotT", [P, DEPTH, G * P])
        prod = m.acc_l0[:, 0:G * DIM].rearrange("p (g d) -> p g d", d=DIM)
        off = sb("off", [1, STEPS], I16)
        kx = pb("kx", [P, 8, 512])
        bc_in, col_in = ([sem(f"{n}{h}") for h in range(DEPTH)] for n in ("bc_in", "col_in"))
        got = [ctx.gather_sem(m, f"got{h}") for h in range(DEPTH)]
        used, hot, kx_in, kx_used, dv, off_in = (sem(n) for n in ("used", "hot", "kx_in", "kx_used", "dve", "off_in"))
        ROUND = GROUPS // DEPTH
        with nc.Block() as block:
            @block.sync
            def _(sp):
                sp.dma_start(off[:, :], edges.off[0:1, 0:STEPS]).then_inc(off_in, 16)
                sp.sem_inc(used, DEPTH)
                fetch_steps(sp, edges, ROUND, used, bc_in, hotT, col_in, col)

            @block.gpsimd
            def _(pool):
                with pool.Fori(0, ROUND) as i:
                    for h in range(DEPTH):
                        gather(m, pool, i, h, col_in, col, ring, got, m.d_q)

            @block.tensor
            def _(pe):
                pe.wait_ge(off_in, 16)
                pe.sem_inc(kx_used, 8)
                starts = Starts(pe, "sc", off, (NB - 1) * DIM)
                with pe.Fori(0, ROUND) as i:
                    for h in range(DEPTH):
                        g = i * DEPTH + h
                        at = starts.load(g * G, G)
                        pe.wait_ge(hot, g + 1)
                        for k in range(G):
                            b = (h * 4 + k // 2) % 8
                            if k % 2 == 0:
                                pe.wait_ge(kx_used, g * 4 + k // 2 + 1)
                            last = nc.tensor.matmul(kx[:, b, (k % 2) * DIM:(k % 2 + 1) * DIM], hotT[:, h, k * P:(k + 1) * P],
                                                    m.tab_a[:, bass.ds(at[k], DIM)], start=True, stop=True)
                            if k % 2 == 1:
                                last.then_inc(kx_in, 1)

            @block.vector
            def _(dve):
                V = nc.vector
                with dve.Fori(0, ROUND) as i:
                    ln = Links(dve, dv, i * DEPTH)
                    for h in range(DEPTH):
                        g = i * DEPTH + h
                        dve.wait_ge(bc_in[h], (i + 1) * 16)
                        V.tensor_scalar(hotT[:, h, :], hotT[:, h, :], m.lane[:, 0:1], None, ALU.is_equal).then_inc(hot, 1)
                        dve.wait_ge(got[h], (i + 1) * (16 * G))
                        for k2 in range(G // 2):
                            dve.wait_ge(kx_in, g * 4 + k2 + 1)
                            V.tensor_tensor(prod[:, 2 * k2:2 * k2 + 2, :], ring[:, h, 2 * k2:2 * k2 + 2, :],
                                            kx[:, (h * 4 + k2) % 8, :].rearrange("p (a d) -> p a d", a=2), ALU.mult).then_inc(kx_used, 1)
                        dve.wait_ge(kx_used, g * 4 + 12)
                        dve.sem_inc(used, 1)
                        ln.mark(V.tensor_reduce(m.sc[:, bass.ds(g * (G * HEADS), G * HEADS)],
                                                prod[:, :].rearrange("p k (h d) -> p (k h) d", d=DH), axis=AX.X, op=ALU.add))
                    assert ln.n == DEPTH


def softmax_weights(nc, m):
    with Stage(nc, "sm") as ctx:
        sb = lambda n, s, d=F32: ctx.enter_context(nc.sbuf_tensor(f"sm_{n}", s, d))
        pb = lambda n, s: ctx.enter_context(nc.psum_tensor(f"sm_{n}", s, F32))
        sem = ctx.sem
        sT = m.big[:, 0:CLEN]
        pen = m.big[:, CLEN:2 * CLEN + 1]
        fwd = m.big[:, 2 * CLEN + 1:3 * CLEN + 1]
        keys = m.big[:, 3 * CLEN + 1:4 * CLEN + 3]
        carry = sb("carry", [P, 8])
        crow = sb("crow", [1, 4, P])
        pt = pb("pt", [P, 2, 4, P])
        pr = pb("pr", [P, 2, P])
        key_in, dv, ask, answer, turned, evac, stored = (sem(n) for n in ("key_in", "dve", "ask", "answer", "turned", "evac", "stored"))
        NT = CSTEPS // 4
        with nc.Block() as block:
            @block.sync
            def _(sp):
                sp.wait_ge(dv, 1)
                sp.dma_start(m.d_skey[0:1, 0:1], carry[0:1, 0:1]).then_inc(stored, 16)
                sp.dma_start(m.d_skey[0:1, 1 + STEPS * P:2 + STEPS * P], carry[0:1, 0:1]).then_inc(stored, 16)
                sp.wait_ge(stored, 32)
                for c in range(CHUNKS):
                    sp.dma_start(keys[c * HEADS:(c + 1) * HEADS, :],
                                 m.d_skey[0:1, c * CLEN:(c + 1) * CLEN + 2].to_broadcast([HEADS, CLEN + 2])).then_inc(key_in, 16)
                sp.wait_ge(key_in, 16 * CHUNKS)

            @block.tensor
            def _(pe):
                T = nc.tensor
                pe.wait_ge(evac, 2)
                for n in range(NT):
                    if n >= 2:
                        pe.wait_ge(evac, n + 1)
                    for k in range(4):
                        last = T.transpose(pt[:, n % 2, k, :], pen[:, (4 * n + k) * P:(4 * n + k + 1) * P], m.ident[:, :])
                    last.then_inc(turned, 1)
                for r in range(2):
                    pe.wait_ge(ask, 2 * r + 1)
                    T.transpose(pr[0:1, 0, :], carry[:, 1:2], m.ident[:, :])
                    T.transpose(pr[0:1, 1, :], carry[:, 2:3], m.ident[:, :]).then_inc(answer, 1)
                    pe.wait_ge(ask, 2 * r + 2)
                    T.matmul(pr[:, 0, 0:1], crow[0:1, 3, :], m.ones[0:1, 0:1], start=True, stop=True).then_inc(answer, 1)
                pe.wait_ge(ask, 5)
                for n in range(NT):
                    pe.wait_ge(evac, NT + n + 1)
                    for k in range(4):
                        last = T.transpose(pt[:, n % 2, k, :], sT[:, (4 * n + k) * P:(4 * n + k + 1) * P], m.ident[:, :])
                    last.then_inc(turned, 1)

            @block.vector
            def _(dve):
                V = nc.vector
                ln = Links(dve, dv)
                sm = Small(dve, V, ln)
                sm.do(V.memset(carry[:, 0:1], -1.0))
                sm.do(V.tensor_copy(pen[:, 0:CLEN].rearrange("p (j c h) -> p c j h", c=CHUNKS, h=HEADS),
                                    m.sc[:, :].rearrange("p (c j h) -> p c j h", c=CHUNKS, h=HEADS)))
                dve.sem_inc(evac, 2)
                for n in range(NT):
                    dve.wait_ge(turned, n + 1)
                    V.tensor_copy(sT[:, 4 * n * P:4 * (n + 1) * P], pt[:, n % 2].rearrange("p k e -> p (k e)")).then_inc(evac, 1)
                dve.wait_ge(key_in, 16 * CHUNKS)
                sm.tt(pen, keys[:, 1:CLEN + 2], keys[:, 0:CLEN + 1], ALU.not_equal)
                sm.ts(pen, pen, -BIG, None, ALU.mult)

                def scan(out, pn, data, back, first):
                    f = (lambda ap: ap[:, ::-1]) if back else (lambda ap: ap)
                    sm.do(V.tensor_tensor_scan(f(out), f(pn), f(data), first, ALU.add, ALU.max))

                def both(out, pn, data, back, r):
                    scan(out, pn, data, back, -BIG)
                    end = 0 if back else CLEN - 1
                    sm.ts(carry[:, 1:2], out[:, end:end + 1], 1.0, None, ALU.mult)
                    sm.do(V.tensor_reduce(carry[:, 2:3], pn, axis=AX.X, op=ALU.add))
                    dve.sem_inc(ask, 1)
                    dve.wait_ge(answer, 2 * r + 1)
                    sm.do(V.tensor_copy(crow[0:1, 0:2, :], pr[0:1, :, :]))
                    sm.do(V.memset(crow[0:1, 2:4, :], -BIG))
                    for h in range(HEADS):
                        pick = lambda n: crow[0:1, n, :].rearrange("o (c h) -> o c h", h=HEADS)[:, :, h]
                        f = (lambda ap: ap[:, ::-1]) if back else (lambda ap: ap)
                        sm.do(V.tensor_tensor_scan(f(pick(2)), f(pick(1)), f(pick(0)), -BIG, ALU.add, ALU.max))
                    if back:
                        sm.do(V.tensor_copy(crow[0:1, 3, 0:P - HEADS], crow[0:1, 2, HEADS:P]))
                    else:
                        sm.do(V.tensor_copy(crow[0:1, 3, HEADS:P], crow[0:1, 2, 0:P - HEADS]))
                    dve.sem_inc(ask, 1)
                    dve.wait_ge(answer, 2 * r + 2)
                    sm.do(V.tensor_copy(carry[:, 3:4], pr[:, 0, 0:1]))
                    scan(out, pn, data, back, carry[:, 3:4])

                both(fwd, pen[:, 0:CLEN], sT, False, 0)
                both(keys[:, 0:CLEN], pen[:, 1:CLEN + 1], fwd, True, 1)
                sm.tt(sT, sT, keys[:, 0:CLEN], ALU.subtract)
                dve.sem_inc(ask, 1)
                scv = m.sc[:, :].rearrange("p (c j h) -> p c j h", c=CHUNKS, h=HEADS)
                for n in range(NT):
                    dve.wait_ge(turned, NT + n + 1)
                    if n == 0:
                        pass
                    V.tensor_copy(scv[:, :, 4 * n:4 * n + 4, :].rearrange("p c j h -> p j c h"),
                                  pt[:, n % 2].rearrange("p k (c h) -> p k c h", h=HEADS)).then_inc(evac, 1)
                dve.wait_ge(evac, 2 + 2 * NT)
                dve.sem_inc(ask, 1)

            @block.scalar
            def _(act):
                act.wait_ge(ask, 6)
                nc.scalar.activation(m.sc[:, :], m.sc[:, :], ACT.Exp, scale=SCORE).then_inc(answer, 1)


def attend(nc, m, edges):
    with Stage(nc, "at") as ctx:
        sb = lambda n, s, d=F32: ctx.enter_context(nc.sbuf_tensor(f"at_{n}", s, d))
        pb = lambda n, s: ctx.enter_context(nc.psum_tensor(f"at_{n}", s, F32))
        sem = ctx.sem
        ring = m.tab_a[:, 0:DEPTH * G * DIM].rearrange("p (t g d) -> p t g d", t=DEPTH, d=DIM)
        col = sb("col", [P, DEPTH, G, 3], I32)
        pv = sb("pv", [P, 2, G, AW])
        hot = sb("hot", [P, 2, G, P])
        off = sb("off", [1, STEPS], I16)
        out = pb("out", [P, 8, 512])
        col_in = [sem(f"col_in{h}") for h in range(DEPTH)]
        got = [ctx.gather_sem(m, f"got{h}") for h in range(DEPTH)]
        used, ready, out_in, summed, dv, off_in = (sem(n) for n in ("used", "ready", "out_in", "summed", "dve", "off_in"))
        ROUND = GROUPS // DEPTH
        with nc.Block() as block:
            @block.sync
            def _(sp):
                sp.dma_start(off[:, :], edges.off[1:2, 0:STEPS]).then_inc(off_in, 16)
                sp.sem_inc(used, DEPTH)
                fetch_steps(sp, edges, ROUND, used, None, None, col_in, col)

            @block.gpsimd
            def _(pool):
                with pool.Fori(0, ROUND) as i:
                    for h in range(DEPTH):
                        gather(m, pool, i, h, col_in, col, ring, got, m.d_v)

            @block.tensor
            def _(pe):
                with pe.Fori(0, ROUND) as i:
                    for h in range(DEPTH):
                        g = i * DEPTH + h
                        pe.wait_ge(ready, g + 1)
                        for k in range(G):
                            pe.wait_ge(summed, g * G + k + 1)
                            nc.tensor.matmul(out[:, k, 0:AW], hot[:, h % 2, k, :], pv[:, h % 2, k, :], start=True, stop=True).then_inc(out_in, 1)

            @block.vector
            def _(dve):
                V = nc.vector
                dve.wait_ge(off_in, 16)
                V.memset(m.acc_l0, 0.0).then_inc(summed, 8)
                starts = Starts(dve, "at", off, (NB - 1) * AW)

                def weigh(i, h):
                    g = i * DEPTH + h
                    dve.wait_ge(col_in[h], (i + 1) * 16)
                    V.tensor_tensor(hot[:, h % 2], m.ramp[:, :].unsqueeze(1).to_broadcast([P, G, P]),
                                    bcast(col[:, h, :, 1].bitcast(F32), P), ALU.is_equal)
                    at = bass.ds(g * (G * HEADS), G * HEADS)
                    V.tensor_copy(pv[:, h % 2, :, DIM:AW], m.sc[:, at].rearrange("p (k h) -> p k h", h=HEADS))
                    dve.wait_ge(got[h], (i + 1) * (16 * G))
                    V.tensor_tensor(pv[:, h % 2, :, 0:DIM].rearrange("p k (h d) -> p k h d", d=DH),
                                    ring[:, h].rearrange("p k (h d) -> p k h d", d=DH),
                                    m.sc[:, at].rearrange("p (k h) -> p k h", h=HEADS).unsqueeze(3).to_broadcast([P, G, HEADS, DH]),
                                    ALU.mult).then_inc(ready, 1)
                    dve.wait_ge(ready, g + 1)
                    dve.sem_inc(used, 1)

                def add(i, h, at):
                    g = i * DEPTH + h
                    for k in range(G):
                        row = m.acc_l0[:, bass.ds(at[k], AW)]
                        dve.wait_ge(out_in, g * G + k + 1)
                        dve.wait_ge(summed, g * G + k + 8)
                        V.tensor_tensor(row, row, out[:, k, 0:AW], ALU.add).then_inc(summed, 1)

                def round_(i, last):
                    for h in range(DEPTH):
                        g = i * DEPTH + h
                        at = starts.load(g * G, G)
                        if h + 1 < DEPTH:
                            weigh(i, h + 1)
                        elif not last:
                            weigh(i + 1, 0)
                        add(i, h, at)

                weigh(0, 0)
                with dve.Fori(0, ROUND - 1) as i:
                    round_(i, False)
                round_(ROUND - 1, True)


class PoolSmall(Small):

    def __init__(self, m, eng, ns, ln):
        super().__init__(eng, ns, ln)
        self.m = m

    def do(self, ins):
        self.ln.mark(ins)
        self.ln.wait()
        self.eng.sem_inc(self.m.nothing, 1)

    def stt(self, out, a, s1, b, op0, op1):
        self.ts(out, a, s1, None, op0)
        self.tt(out, out, b, op1)


MG = 6
PAIRS = MG // 2
CYCLE = 6
MROUNDS = -(-STEPS // (CYCLE * MG))
MSTEPS = MROUNDS * CYCLE * MG
assert MSTEPS <= SP_ and MROUNDS >= 3


def messages(nc, m, edges):
    with Stage(nc, "ms") as ctx:
        sb = lambda n, s, d=F32: ctx.enter_context(nc.sbuf_tensor(f"ms_{n}", s, d))
        pb = lambda n, s: ctx.enter_context(nc.psum_tensor(f"ms_{n}", s, F32))
        sem = ctx.sem
        far = sb("far", [P, 2, MG, 2 * DIM])
        us = sb("us", [P, 3, MG, DIM])
        col = sb("col", [P, CYCLE, MG, 3], I32)
        hotT = sb("hotT", [P, 2, MG * P])
        hot = sb("hot", [P, 2, P])
        r_wd, r_aw2, nb2 = sb("r_wd", [P, DIM]), sb("r_aw2", [P, DIM]), sb("nb2", [P, 1])
        junk = sb("junk", [P, 2, DIM], BF16)
        junk2 = m.big[:, 2 * NB * DIM:2 * NB * DIM + DIM].bitcast(BF16).rearrange("p (k d) -> p k d", k=2)
        w = sb("w", [P, 3, 18, MG])
        off = sb("off", [1, MSTEPS // MG * 8], I16)
        px = pb("px", [P, 2 * PAIRS, 512])
        out = pb("out", [P, 2, 512])
        bc_in = [sem(f"bc_in{h}") for h in range(2)]
        col_in = [sem(f"col_in{h}") for h in range(CYCLE)]
        got = [ctx.gather_sem(m, f"got{h}") for h in range(2)]
        (c_in, used, worked, hotT_in, px_in, dv, pl, summed, u_in, v_in, uu_in, silu_in, al_in, ab_in, root_in, z_in, ln_in,
         nn_in, norm_in, ex_in, den_in, rden_in, c_ready, hot_in, out_in, nb2_in, off_in) = (sem(n) for n in (
             "c_in", "used", "worked", "hotT_in", "px_in", "dve", "pool", "summed", "u_in", "v_in", "uu_in", "silu_in", "al_in",
             "ab_in", "root_in", "z_in", "ln_in", "nn_in", "norm_in", "ex_in", "den_in", "rden_in", "c_ready", "hot_in",
             "out_in", "nb2_in", "off_in"))
        MINK, XY, UU, AL, EX, C, X0Y0, DOT, T, A, R, ROOT, Z, S, LN, NN, DEN, DIST = range(18)
        U0 = 2 * PAIRS
        X0 = PAIRS + 1
        END = (MROUNDS - 1, CYCLE - 1)

        def by(i, h, d):
            if h + d < 0:
                return i - 1, h + d + CYCLE
            return (i, h + d) if h + d < CYCLE else (i + 1, h + d - CYCLE)

        def turns(i, h, places):
            return i * (CYCLE // places) + h // places + 1

        def run(eng, period):
            for h in range(CYCLE):
                period(0, h, h, True)
            with eng.Fori(1, MROUNDS - 1) as i:
                for h in range(CYCLE):
                    period(i, h, CYCLE, True)
            for h in range(CYCLE):
                period(MROUNDS - 1, h, CYCLE, h + 1 < CYCLE)

        with nc.Block() as block:
            @block.sync
            def _(sp):
                sp.dma_start(r_wd[:, :], m.in_aw1[2 * DIM:2 * DIM + 1, :].to_broadcast([P, DIM])).then_inc(c_in, 16)
                sp.dma_start(r_aw2[:, :], m.in_aw2.rearrange("n o -> o n").to_broadcast([P, DIM])).then_inc(c_in, 16)
                sp.dma_start(nb2[:, :], m.in_ab2.unsqueeze(0).to_broadcast([P, 1])).then_inc(c_in, 16)
                sp.dma_start(off[:, :].rearrange("o (g k) -> o g k", k=8)[:, :, 0:MG],
                             edges.off[0:1, 0:MSTEPS].rearrange("o (g k) -> o g k", k=MG)).then_inc(off_in, 16)
                sp.sem_inc(used, CYCLE)
                with sp.Fori(0, MROUNDS) as i:
                    for h in range(CYCLE):
                        n = i * CYCLE + h
                        sp.wait_ge(used, n + 1)
                        sp.dma_start(col[:, h], edges.cols[:, bass.ds(n * MG, MG), :]).then_inc(col_in[h], 16)
                        sp.wait_ge(px_in, n * PAIRS + 1)
                        sp.dma_start(hotT[:, h % 2, :],
                                     edges.lk[:, bass.ds(n * (MG * P), MG * P)].to_broadcast([P, MG * P])).then_inc(bc_in[h % 2], 16)

            @block.gpsimd
            def _(pool):
                GP = nc.gpsimd
                PER = 13

                def after(sem, v):
                    pool.wait_ge(sem, v)
                    pool.sem_inc(m.nothing, 1)

                def fetch(i, h):
                    after(worked, i * CYCLE + h + 1)
                    after(col_in[h], (i + 1) * 16)
                    for k in range(MG):
                        pool.indirect_dma_start(out=far[:, h % 2, k, :], out_offset=None, in_=m.d_xr,
                                                in_offset=bass.IndirectOffsetOnAxis(ap=col[:, h, k, 0:1], axis=0)).then_inc(got[h % 2], 16)

                def finish(i, h):
                    n = i * CYCLE + h
                    sm = PoolSmall(m, pool, GP, Links(pool, pl, n * PER))
                    W = lambda j: w[:, h % 3, j, :]
                    after(norm_in, n + 1)
                    after(ex_in, n + 1)
                    sm.stt(W(DEN), W(EX), 1.0, W(NN), ALU.add, ALU.mult)
                    pool.sem_inc(den_in, 1)
                    sm.ts(W(S), W(A), 3.0 / 160, -1.0 / 12, ALU.mult, ALU.add)
                    sm.tt(W(S), W(S), W(A), ALU.mult)
                    sm.stt(W(S), W(S), 1.0, W(ROOT), ALU.add, ALU.mult)
                    after(ln_in, n + 1)
                    sm.ts(W(A), W(A), 0.01, None, ALU.is_lt)
                    sm.tt(W(S), W(S), W(LN), ALU.subtract)
                    sm.tt(W(S), W(S), W(A), ALU.mult)
                    sm.tt(W(DIST), W(S), W(LN), ALU.add)
                    sm.stt(W(DIST), W(DIST), math.sqrt(FAR), col[:, h, :, 2].bitcast(F32), ALU.min, ALU.mult)
                    after(rden_in, n + 1)
                    sm.tt(W(C), W(DIST), W(DEN), ALU.mult)
                    pool.sem_inc(c_ready, 1)
                    assert sm.ln.n == PER, sm.ln.n

                def period(i, h, before, more):
                    if more:
                        fetch(*by(i, h, 1))
                    if before >= 1:
                        finish(*by(i, h, -1))

                fetch(0, 0)
                run(pool, period)
                finish(*END)

            @block.tensor
            def _(pe):
                TE = nc.tensor
                pe.wait_ge(off_in, 16)
                pe.sem_inc(px_in, X0)
                starts = [Starts(pe, f"ms{s}", off, (NB - 1) * DIM) for s in range(2)]

                def near(i, h, p):
                    n = i * CYCLE + h
                    if p == 0:
                        starts[h % 2].fetch(n * 8, MG)
                        pe.wait_ge(hotT_in, n + 1)
                        pe.wait_ge(got[h % 2], turns(i, h, 2) * (16 * MG))
                    at = starts[h % 2].values(2 * p, 2)
                    pe.wait_ge(u_in, (n * PAIRS + p) * 2 + 2)
                    for k in (2 * p, 2 * p + 1):
                        hk = hotT[:, h % 2, k * P:(k + 1) * P]
                        rows = bass.ds(at[k % 2], DIM)
                        TE.matmul(px[:, k, 0:DIM], hk, m.tab_a[:, rows], start=True, stop=True)
                        TE.matmul(px[:, k, DIM:2 * DIM], hk, m.tab_c[:, rows], start=True, stop=False)
                        last = TE.matmul(px[:, k, DIM:2 * DIM], m.ident[:, :], far[:, h % 2, k, DIM:2 * DIM], start=False, stop=True)
                    last.then_inc(px_in, 1)

                def sums(i, h, p):
                    n = i * CYCLE + h
                    for k in (2 * p, 2 * p + 1):
                        pe.wait_ge(hot_in, n * MG + k + 1)
                        pe.wait_ge(summed, n * MG + k + 1)
                        TE.matmul(out[:, k % 2, 0:DIM], hot[:, k % 2, :], us[:, h % 3, k, :], start=True, stop=True).then_inc(out_in, 1)

                def period(i, h, before, more):
                    for p in range(PAIRS):
                        if before >= 2:
                            sums(*by(i, h, -2), p)
                        if p == 0:
                            near(i, h, 2)
                    if more:
                        near(*by(i, h, 1), 0)
                        near(*by(i, h, 1), 1)

                near(0, 0, 0)
                near(0, 0, 1)
                run(pe, period)
                for d in (-1, 0):
                    for p in range(PAIRS):
                        sums(*by(*END, d), p)

            @block.scalar
            def _(act):
                AC = nc.scalar
                one = m.ones[:, 0:1]
                act.wait_ge(nb2_in, 1)

                def chain(i, h):
                    n = i * CYCLE + h
                    W = lambda j: w[:, h % 3, j, :]
                    act.wait_ge(ab_in, n + 1)
                    AC.activation(W(R), W(R), ACT.Sqrt).then_inc(root_in, 1)
                    AC.activation(W(ROOT), W(A), ACT.Sqrt, scale=2.0).then_inc(root_in, 1)
                    act.wait_ge(nn_in, n + 1)
                    AC.activation(W(NN), W(NN), ACT.Sqrt).then_inc(norm_in, 1)
                    act.wait_ge(al_in, n + 1)
                    AC.activation(W(EX), W(AL), ACT.Exp, scale=-1.0, bias=nb2[:, 0:1]).then_inc(ex_in, 1)
                    act.wait_ge(z_in, n + 1)
                    AC.activation(W(LN), W(Z), ACT.Ln, bias=one).then_inc(ln_in, 1)

                def period(i, h, before, more):
                    n = i * CYCLE + h
                    if before >= 1:
                        chain(*by(i, h, -1))
                    for k in range(MG):
                        act.wait_ge(v_in, n * MG + k + 1)
                        AC.activation(far[:, h % 2, k, DIM:2 * DIM], far[:, h % 2, k, DIM:2 * DIM], ACT.Silu).then_inc(silu_in, 1)
                        act.wait_ge(u_in, U0 + n * MG + k + 1)
                        if before >= 1 or k >= 2:
                            act.wait_ge(uu_in, n * MG + k - 1)
                        AC.activation(junk2[:, k % 2, 1:DIM], us[:, h % 3, k, 1:DIM], ACT.Square,
                                      accum_out=w[:, h % 3, UU, k:k + 1]).then_inc(uu_in, 1)

                run(act, period)
                chain(*END)

            @block.vector
            def _(dve):
                V = nc.vector
                V.memset(m.acc_l1, 0.0).then_inc(summed, 2)
                dve.wait_ge(c_in, 48)
                V.tensor_scalar(nb2[:, :], nb2[:, :], -1.0, None, ALU.mult).then_inc(nb2_in, 1)
                dve.wait_ge(off_in, 16)
                dve.sem_inc(u_in, U0)
                dve.sem_inc(worked, 2)
                starts = Starts(dve, "ms", off, (NB - 1) * DIM)
                PER = 5 * PAIRS + MG + 4

                def compare(i, h):
                    dve.wait_ge(bc_in[h % 2], turns(i, h, 2) * 16)
                    V.tensor_scalar(hotT[:, h % 2, :], hotT[:, h % 2, :], m.lane[:, 0:1], None, ALU.is_equal).then_inc(hotT_in, 1)

                def hots(i, h, p):
                    for k in (2 * p, 2 * p + 1):
                        V.tensor_scalar(hot[:, k % 2, :], m.ramp[:, :], col[:, h, k, 1:2].bitcast(F32), w[:, h % 3, C, k:k + 1],
                                        ALU.is_equal, ALU.mult).then_inc(hot_in, 1)

                def add(i, h, k, at):
                    n = i * CYCLE + h
                    dve.wait_ge(out_in, n * MG + k + 1)
                    row = m.acc_l1[:, bass.ds(at[k], DIM)]
                    dve.wait_ge(summed, n * MG + k + 2)
                    V.tensor_tensor(row, row, out[:, k % 2, 0:DIM], ALU.add).then_inc(summed, 1)

                def reciprocals(i, h):
                    dve.wait_ge(den_in, i * CYCLE + h + 1)
                    V.reciprocal(w[:, h % 3, DEN, :], w[:, h % 3, DEN, :]).then_inc(rden_in, 1)

                def period(i, h, before, more):
                    n = i * CYCLE + h
                    ln = Links(dve, dv, n * PER)
                    W = lambda j: w[:, h % 3, j, :]
                    back = by(i, h, -2)
                    if before >= 2:
                        starts.fetch((back[0] * CYCLE + back[1]) * 8, MG)
                        at = starts.values(0, MG)
                        dve.wait_ge(c_ready, back[0] * CYCLE + back[1] + 1)
                    dve.wait_ge(col_in[h], (i + 1) * 16)
                    dve.wait_ge(got[h % 2], turns(i, h, 2) * (16 * MG))

                    def attention(p):
                        for k in (2 * p, 2 * p + 1):
                            dve.wait_ge(silu_in, n * MG + k + 1)
                            if p == PAIRS - 1:
                                ln.wait(1)
                            ln.mark(V.tensor_tensor_reduce(out=junk[:, k % 2, :], in0=far[:, h % 2, k, DIM:2 * DIM], in1=r_aw2[:, :],
                                                           scale=1.0, scalar=0.0, op0=ALU.mult, op1=ALU.add, accum_out=w[:, h % 3, AL, k:k + 1]))

                    for p in range(PAIRS):
                        k0 = 2 * p
                        two = lambda j: w[:, h % 3, j, k0:k0 + 2]
                        if p == 1 and more:
                            compare(*by(i, h, 1))
                        if before >= 2:
                            hots(*back, p)
                        dve.wait_ge(px_in, X0 + n * PAIRS + p + 1)

                        def add_wd(k):
                            V.scalar_tensor_tensor(far[:, h % 2, k0 + k, DIM:2 * DIM], r_wd[:, :], col[:, h, k0 + k, 2:3].bitcast(F32),
                                                   px[:, k0 + k, DIM:2 * DIM], ALU.mult, ALU.add).then_inc(v_in, 1)

                        ln.mark(V.tensor_tensor(two(X0Y0), px[:, k0:k0 + 2, 0], far[:, h % 2, k0:k0 + 2, 0], ALU.mult))
                        for k in range(2):
                            if p >= 2:
                                ln.wait(2)
                            ln.mark(V.tensor_tensor_reduce(out=junk[:, k, 1:DIM], in0=px[:, k0 + k, 1:DIM], in1=far[:, h % 2, k0 + k, 1:DIM],
                                                           scale=1.0, scalar=0.0, op0=ALU.mult, op1=ALU.add,
                                                           accum_out=w[:, h % 3, DOT, k0 + k:k0 + k + 1]))
                        add_wd(0)
                        ln.wait()
                        ln.mark(V.tensor_tensor(two(MINK), two(DOT), two(X0Y0), ALU.subtract))
                        add_wd(1)
                        ln.wait()
                        ln.mark(V.tensor_scalar(two(XY), two(MINK), -1.0 - EPS, None, ALU.min))
                        if p == 0 and before >= 1:
                            j, g = by(i, h, -1), n - 1
                            L = lambda r: w[:, j[1] % 3, r, :]
                            dve.wait_ge(uu_in, g * MG + MG)
                            ln.mark(V.scalar_tensor_tensor(L(NN), us[:, j[1] % 3, :, 0], -1.0, us[:, j[1] % 3, :, 0], ALU.mult, ALU.mult))
                            dve.wait_ge(root_in, g * 2 + 2)
                            V.tensor_tensor(L(Z), L(A), L(R), ALU.add).then_inc(z_in, 1)
                            ln.wait()
                            ln.mark(V.tensor_tensor(L(NN), L(NN), L(UU), ALU.add))
                            ln.wait()
                            V.tensor_scalar(L(NN), L(NN), EPS, None, ALU.max).then_inc(nn_in, 1)
                        elif p == 0:
                            dve.sem_inc(dv, 2)
                            ln.n += 2
                        if before >= 2:
                            add(*back, k0, at)
                        ln.wait()
                        for k in range(2):
                            V.scalar_tensor_tensor(us[:, h % 3, k0 + k, :], px[:, k0 + k, 0:DIM], w[:, h % 3, XY, k0 + k:k0 + k + 1],
                                                   far[:, h % 2, k0 + k, 0:DIM], ALU.mult, ALU.add).then_inc(u_in, 1)
                        if p == PAIRS - 1:
                            ln.mark(V.tensor_scalar(W(T), W(MINK), -1.0, 1.0 + EPS, ALU.mult, ALU.max))
                        if before >= 2:
                            add(*back, k0 + 1, at)
                        if p == PAIRS - 1:
                            ln.wait()
                            ln.mark(V.tensor_scalar(W(A), W(T), 1.0, None, ALU.subtract))
                            if before >= 1:
                                reciprocals(*by(i, h, -1))
                            ln.wait()
                            V.scalar_tensor_tensor(W(R), W(T), 1.0, W(A), ALU.add, ALU.mult).then_inc(ab_in, 1)
                        if p >= 1:
                            attention(p - 1)
                    attention(PAIRS - 1)
                    ln.wait()
                    dve.sem_inc(al_in, 1)
                    dve.sem_inc(worked, 1)
                    if before >= 2:
                        dve.sem_inc(used, 1)
                    assert ln.n == PER, ln.n

                compare(0, 0)
                run(dve, period)
                end = MROUNDS * CYCLE - 1
                last = lambda r: w[:, (CYCLE - 1) % 3, r, :]
                sm = Small(dve, V, Links(dve, dv, (end + 1) * PER))
                dve.wait_ge(uu_in, end * MG + MG)
                time = us[:, (CYCLE - 1) % 3, :, 0]
                sm.tt(last(NN), time, time, ALU.mult)
                sm.tt(last(NN), last(UU), last(NN), ALU.subtract)
                sm.ts(last(NN), last(NN), EPS, None, ALU.max)
                dve.sem_inc(nn_in, 1)
                dve.wait_ge(root_in, end * 2 + 2)
                sm.tt(last(Z), last(A), last(R), ALU.add)
                dve.sem_inc(z_in, 1)
                for d in (-1, 0):
                    i, h = by(*END, d)
                    if d == 0:
                        reciprocals(i, h)
                    starts.fetch((i * CYCLE + h) * 8, MG)
                    at = starts.values(0, MG)
                    dve.wait_ge(c_ready, i * CYCLE + h + 1)
                    for p in range(PAIRS):
                        hots(i, h, p)
                        for k in (2 * p, 2 * p + 1):
                            add(i, h, k, at)


_INS = ["x", "src", "dst", "edge_weight1", "L0_gnn_Wq", "L0_gnn_bq", "L0_gnn_Wk", "L0_gnn_bk", "L0_gnn_Wv", "L0_gnn_bv",
        "L1_gnn_att_w1", "L1_gnn_att_b1", "L1_gnn_att_w2", "L1_gnn_att_b2", "L1_gnn_mlp_w1", "L1_gnn_mlp_b1",
        "L1_gnn_mlp_w2", "L1_gnn_mlp_b2"]
_OUTS = [((NODES, DIM), "float32")]
_DEBUG = []


def program(nc, ins, out, dbg):
    m = Mem()
    (m.in_x, m.in_src, m.in_dst, m.in_w, m.in_wq, m.in_bq, m.in_wk, m.in_bk, m.in_wv, m.in_bv, m.in_aw1, m.in_ab1,
     m.in_aw2, m.in_ab2, m.in_mw1, m.in_mb1, m.in_mw2, m.in_mb2) = ins
    m.out = out
    with ExitStack() as ctx:
        sb = lambda n, s, d=F32: ctx.enter_context(nc.sbuf_tensor(n, s, d))
        m.ctx = ctx
        dr = lambda n, s, d=F32: nc.dram_tensor(n, s, d).ap()
        m.ramp, m.lane = sb("ramp", [P, P]), sb("lane", [P, 1])
        m.step_no = sb("step_no", [P, SCOL])
        m.ones, m.ident, m.neg_ln2 = sb("ones", [P, P]), sb("ident", [P, P]), sb("neg_ln2", [P, 1])

        m.nothing = ctx.enter_context(nc.semaphore("nothing"))
        m.d_key, m.d_lo = dr("d_key", (ET, P)), dr("d_lo", (ET, P))
        m.d_key_flat, m.d_lo_flat = (d.rearrange("(o t) e -> o (t e)", o=1) for d in (m.d_key, m.d_lo))
        m.d_skey, m.d_skey2 = dr("d_skey", (1, SP_ * P + P)), dr("d_skey2", (1, SP_ * P + P))
        m.d_q, m.d_v, m.d_x1, m.d_xr = dr("d_q", (NP_, DIM)), dr("d_v", (NP_, DIM)), dr("d_x1", (NP_, DIM)), dr("d_xr", (NP_, 2 * DIM))
        m.d_sink = dr("d_sink", (4, 16))
        m.d_out = dr("d_out", (NP_, DIM))
        rec = dr("rec", (ET * P, 4), I32)
        by_dst, by_src = Mem(), Mem()
        with ExitStack() as early:
            sb_early = lambda n, s, d=F32: early.enter_context(nc.sbuf_tensor(n, s, d))
            m.ramp16, m.zeros = sb_early("ramp16", [P, P], BF16), sb_early("zeros", [P, P])
            m.before_row, m.before_col = sb_early("before_row", [P, P]), sb_early("before_col", [P, P])
            consts(nc, m)
            for tag, e, key, other in (("by_dst", by_dst, m.in_dst, m.in_src), ("by_src", by_src, m.in_src, m.in_dst)):
                lk = dr(f"{tag}_lk", (SP_, P))
                e.lk, e.cols, e.off = lk.rearrange("(o s) e -> o (s e)", o=1), dr(f"{tag}_edge_cols", (P, SP_, 3), I32), dr(f"{tag}_block_at", (2, SP_), I16)
                sort_edges(nc, m, tag, key, other, rec, lk, e.cols, e.off, m.d_skey if e is by_dst else m.d_skey2)
        TAB, SUMS = NB * DIM, NB * AW
        m.big = sb("big", [P, 2 * TAB + SUMS])
        m.tab_a = m.big[:, 0:TAB]
        m.acc_l0 = m.big[:, TAB:TAB + SUMS]
        m.acc_l1 = m.big[:, TAB:2 * TAB]
        m.tab_c = m.big[:, TAB + SUMS:2 * TAB + SUMS]
        m.sc = m.big[:, 2 * TAB + SUMS - STEPS * HEADS:2 * TAB + SUMS]
        node_stage(nc, m, "qkv", "qkv")
        scores(nc, m, by_dst)
        softmax_weights(nc, m)
        attend(nc, m, by_dst)
        node_stage(nc, m, "mid", "mid")
        messages(nc, m, by_src)
        node_stage(nc, m, "fin", "out")
        store(nc, m)


def store(nc, m):
    with nc.semaphore("out_done") as done, nc.Block() as block:
        @block.sync
        def _(sp):
            sp.dma_start(m.out, m.d_out[0:NODES, :]).then_inc(done, 16)
            sp.wait_ge(done, 16)


def kernel(**inputs):
    import numpy as _np
    import concourse.bacc as _bacc
    from concourse import mybir as _mybir
    from concourse.bass_utils import run_bass_kernel_spmd as _run

    nc = _bacc.Bacc("TRN2", target_bir_lowering=False, num_devices=1)
    arrays, args = {}, []
    for name in _INS:
        a = _np.ascontiguousarray(inputs[name])
        if name == "x":
            a = _np.concatenate([a, _np.zeros((NP_ - NODES, DIM), a.dtype)])
        elif name in ("src", "dst"):
            a = _np.concatenate([a, _np.full(ET * P - EDGES, PAD_NODE, a.dtype)]).reshape(ET, P)
        elif name == "edge_weight1":
            a = _np.concatenate([a.reshape(-1), _np.zeros(ET * P - EDGES, a.dtype)]).reshape(ET, P)
        arrays[f"in_{name}_dram"] = a
        args.append(nc.dram_tensor(f"in_{name}_dram", a.shape, _mybir.dt.from_np(a.dtype), kind="ExternalInput").ap())
    outs = []
    for i, (shape, dtype) in enumerate(_OUTS + _DEBUG):
        dt = _mybir.dt.from_np(_np.dtype(dtype))
        outs.append(nc.dram_tensor(f"out_{i}_dram", shape, dt, kind="ExternalOutput").ap())
    program(nc, args, outs[0], outs[1:])
    r = _run(nc, [arrays], core_ids=[0])
    return r.results[0]["out_0_dram"]
```
